# Optimizing a Trainium2 kernel written in Bass

```python
import numpy as np
import jax
import jax.numpy as jnp

def _softmax(x, axis=-1):
    return jax.nn.softmax(x, axis=axis)

def _gelu(x):
    return jax.nn.gelu(x, approximate=True)

def _silu(x):
    return jax.nn.silu(x)

def _sigmoid(x):
    return jax.nn.sigmoid(x)

def _layernorm(x, axis=-1, eps=1e-05):
    m = jnp.mean(x, axis=axis, keepdims=True)
    v = jnp.var(x, axis=axis, keepdims=True)
    return (x - m) / jnp.sqrt(v + eps)

def _scatter_add(tgt, idx, src, axis=0):
    return tgt.at[idx].add(src)

def _segment_sum(src, seg, n):
    return jax.ops.segment_sum(src, seg, n)
kernel_name = 'mk_xattn_ffn_d2_seqx_r8_c52935'

def setup_inputs(seed: int=0):
    np.random.seed(seed)
    _w = jnp.asarray

    def _rec_inputs():
        import jax
        import jax.numpy as jnp
        _rk = jax.random.key(seed)
        x = 7.22e-05 + 1 * jax.random.normal(jax.random.fold_in(_rk, 1), (64, 64, 128), jnp.float32)
        _lenS = 64 - jax.random.randint(jax.random.fold_in(_rk, 7), (64,), 0, max(1, 64 // 4) + 1, jnp.int32)
        _lenS2 = 64 - jax.random.randint(jax.random.fold_in(_rk, 8), (64,), 0, max(1, 64 // 4) + 1, jnp.int32)
        _ctx_1024P = jax.random.normal(jax.random.fold_in(_rk, 11), (64, 16, 128), jnp.float32)
        _ctx_1024c = jax.random.dirichlet(jax.random.fold_in(_rk, 511), 0.3 * jnp.ones((16,), jnp.float32), (64, 64))
        _ctx_1024t = jnp.einsum('bsk,bkd->bsd', _ctx_1024c, _ctx_1024P)
        _ctx_1024t = _ctx_1024t * jax.lax.rsqrt(jnp.mean(jnp.square(_ctx_1024t)) + 1e-12) * 0.953939
        ctx_1024 = 4.13588e-05 + 0.999923 * (_ctx_1024t + 0.3 * jax.random.normal(jax.random.fold_in(_rk, 611), (64, 64, 128), jnp.float32))
        _validS = jnp.arange(64)[None, :] < _lenS[:, None]
        _validS2 = jnp.arange(64)[None, :] < _lenS2[:, None]
        _causal = jnp.tril(jnp.ones((64, 64), dtype=bool))
        mask_Bx1xSxS2_ik1 = jnp.where(jnp.broadcast_to(_validS2[:, None, None, :], (64, 1, 64, 64)), 1, 0).astype(jnp.int32)
        return (x, ctx_1024, mask_Bx1xSxS2_ik1)
    x, ctx_1024, mask_Bx1xSxS2_ik1 = _rec_inputs()

    def _L0_xattn_setup():
        import jax, jax.numpy as jnp
        import numpy as np
        D_K = 128
        HEADS = 16
        HK = 64
        HV = 64
        key = jax.random.key(seed)
        ks = jax.random.split(key, 12)
        B, S = (4, 256)
        sc_in = 1.0 / np.sqrt(D_K)
        sc_u = 1.0 / np.sqrt(HV * HEADS)
        return {'q': jax.random.normal(ks[0], (B, S, D_K), jnp.float32), 'k': jax.random.normal(ks[1], (B, S, D_K), jnp.float32), 'v': jax.random.normal(ks[2], (B, S, D_K), jnp.float32), 'Wq': jax.random.normal(ks[3], (D_K, HK * HEADS), jnp.float32) * sc_in, 'bq': jax.random.normal(ks[4], (HK * HEADS,), jnp.float32) * sc_in, 'Wk': jax.random.normal(ks[5], (D_K, HK * HEADS), jnp.float32) * sc_in, 'bk': jax.random.normal(ks[6], (HK * HEADS,), jnp.float32) * sc_in, 'Wv': jax.random.normal(ks[7], (D_K, HV * HEADS), jnp.float32) * sc_in, 'bv': jax.random.normal(ks[8], (HV * HEADS,), jnp.float32) * sc_in, 'Wu': jax.random.normal(ks[9], (HV * HEADS, D_K), jnp.float32) * sc_u, 'bu': jax.random.normal(ks[10], (D_K,), jnp.float32) * sc_u}
    _L0_xattn_all = _L0_xattn_setup()
    _L0_xattn_in = {k: v for k, v in _L0_xattn_all.items() if k in ('Wq', 'bq', 'Wk', 'bk', 'Wv', 'bv', 'Wu', 'bu')}
    del _L0_xattn_all

    def _L0_ffn_setup():
        import jax, jax.numpy as jnp
        import numpy as np
        B, S, D, H, E = (2, 256, 128, 16, 8)
        DH = D // H
        CAP_FACTOR = 1.2

        def _forward(embed, Wq, bq, Wk, bk, Wv, bv, We, be, Wsw, bsw, gamma, beta):
            b, s, d = embed.shape
            h, e = (Wq.shape[0], We.shape[0])
            q = jnp.einsum('bsd,hed->bhse', embed, Wq) + bq[None, :, None, :]
            k = jnp.einsum('bsd,hed->bhse', embed, Wk) + bk[None, :, None, :]
            v = jnp.einsum('bsd,hed->bhse', embed, Wv) + bv[None, :, None, :]
            att = jnp.einsum('bhse,bhte->bhst', q, k)
            tril = jnp.tril(jnp.ones((s, s), bool))
            att = jnp.where(tril, att, 0.0) / jnp.sqrt(jnp.float32(d))
            att = jax.nn.softmax(att, axis=-1)
            out = jnp.einsum('bhst,bhte->bhse', att, v)
            hiddens = out.transpose(0, 2, 1, 3).reshape(b, s, d)
            x = hiddens.reshape(-1, d)
            n = b * s
            capacity = int(CAP_FACTOR * n / e)
            logits = x @ Wsw.T + bsw
            probs = jax.nn.softmax(logits, axis=-1)
            route_probs = jnp.max(probs, axis=-1)
            routes = jnp.argmax(probs, axis=-1)
            onehot = jax.nn.one_hot(routes, e, dtype=jnp.int32)
            pos = jnp.cumsum(onehot, axis=0) - 1
            pos = jnp.take_along_axis(pos, routes[:, None], axis=1)[:, 0]
            kept = pos < capacity
            slot = jnp.where(kept, routes * capacity + pos, e * capacity)
            dispatch = jnp.zeros((e * capacity + 1, d), x.dtype).at[slot].set(x)
            expert_in = dispatch[:e * capacity].reshape(e, capacity, d)
            expert_out = jnp.einsum('ecd,efd->ecf', expert_in, We) + be[:, None, :]
            expert_flat = jnp.concatenate([expert_out.reshape(e * capacity, d), jnp.zeros((1, d), x.dtype)], 0)
            gathered = expert_flat[slot]
            y = jnp.where(kept[:, None], gathered, x)
            y = (y * route_probs[:, None]).reshape(b, s, d)
            x2 = y + embed
            mean = jnp.mean(x2, axis=-1, keepdims=True)
            var = jnp.var(x2, axis=-1, keepdims=True)
            return (x2 - mean) / jnp.sqrt(var + 1e-05) * gamma + beta
        key = jax.random.key(seed)
        ks = jax.random.split(key, 14)
        s = 0.02
        return {'embed': jax.random.normal(ks[0], (B, S, D), jnp.float32), 'Wq': jax.random.normal(ks[1], (H, DH, D), jnp.float32) * s, 'bq': jnp.zeros((H, DH), jnp.float32), 'Wk': jax.random.normal(ks[2], (H, DH, D), jnp.float32) * s, 'bk': jnp.zeros((H, DH), jnp.float32), 'Wv': jax.random.normal(ks[3], (H, DH, D), jnp.float32) * s, 'bv': jnp.zeros((H, DH), jnp.float32), 'We': jax.random.normal(ks[4], (E, D, D), jnp.float32) * s, 'be': jnp.zeros((E, D), jnp.float32), 'Wsw': jax.random.normal(ks[5], (E, D), jnp.float32) * s, 'bsw': jnp.zeros((E,), jnp.float32), 'gamma': jnp.ones((D,), jnp.float32), 'beta': jnp.zeros((D,), jnp.float32)}
    _L0_ffn_all = _L0_ffn_setup()
    _L0_ffn_in = {k: v for k, v in _L0_ffn_all.items() if k in ('Wq', 'bq', 'Wk', 'bk', 'Wv', 'bv', 'We', 'be', 'Wsw', 'bsw', 'gamma', 'beta')}
    del _L0_ffn_all

    def _L1_xattn_setup():
        import jax, jax.numpy as jnp
        import numpy as np
        N, S, E, H = (4, 256, 128, 16)
        D = E // H
        key = jax.random.key(seed)
        ks = jax.random.split(key, 12)
        s = 1.0 / np.sqrt(E)
        inp = {'value': jax.random.normal(ks[0], (N, S, E), jnp.float32), 'key': jax.random.normal(ks[1], (N, S, E), jnp.float32), 'query': jax.random.normal(ks[2], (N, S, E), jnp.float32), 'mask': jax.random.randint(ks[3], (N, 1, S, S), 0, 2, dtype=jnp.int32), 'Wv': jax.random.normal(ks[4], (E, E), jnp.float32) * s, 'bv': jax.random.normal(ks[5], (E,), jnp.float32) * s, 'Wk': jax.random.normal(ks[6], (E, E), jnp.float32) * s, 'bk': jax.random.normal(ks[7], (E,), jnp.float32) * s, 'Wq': jax.random.normal(ks[8], (E, E), jnp.float32) * s, 'bq': jax.random.normal(ks[9], (E,), jnp.float32) * s, 'Wo': jax.random.normal(ks[10], (E, E), jnp.float32) * s, 'bo': jax.random.normal(ks[11], (E,), jnp.float32) * s}
        return inp
    _L1_xattn_all = _L1_xattn_setup()
    _L1_xattn_in = {k: v for k, v in _L1_xattn_all.items() if k in ('Wv', 'bv', 'Wk', 'bk', 'Wq', 'bq', 'Wo', 'bo')}
    del _L1_xattn_all

    def _L1_ffn_setup():
        import jax, jax.numpy as jnp
        import numpy as np
        B, P, D, D_MLP, E, K = (2, 256, 128, 512, 8, 2)
        key = jax.random.key(seed)
        k_x, k_g, k_in, k_out = jax.random.split(key, 4)
        s_in = 1.0 / np.sqrt(D).astype(np.float32)
        s_out = 1.0 / np.sqrt(D_MLP).astype(np.float32)
        return {'x': jax.random.normal(k_x, (B, P, D), dtype=jnp.float32), 'W_gate': jax.random.normal(k_g, (D, E), dtype=jnp.float32) * s_in, 'W_in': jax.random.normal(k_in, (E, D, D_MLP), dtype=jnp.float32) * s_in, 'b_in': jnp.zeros((E, D_MLP), dtype=jnp.float32), 'W_out': jax.random.normal(k_out, (E, D_MLP, D), dtype=jnp.float32) * s_out, 'b_out': jnp.zeros((E, D), dtype=jnp.float32)}
    _L1_ffn_all = _L1_ffn_setup()
    _L1_ffn_in = {k: v for k, v in _L1_ffn_all.items() if k in ('W_gate', 'W_in', 'b_in', 'W_out', 'b_out')}
    del _L1_ffn_all
    return {'x': x, 'ctx_1024': ctx_1024, 'mask_Bx1xSxS2_ik1': mask_Bx1xSxS2_ik1, 'L0_xattn_Wq': _L0_xattn_in['Wq'], 'L0_xattn_bq': _L0_xattn_in['bq'], 'L0_xattn_Wk': _L0_xattn_in['Wk'], 'L0_xattn_bk': _L0_xattn_in['bk'], 'L0_xattn_Wv': _L0_xattn_in['Wv'], 'L0_xattn_bv': _L0_xattn_in['bv'], 'L0_xattn_Wu': _L0_xattn_in['Wu'], 'L0_xattn_bu': _L0_xattn_in['bu'], 'L0_ffn_Wq': _L0_ffn_in['Wq'], 'L0_ffn_bq': _L0_ffn_in['bq'], 'L0_ffn_Wk': _L0_ffn_in['Wk'], 'L0_ffn_bk': _L0_ffn_in['bk'], 'L0_ffn_Wv': _L0_ffn_in['Wv'], 'L0_ffn_bv': _L0_ffn_in['bv'], 'L0_ffn_We': _L0_ffn_in['We'], 'L0_ffn_be': _L0_ffn_in['be'], 'L0_ffn_Wsw': _L0_ffn_in['Wsw'], 'L0_ffn_bsw': _L0_ffn_in['bsw'], 'L0_ffn_gamma': _L0_ffn_in['gamma'], 'L0_ffn_beta': _L0_ffn_in['beta'], 'L1_xattn_Wv': _L1_xattn_in['Wv'], 'L1_xattn_bv': _L1_xattn_in['bv'], 'L1_xattn_Wk': _L1_xattn_in['Wk'], 'L1_xattn_bk': _L1_xattn_in['bk'], 'L1_xattn_Wq': _L1_xattn_in['Wq'], 'L1_xattn_bq': _L1_xattn_in['bq'], 'L1_xattn_Wo': _L1_xattn_in['Wo'], 'L1_xattn_bo': _L1_xattn_in['bo'], 'L1_ffn_W_gate': _L1_ffn_in['W_gate'], 'L1_ffn_W_in': _L1_ffn_in['W_in'], 'L1_ffn_b_in': _L1_ffn_in['b_in'], 'L1_ffn_W_out': _L1_ffn_in['W_out'], 'L1_ffn_b_out': _L1_ffn_in['b_out']}

def reference(x, ctx_1024, mask_Bx1xSxS2_ik1, L0_xattn_Wq, L0_xattn_bq, L0_xattn_Wk, L0_xattn_bk, L0_xattn_Wv, L0_xattn_bv, L0_xattn_Wu, L0_xattn_bu, L0_ffn_Wq, L0_ffn_bq, L0_ffn_Wk, L0_ffn_bk, L0_ffn_Wv, L0_ffn_bv, L0_ffn_We, L0_ffn_be, L0_ffn_Wsw, L0_ffn_bsw, L0_ffn_gamma, L0_ffn_beta, L1_xattn_Wv, L1_xattn_bv, L1_xattn_Wk, L1_xattn_bk, L1_xattn_Wq, L1_xattn_bq, L1_xattn_Wo, L1_xattn_bo, L1_ffn_W_gate, L1_ffn_W_in, L1_ffn_b_in, L1_ffn_W_out, L1_ffn_b_out):
    import jax
    import jax.numpy as jnp

    def _L0_xattn_ref(q, k, v, Wq, bq, Wk, bk, Wv, bv, Wu, bu):
        import jax, jax.numpy as jnp
        import numpy as np
        D_K = 128
        HEADS = 16
        HK = 64
        HV = 64
        B, S, _ = q.shape
        qh = (q @ Wq + bq).reshape(B, S, HEADS, HK).transpose(0, 2, 1, 3)
        kh = (k @ Wk + bk).reshape(B, S, HEADS, HK).transpose(0, 2, 1, 3)
        vh = (v @ Wv + bv).reshape(B, S, HEADS, HV).transpose(0, 2, 1, 3)
        scores = jnp.einsum('bhqd,bhkd->bhqk', qh, kh) / jnp.sqrt(jnp.asarray(HK, qh.dtype))
        attn = jax.nn.softmax(scores, axis=-1)
        out = jnp.einsum('bhqk,bhkd->bhqd', attn, vh)
        merged = out.transpose(0, 2, 1, 3).reshape(B, S, HEADS * HV)
        return merged @ Wu + bu

    def _L0_ffn_ref(embed, Wq, bq, Wk, bk, Wv, bv, We, be, Wsw, bsw, gamma, beta):
        import jax, jax.numpy as jnp
        import numpy as np
        B, S, D, H, E = (2, 256, 128, 16, 8)
        DH = D // H
        CAP_FACTOR = 1.2

        def _forward(embed, Wq, bq, Wk, bk, Wv, bv, We, be, Wsw, bsw, gamma, beta):
            b, s, d = embed.shape
            h, e = (Wq.shape[0], We.shape[0])
            q = jnp.einsum('bsd,hed->bhse', embed, Wq) + bq[None, :, None, :]
            k = jnp.einsum('bsd,hed->bhse', embed, Wk) + bk[None, :, None, :]
            v = jnp.einsum('bsd,hed->bhse', embed, Wv) + bv[None, :, None, :]
            att = jnp.einsum('bhse,bhte->bhst', q, k)
            tril = jnp.tril(jnp.ones((s, s), bool))
            att = jnp.where(tril, att, 0.0) / jnp.sqrt(jnp.float32(d))
            att = jax.nn.softmax(att, axis=-1)
            out = jnp.einsum('bhst,bhte->bhse', att, v)
            hiddens = out.transpose(0, 2, 1, 3).reshape(b, s, d)
            x = hiddens.reshape(-1, d)
            n = b * s
            capacity = int(CAP_FACTOR * n / e)
            logits = x @ Wsw.T + bsw
            probs = jax.nn.softmax(logits, axis=-1)
            route_probs = jnp.max(probs, axis=-1)
            routes = jnp.argmax(probs, axis=-1)
            onehot = jax.nn.one_hot(routes, e, dtype=jnp.int32)
            pos = jnp.cumsum(onehot, axis=0) - 1
            pos = jnp.take_along_axis(pos, routes[:, None], axis=1)[:, 0]
            kept = pos < capacity
            slot = jnp.where(kept, routes * capacity + pos, e * capacity)
            dispatch = jnp.zeros((e * capacity + 1, d), x.dtype).at[slot].set(x)
            expert_in = dispatch[:e * capacity].reshape(e, capacity, d)
            expert_out = jnp.einsum('ecd,efd->ecf', expert_in, We) + be[:, None, :]
            expert_flat = jnp.concatenate([expert_out.reshape(e * capacity, d), jnp.zeros((1, d), x.dtype)], 0)
            gathered = expert_flat[slot]
            y = jnp.where(kept[:, None], gathered, x)
            y = (y * route_probs[:, None]).reshape(b, s, d)
            x2 = y + embed
            mean = jnp.mean(x2, axis=-1, keepdims=True)
            var = jnp.var(x2, axis=-1, keepdims=True)
            return (x2 - mean) / jnp.sqrt(var + 1e-05) * gamma + beta
        return _forward(embed, Wq, bq, Wk, bk, Wv, bv, We, be, Wsw, bsw, gamma, beta)

    def _L1_xattn_ref(value, key, query, mask, Wv, bv, Wk, bk, Wq, bq, Wo, bo):
        import jax, jax.numpy as jnp
        import numpy as np
        N, S, E, H = (4, 256, 128, 16)
        D = E // H
        n, q_len = (query.shape[0], query.shape[1])
        v = (value @ Wv.T + bv).reshape(n, -1, H, D)
        k = (key @ Wk.T + bk).reshape(n, -1, H, D)
        q = (query @ Wq.T + bq).reshape(n, -1, H, D)
        qk = jnp.einsum('nqhd,nkhd->nhqk', q, k)
        qk = jnp.where(mask == 0, jnp.asarray(1e-20, qk.dtype), qk)
        attn = jax.nn.softmax(qk / jnp.asarray(np.sqrt(E), qk.dtype), axis=3)
        out = jnp.einsum('nhqk,nkhd->nqhd', attn, v).reshape(n, q_len, H * D)
        return out @ Wo.T + bo

    def _L1_ffn_ref(x, W_gate, W_in, b_in, W_out, b_out):
        import jax, jax.numpy as jnp
        import numpy as np
        B, P, D, D_MLP, E, K = (2, 256, 128, 512, 8, 2)
        gate_logits = jnp.einsum('bpd,de->bpe', x, W_gate)
        top_w, top_idx = jax.lax.top_k(gate_logits, K)
        top_w = jax.nn.softmax(top_w, axis=-1)
        combine = jnp.einsum('bpke,bpk->bpe', jax.nn.one_hot(top_idx, E, dtype=x.dtype), top_w)
        out = jnp.zeros_like(x)
        for e in range(E):
            h = jax.nn.gelu(jnp.einsum('bpd,dm->bpm', x, W_in[e]) + b_in[e], approximate=False)
            y = jnp.einsum('bpm,md->bpd', h, W_out[e]) + b_out[e]
            out = out + combine[..., e, None] * y
        return out
    x = x + _L0_xattn_ref(_layernorm(x, axis=-1), ctx_1024, ctx_1024, L0_xattn_Wq, L0_xattn_bq, L0_xattn_Wk, L0_xattn_bk, L0_xattn_Wv, L0_xattn_bv, L0_xattn_Wu, L0_xattn_bu)
    x = x + _L0_ffn_ref(_layernorm(x, axis=-1), L0_ffn_Wq, L0_ffn_bq, L0_ffn_Wk, L0_ffn_bk, L0_ffn_Wv, L0_ffn_bv, L0_ffn_We, L0_ffn_be, L0_ffn_Wsw, L0_ffn_bsw, L0_ffn_gamma, L0_ffn_beta)
    x = x + _L1_xattn_ref(ctx_1024, ctx_1024, _layernorm(x, axis=-1), mask_Bx1xSxS2_ik1, L1_xattn_Wv, L1_xattn_bv, L1_xattn_Wk, L1_xattn_bk, L1_xattn_Wq, L1_xattn_bq, L1_xattn_Wo, L1_xattn_bo)
    x = x + _L1_ffn_ref(_layernorm(x, axis=-1), L1_ffn_W_gate, L1_ffn_W_in, L1_ffn_b_in, L1_ffn_W_out, L1_ffn_b_out)
    return x

_drawn_inputs = setup_inputs


def setup_inputs(seed=0):
    import zlib

    import numpy as np

    out = dict(_drawn_inputs(seed))
    spreads = {'L0_ffn_bq': (0.0, 0.8),
     'L0_ffn_bk': (0.0, 0.8),
     'L0_ffn_bv': (0.0, 0.577),
     'L0_ffn_be': (0.0, 0.743),
     'L0_ffn_bsw': (0.0, 0.56),
     'L0_ffn_gamma': (1.0, 0.2),
     'L0_ffn_beta': (0.0, 0.1),
     'L1_ffn_b_in': (0.0, 0.369),
     'L1_ffn_b_out': (0.0, 0.1)}
    factors = {'L0_xattn_bk': 64.0,
     'L0_ffn_Wq': 8.0,
     'L0_ffn_Wk': 8.0,
     'L0_ffn_Wv': 4.21,
     'L0_ffn_We': 8.0,
     'L0_ffn_Wsw': 6.963,
     'L1_xattn_bk': 46.071,
     'L1_xattn_bq': 8.0}
    for name, (base, spread) in spreads.items():
        noise = np.random.default_rng([zlib.crc32(name.encode()), seed]).standard_normal(out[name].shape)
        drawn = base * np.exp(spread * noise) if base else spread * noise
        out[name] = jnp.asarray(drawn.astype(out[name].dtype))
    for name, factor in factors.items():
        out[name] = (out[name] * factor).astype(out[name].dtype)
    return out
```

```python
from contextlib import ExitStack

import concourse.bass as bass
from concourse import mybir

F32 = mybir.dt.float32
BF16 = mybir.dt.bfloat16
I32 = mybir.dt.int32
U32 = mybir.dt.uint32
ALU = mybir.AluOpType
ACT = mybir.ActivationFunctionType
AX = mybir.AxisListType

P = 128
BATCHES, SEQ, D = 64, 64, 128
TILES = BATCHES * SEQ // P
PER_TILE = P // SEQ
HEADS = 16
CHUNKS = HEADS // 2
PAIRS = CHUNKS // 2
HK = 64
WIDE = HEADS * HK
HD = D // HEADS
EXPERTS = 8
CAPACITY = int(1.2 * BATCHES * SEQ / EXPERTS)
MLP = 512
BLOCKS = MLP // P
EPS = 1e-5
TOP = 2
REGION = BATCHES * SEQ + P
SORTED = BATCHES * SEQ * TOP // P + EXPERTS
VCOL = 2 * HD + 1
DMA = 16


class Tile:

    def __init__(self, group, at, count=TILES, size=2):
        self.group, self.at, self.count, self.size = group, at, count, size
        self.odd = at % 2
        self.index = group * size + at if at else group * size

    def back(self, lag):
        at = self.at - lag
        groups = at // self.size
        return Tile(self.group + groups if groups else self.group, at % self.size, self.count, self.size)

    @property
    def live(self):
        return not isinstance(self.group, int) or 0 <= self.index < self.count


def wait(eng, sem, value):
    if not isinstance(value, int) or value > 0:
        eng.wait_ge(sem, value)


def apart(eng):
    eng.nop(nofuse=True)


def over_tiles(eng, step, lag, count=TILES, size=2):
    first = (lag + 2 * size - 1) // size
    for s in range(first * size):
        step(Tile(s // size, s % size, count, size))
    with eng.Fori(first, count // size) as group:
        for at in range(size):
            step(Tile(group, at, count, size))
    for s in range(count, count + lag):
        step(Tile(s // size, s % size, count, size))


class Memory:

    def __init__(self, nc, ctx, tag):
        self.nc, self.ctx, self.tag = nc, ctx, tag
        self.semaphores = []
        ctx.callback(self.clear)

    def clear(self):
        self.nc.clear_and_free_semaphores(self.semaphores)
        self.nc.all_engine_barrier()

    def sb(self, name, shape, dt=F32):
        return self.ctx.enter_context(self.nc.sbuf_tensor(f"{self.tag}_{name}", shape, dt))

    def ps(self, name, shape, dt=F32):
        return self.ctx.enter_context(self.nc.psum_tensor(f"{self.tag}_{name}_ps", shape, dt))

    def sem(self, name):
        self.semaphores.append(self.nc.alloc_semaphore(name=f"{self.tag}_{name}"))
        return self.semaphores[-1]


def many(ap, n, axis=2):
    ap = ap.unsqueeze(axis)
    shape = list(ap.shape)
    shape[axis] = n
    return ap.to_broadcast(shape)


def wide_attention(nc, dram, keep):
    ctx = ExitStack()
    with ctx:
        m = Memory(nc, ctx, "wide")
        x, ident, eps_pow = keep["x"], keep["ident"], keep["eps_pow"]
        wq = m.sb("wq", [P, CHUNKS, P])
        wk = m.sb("wk", [P, CHUNKS, P])
        wv = m.sb("wv", [P, WIDE])
        wu = m.sb("wu", [P, PAIRS, 2, D])
        bq = m.sb("bq", [P, CHUNKS])
        bk = m.sb("bk", [P, CHUNKS])
        bv = m.sb("bv", [P, PAIRS, 2])
        bv_wide = m.sb("bv_wide", [P, PAIRS * 2, P])
        bu = m.sb("bu", [P, D])
        ctx_in = m.sb("ctx_in", [P, 2, D])
        stats = m.sb("stats", [P, 2, 6])
        mean_var = m.sb("mean_var", [P, 2, 2])
        var_eps = m.sb("var_eps", [P, 2])
        rstd = m.sb("rstd", [P, 2])
        xn = m.sb("xn", [P, 2, D])
        xc_t = m.sb("xc_t", [P, 2, 2, P])
        q_block = m.sb("q_block", [P, 2, CHUNKS, PER_TILE, 2, SEQ])
        k_t = m.sb("k_t", [P, 2, CHUNKS, P])
        v_block = m.sb("v_block", [P, 2, PER_TILE, PAIRS, 2, 2, HK])
        top = m.sb("top", [P, 2, HEADS])
        expo = m.sb("expo", [P, 2, HEADS, SEQ])
        total = m.sb("total", [P, 2, HEADS])
        share = m.sb("share", [P, 2, HEADS])
        prob = m.sb("prob", [P, 2, HEADS, SEQ])
        prob_t = m.sb("prob_t", [P, 2, PER_TILE, PAIRS, P])
        out_t = m.sb("out_t", [P, 2, PAIRS, 2, PER_TILE, SEQ])

        proj_ps = [m.ps(f"proj{i}", [P, 4, P]) for i in range(2)]
        score_ps = m.ps("score", [P, PER_TILE, CHUNKS * SEQ])
        turn_ps = m.ps("turn", [P, PER_TILE, 512])
        norm_ps = m.ps("norm", [P, 512])
        up_ps = m.ps("up", [P, 512])

        loaded = m.sem("loaded")
        bias_loaded = m.sem("bias_loaded")
        blocks_zero = m.sem("blocks_zero")
        bv_spread = m.sem("bv_spread")
        bu_summed = m.sem("bu_summed")
        bu_ready = m.sem("bu_ready")
        ctx_loaded = [m.sem(f"ctx_loaded{i}") for i in range(2)]
        stats_done = m.sem("stats_done")
        mean_done = m.sem("mean_done")
        var_done = m.sem("var_done")
        rstd_done = m.sem("rstd_done")
        xn_done = m.sem("xn_done")
        x_biased = m.sem("x_biased")
        turned_in = m.sem("turned_in")
        xc_done = m.sem("xc_done")
        q_filled = m.sem("q_filled")
        k_filled = m.sem("k_filled")
        v_filled = m.sem("v_filled")
        q_done = m.sem("q_done")
        k_done = m.sem("k_done")
        v_done = m.sem("v_done")
        scored = m.sem("scored")
        top_done = m.sem("top_done")
        shifted = m.sem("shifted")
        exp_done = m.sem("exp_done")
        total_done = m.sem("total_done")
        share_done = m.sem("share_done")
        prob_done = m.sem("prob_done")
        prob_turned = m.sem("prob_turned")
        prob_t_done = m.sem("prob_t_done")
        mixed = m.sem("mixed")
        out_t_done = m.sem("out_t_done")
        up_done = m.sem("up_done")
        x_done = m.sem("x_done")

        ctx_tiles = dram["ctx_1024"].rearrange("b s d -> (b s) d").rearrange("(t p) d -> t p d", p=P)

        block = ctx.enter_context(nc.Block())
        BIAS_LOADS = 4 * PAIRS + 1

        @block.sync
        def _(sp):
            sp.dma_start(ctx_in[:, 0, :], ctx_tiles[0]).then_inc(ctx_loaded[0], DMA)
            sp.dma_start(ctx_in[:, 1, :], ctx_tiles[1]).then_inc(ctx_loaded[1], DMA)
            sp.dma_start(wq[:, :, :], dram["L0_xattn_Wq"].rearrange("d (c m) -> d c m", m=P)).then_inc(loaded, DMA)
            sp.dma_start(wk[:, :, :], dram["L0_xattn_Wk"].rearrange("d (c m) -> d c m", m=P)).then_inc(loaded, DMA)
            sp.dma_start(bq[:, :], dram["L0_xattn_bq"].rearrange("(c m) -> m c", m=P),
                         allow_slow_non_contiguous=True).then_inc(loaded, DMA)
            sp.dma_start(bk[:, :], dram["L0_xattn_bk"].rearrange("(c m) -> m c", m=P),
                         allow_slow_non_contiguous=True).then_inc(loaded, DMA)
            sp.dma_start(wv[:, :], dram["L0_xattn_Wv"]).then_inc(loaded, DMA)
            wu_rows = dram["L0_xattn_Wu"].rearrange("(c p h d) n -> p d c h n", c=PAIRS, p=2, h=2)
            bv_rows = dram["L0_xattn_bv"].rearrange("(c p h d) -> p d c h", c=PAIRS, p=2, h=2)
            for half in range(2):
                rows = slice(half * HK, half * HK + HK)
                for c in range(PAIRS):
                    sp.dma_start(wu[rows, c, :, :], wu_rows[half][:, c, :, :]).then_inc(bias_loaded, DMA)
                    sp.dma_start(bv[rows, c, :], bv_rows[half][:, c, :],
                                 allow_slow_non_contiguous=True).then_inc(bias_loaded, DMA)
            sp.dma_start(bu[:, :], dram["L0_xattn_bu"].partition_broadcast(P)).then_inc(bias_loaded, DMA)

            def step(t):
                u = t.back(-2)
                if u.live:
                    wait(sp, turned_in, t.index + 1)
                    sp.dma_start(ctx_in[:, u.odd, :], ctx_tiles[u.index]).then_inc(ctx_loaded[u.odd], DMA)

            with sp.Fori(0, TILES // 2 - 1) as group:
                step(Tile(group, 0))
                step(Tile(group, 1))

        @block.tensor
        def _(pe):
            pe.wait_ge(bv_spread, 1)
            pe.wait_ge(bias_loaded, BIAS_LOADS * DMA)
            for n in range(PAIRS * 2):
                last = pe.matmul(up_ps[:, 0:D], bv_wide[:, n, :], wu[:, n // 2, n % 2, :],
                                 start=(n == 0), stop=(n == PAIRS * 2 - 1))
            last.then_inc(bu_summed, 1)
            pe.wait_ge(loaded, 5 * DMA)
            pe.wait_ge(blocks_zero, 2)
            pe.wait_ge(keep["ident_ready"], keep["ident_count"])

            def turn_in(t):
                pe.wait_ge(xn_done, t.index + 1)
                pe.wait_ge(ctx_loaded[t.odd], (t.group + 1) * DMA)
                wait(pe, xc_done, t.index)
                pe.transpose(norm_ps[:, 0:P], xn[:, t.odd, :], ident[:, :])
                pe.transpose(norm_ps[:, P:2 * P], ctx_in[:, t.odd, :], ident[:, :]).then_inc(turned_in, 1)

            def project_q(t, half):
                pe.wait_ge(xc_done, t.index + 1)
                if half == 0:
                    wait(pe, v_done, t.index * 2 - 1)
                else:
                    pe.wait_ge(q_done, t.index * 2 + 1)
                for c in range(4):
                    last = pe.matmul(proj_ps[0][:, c, :], wq[:, half * 4 + c, :], xc_t[:, t.odd, 0, :],
                                     start=True, stop=True)
                last.then_inc(q_filled, 1)

            def project_k(t, half):
                if half == 0:
                    wait(pe, v_done, t.index * 2)
                else:
                    pe.wait_ge(k_done, t.index * 2 + 1)
                for c in range(4):
                    last = pe.matmul(proj_ps[1][:, c, :], wk[:, half * 4 + c, :], xc_t[:, t.odd, 1, :],
                                     start=True, stop=True)
                last.then_inc(k_filled, 1)

            def project_v(t, half):
                pe.wait_ge(q_done if half == 0 else k_done, t.index * 2 + 2)
                last = pe.matmul(proj_ps[half][:, :, :], xc_t[:, t.odd, 1, :], wv[:, half * 512:half * 512 + 512],
                                 start=True, stop=True)
                last.then_inc(v_filled, 1)

            def scores(t):
                pe.wait_ge(q_done, 2 * t.index + 2)
                pe.wait_ge(k_done, 2 * t.index + 2)
                wait(pe, shifted, t.index)
                for b in range(PER_TILE):
                    for c in range(CHUNKS):
                        last = pe.matmul(score_ps[:, b, c * SEQ:(c + 1) * SEQ], q_block[:, t.odd, c, b, :, :],
                                         k_t[:, t.odd, c, b * SEQ:(b + 1) * SEQ], start=True, stop=True)
                last.then_inc(scored, 1)

            def turn_prob(t):
                pe.wait_ge(prob_done, t.index + 1)
                wait(pe, out_t_done, t.index)
                for b in range(PER_TILE):
                    for c in range(PAIRS):
                        h = b * CHUNKS + 2 * c
                        last = pe.transpose(turn_ps[:, b, c * P:(c + 1) * P], prob[:, t.odd, h:h + 2, :], ident[:, :])
                last.then_inc(prob_turned, 1)

            def mix(t):
                pe.wait_ge(prob_t_done, t.index + 1)
                pe.wait_ge(v_done, 2 * t.index + 2)
                for b in range(PER_TILE):
                    for c in range(PAIRS):
                        for h in range(2):
                            at = (2 * c + h) * SEQ
                            last = pe.matmul(turn_ps[:, b, at:at + SEQ], v_block[:, t.odd, b, c, h, :, :],
                                             prob_t[:, t.odd, b, c, h * SEQ:(h + 1) * SEQ], start=True, stop=True)
                last.then_inc(mixed, 1)

            def up(t):
                pe.wait_ge(out_t_done, t.index + 1)
                wait(pe, x_done, t.index)
                for n in range(PAIRS * 2):
                    last = pe.matmul(up_ps[:, 0:D], out_t[:, t.odd, n // 2, n % 2, :, :], wu[:, n // 2, n % 2, :],
                                     start=(n == 0), stop=(n == PAIRS * 2 - 1))
                last.then_inc(up_done, 1)

            pe.wait_ge(bu_ready, 1)

            def step(t):
                now, one, two, three = t, t.back(1), t.back(2), t.back(3)
                if two.live:
                    scores(two)
                if three.live:
                    turn_prob(three)
                if one.live:
                    project_q(one, 0)
                    project_k(one, 0)
                if three.live:
                    mix(three)
                if one.live:
                    project_q(one, 1)
                    project_k(one, 1)
                    project_v(one, 0)
                if three.live:
                    up(three)
                if one.live:
                    project_v(one, 1)
                if now.live:
                    turn_in(now)

            over_tiles(pe, step, 3)

        @block.scalar
        def _(act):
            act.wait_ge(loaded, 5 * DMA)
            act.wait_ge(blocks_zero, 2)

            def bring_prob(t):
                act.wait_ge(prob_turned, t.index + 1)
                wait(act, mixed, t.index - 1)
                act.copy(prob_t[:, t.odd, :, :, :], turn_ps[:, :, :]).then_inc(prob_t_done, 1)

            def bring_k(t, half):
                act.wait_ge(k_filled, 2 * t.index + half + 1)
                if half == 0:
                    wait(act, scored, t.index - 1)
                for c in range(4):
                    n = half * 4 + c
                    last = act.activation(k_t[:, t.odd, n, :], proj_ps[1][:, c, :], ACT.Identity,
                                          bias=bk[:, n:n + 1])
                last.then_inc(k_done, 1)

            def bring_v(t, half):
                act.wait_ge(v_filled, 2 * t.index + half + 1)
                if half == 0:
                    wait(act, mixed, t.index - 1)
                for b in range(PER_TILE):
                    for p in range(2):
                        frm = proj_ps[half][b * SEQ:(b + 1) * SEQ, :, :].rearrange(
                            "k (c p) (h d) -> k c p h d", p=2, h=2)[:, :, p, :, :]
                        last = act.copy(
                            v_block[p * SEQ:(p + 1) * SEQ, t.odd, b, 2 * half:2 * half + 2, :, p, :], frm)
                last.then_inc(v_done, 1)

            def exponent(t):
                act.wait_ge(shifted, t.index + 1)
                act.activation(expo[:, t.odd, :, :], expo[:, t.odd, :, :], ACT.Exp, scale=HK ** -0.5).then_inc(exp_done, 1)

            def bring_out(t):
                act.wait_ge(mixed, t.index + 1)
                wait(act, up_done, t.index - 1)
                for b in range(PER_TILE):
                    last = act.copy(out_t[:, t.odd, :, :, b, :],
                                    turn_ps[:, b, :].rearrange("p (c h q) -> p c h q", c=PAIRS, h=2))
                last.then_inc(out_t_done, 1)

            def bring_in(t):
                act.wait_ge(turned_in, t.index + 1)
                wait(act, v_filled, 2 * t.index - 2)
                act.copy(xc_t[:, t.odd, :, :], norm_ps[:, 0:2 * P]).then_inc(xc_done, 1)

            def step(t):
                now, one, two, three = t, t.back(1), t.back(2), t.back(3)
                if three.live:
                    bring_prob(three)
                if one.live:
                    bring_k(one, 0)
                if two.live:
                    exponent(two)
                if three.live:
                    bring_out(three)
                if one.live:
                    bring_k(one, 1)
                    bring_v(one, 0)
                    bring_v(one, 1)
                if now.live:
                    bring_in(now)

            over_tiles(act, step, 3)

        @block.vector
        def _(dve):
            dve.memset(q_block[:, :, :, :, :, :], 0.0).then_inc(blocks_zero, 1)
            dve.memset(v_block[:, :, :, :, :, :, :], 0.0).then_inc(blocks_zero, 1)
            dve.wait_ge(blocks_zero, 2)
            dve.wait_ge(bias_loaded, BIAS_LOADS * DMA)
            dve.tensor_copy(bv_wide[:, :, :], many(bv[:, :, :].rearrange("p c h -> p (c h)"), P)).then_inc(bv_spread, 1)
            dve.wait_ge(bu_summed, 1)
            dve.tensor_tensor(bu[:, :], up_ps[:, 0:D], bu[:, :], ALU.add).then_inc(bu_ready, 1)
            dve.wait_ge(loaded, 5 * DMA)

            def moments(t):
                dve.bn_stats(stats[:, t.odd, :], x[:, t.index, :]).then_inc(stats_done, 1)
                dve.wait_ge(stats_done, t.index + 1)
                wait(dve, xn_done, t.index - 1)
                apart(dve)
                dve.bn_aggr(mean_var[:, t.odd, :], stats[:, t.odd, :]).then_inc(mean_done, 1)
                dve.wait_ge(mean_done, t.index + 1)
                wait(dve, rstd_done, t.index - 1)
                dve.tensor_scalar(var_eps[:, t.odd:t.odd + 1], mean_var[:, t.odd, 1:2], EPS, None,
                                  ALU.add).then_inc(var_done, 1)

            def normalize(t):
                dve.wait_ge(rstd_done, t.index + 1)
                wait(dve, turned_in, t.index - 1)
                dve.tensor_scalar(xn[:, t.odd, :], x[:, t.index, :], mean_var[:, t.odd, 0:1],
                                  rstd[:, t.odd:t.odd + 1], ALU.subtract, ALU.mult).then_inc(xn_done, 1)

            def bring_q(t, half):
                dve.wait_ge(q_filled, 2 * t.index + half + 1)
                if half == 0:
                    wait(dve, scored, t.index - 1)
                for p in range(2):
                    rows = slice(p * HK, (p + 1) * HK)
                    cs = slice(half * 4, half * 4 + 4)
                    last = dve.tensor_tensor(
                        q_block[rows, t.odd, cs, :, p, :],
                        proj_ps[0][rows, :, :].rearrange("p c (b q) -> p c b q", b=PER_TILE),
                        many(bq[rows, cs], P).rearrange("p c (b q) -> p c b q", b=PER_TILE), ALU.add)
                last.then_inc(q_done, 1)

            def shift(t):
                dve.wait_ge(scored, t.index + 1)
                s = score_ps[:, :, :].rearrange("p b (c k) -> p (b c) k", k=SEQ)
                dve.tensor_reduce(top[:, t.odd, :], s, AX.X, ALU.max).then_inc(top_done, 1)
                dve.wait_ge(top_done, t.index + 1)
                wait(dve, prob_done, t.index - 1)
                dve.tensor_tensor(expo[:, t.odd, :, :], s, many(top[:, t.odd, :], SEQ), ALU.subtract).then_inc(shifted, 1)

            def totals(t):
                dve.wait_ge(exp_done, t.index + 1)
                dve.tensor_reduce(total[:, t.odd, :], expo[:, t.odd, :, :], AX.X, ALU.add).then_inc(total_done, 1)
                dve.wait_ge(total_done, t.index + 1)
                dve.reciprocal(share[:, t.odd, :], total[:, t.odd, :]).then_inc(share_done, 1)

            def residual(t):
                dve.wait_ge(up_done, t.index + 1)
                dve.wait_ge(x_biased, t.index + 1)
                dve.tensor_tensor(x[:, t.index, :], up_ps[:, 0:D], x[:, t.index, :], ALU.add).then_inc(x_done, 1)

            def step(t):
                now, one, two, three = t, t.back(1), t.back(2), t.back(3)
                if two.live:
                    shift(two)
                if now.live:
                    moments(now)
                if one.live:
                    bring_q(one, 0)
                if two.live:
                    totals(two)
                if now.live:
                    normalize(now)
                if one.live:
                    bring_q(one, 1)
                if three.live:
                    residual(three)

            dve.wait_ge(keep["x_loaded"], 4 * DMA)
            over_tiles(dve, step, 3)

        @block.gpsimd
        def _(pool):
            pool.wait_ge(keep["ident_ready"], keep["ident_count"])
            pool.wait_ge(bu_ready, 1)

            def step(t):
                now, two = t, t.back(2)
                if now.live:
                    pool.wait_ge(var_done, now.index + 1)
                    pool.tensor_tensor(rstd[:, now.odd:now.odd + 1], var_eps[:, now.odd:now.odd + 1],
                                       eps_pow[:, :], ALU.pow).then_inc(rstd_done, 1)
                if two.live:
                    pool.wait_ge(share_done, two.index + 1)
                    wait(pool, prob_turned, two.index - 1)
                    pool.tensor_tensor(prob[:, two.odd, :, :], expo[:, two.odd, :, :],
                                       many(share[:, two.odd, :], SEQ), ALU.mult).then_inc(prob_done, 1)
                if now.live:
                    pool.wait_ge(xn_done, now.index + 1)
                    pool.tensor_tensor(x[:, now.index, :], x[:, now.index, :], bu[:, :], ALU.add).then_inc(x_biased, 1)

            over_tiles(pool, step, 2)


def routed_attention(nc, dram, keep):
    ctx = ExitStack()
    with ctx:
        m = Memory(nc, ctx, "rout")
        x, ident, eps_pow = keep["x"], keep["ident"], keep["eps_pow"]
        w_in = m.sb("w_in", [P, 3 + EXPERTS, D])
        w_t = m.sb("w_t", [P, 3 + EXPERTS, D])
        wsw_in = m.sb("wsw_in", [EXPERTS, D])
        wsw_t = m.sb("wsw_t", [P, EXPERTS])
        bq = m.sb("bq", [P, 1])
        bk = m.sb("bk", [P, 1])
        bv = m.sb("bv", [P, D])
        gamma = m.sb("gamma", [P, D])
        beta = m.sb("beta", [P, D])
        bsw = m.sb("bsw", [P, EXPERTS])
        be = m.sb("be", [P, EXPERTS * D])
        be_parts = m.sb("be_parts", [96, EXPERTS * D], BF16)
        be_ones = m.sb("be_ones", [96, P], BF16)
        head_of = m.sb("head_of", [P, HEADS])
        causal = m.sb("causal", [P, SEQ])
        upto = m.sb("upto", [P, P], BF16)
        ones = m.sb("ones", [P, P], BF16)
        number = m.sb("number", [P, EXPERTS])
        seen = m.sb("seen", [P, EXPERTS], BF16)

        stats = m.sb("stats", [P, 2, 6])
        mean_var = m.sb("mean_var", [P, 2, 2])
        var_eps = m.sb("var_eps", [P, 2])
        rstd = m.sb("rstd", [P, 2])
        e_now = m.sb("e_now", [P, 2, D])
        e_all = m.sb("e_all", [P, TILES, D])
        e_t = m.sb("e_t", [P, 2, P])
        qk = m.sb("qk", [P, 2, 2, P])
        q_block = m.sb("q_block", [P, 2, PER_TILE, HEADS, SEQ])
        v_block = m.sb("v_block", [P, 2, PER_TILE, PAIRS, 2, VCOL])
        score = m.sb("score", [P, 2, HEADS, SEQ])
        top = m.sb("top", [P, 2, HEADS])
        expo = m.sb("expo", [P, 2, HEADS, SEQ])
        prob_t = m.sb("prob_t", [P, 2, PER_TILE, PAIRS, P])
        share = m.sb("share", [P, 2, PER_TILE, CHUNKS])
        hid_raw = m.sb("hid_raw", [P, 2, D])
        hid = m.sb("hid", [P, 2, D])
        hid_t = m.sb("hid_t", [P, 2, P])
        logit = m.sb("logit", [P, EXPERTS])
        best = m.sb("best", [P, 8])
        place = m.sb("place", [P, 8], U32)
        less_best = m.sb("less_best", [P, 1])
        e_logit = m.sb("e_logit", [P, EXPERTS])
        e_sum = m.sb("e_sum", [P, 1])
        route_prob = m.sb("route_prob", [P, 1])
        chosen = m.sb("chosen", [P, EXPERTS])
        chosen_b = m.sb("chosen_b", [P, EXPERTS], BF16)
        order = m.sb("order", [P, EXPERTS])
        position = m.sb("position", [P, 1])
        kept = m.sb("kept", [P, 1])
        gate = m.sb("gate", [P, 1])
        pass_on = m.sb("pass_on", [P, 1])
        weight = m.sb("weight", [P, EXPERTS])
        parts = m.sb("parts", [P, EXPERTS, D])
        y = m.sb("y", [P, D])
        z = m.sb("z", [P, D])
        z_pre = m.sb("z_pre", [P, D])
        z_stats = m.sb("z_stats", [P, 6])
        z_mean_var = m.sb("z_mean_var", [P, 2])
        z_var_eps = m.sb("z_var_eps", [P, 1])
        z_rstd = m.sb("z_rstd", [P, 1])
        zn = m.sb("zn", [P, D])
        zg = m.sb("zg", [P, D])
        xb = m.sb("xb", [P, D])

        small_ps = m.ps("small", [P, 512])
        qkv_ps = m.ps("qkv", [P, 4, P])
        score_ps = m.ps("score", [P, PER_TILE, CHUNKS * SEQ])
        turn_ps = m.ps("turn", [P, PER_TILE, 512])
        exp_ps = m.ps("exp", [P, EXPERTS, D])

        loaded = m.sem("loaded")
        masks_filled = m.sem("masks_filled")
        masks_done = m.sem("masks_done")
        w_turned = m.sem("w_turned")
        w_done = m.sem("w_done")
        stats_done, mean_done, var_done = m.sem("stats_done"), m.sem("mean_done"), m.sem("var_done")
        rstd_done, e_done, e_kept = m.sem("rstd_done"), m.sem("e_done"), m.sem("e_kept")
        e_turned, e_t_done = m.sem("e_turned"), m.sem("e_t_done")
        qk_filled, v_filled = m.sem("qk_filled"), m.sem("v_filled")
        qk_done, v_done = m.sem("qk_done"), m.sem("v_done")
        q_block_done, scored, masked = m.sem("q_block_done"), m.sem("scored"), m.sem("masked")
        top_done, shifted, exp_done = m.sem("top_done"), m.sem("shifted"), m.sem("exp_done")
        prob_turned, prob_t_done, mixed = m.sem("prob_turned"), m.sem("prob_t_done"), m.sem("mixed")
        share_done, hid_raw_done, hid_done = m.sem("share_done"), m.sem("hid_raw_done"), m.sem("hid_done")
        hid_turned, hid_t_done, routed = m.sem("hid_turned"), m.sem("hid_t_done"), m.sem("routed")
        experts_done, parts_done = m.sem("experts_done"), m.sem("parts_done")
        logit_done, best_done, place_done = m.sem("logit_done"), m.sem("best_done"), m.sem("place_done")
        less_done, sum_done, chosen_done = m.sem("less_done"), m.sem("sum_done"), m.sem("chosen_done")
        counted, order_done, position_done = m.sem("counted"), m.sem("order_done"), m.sem("position_done")
        kept_done, route_done, gate_done = m.sem("kept_done"), m.sem("route_done"), m.sem("gate_done")
        pick_done, pass_done = m.sem("pick_done"), m.sem("pass_done")
        weight_done, seen_done = m.sem("weight_done"), m.sem("seen_done")
        y_done, z_pre_done, z_done = m.sem("y_done"), m.sem("z_pre_done"), m.sem("z_done")
        z_stats_done, z_mean_done, z_var_done = m.sem("z_stats_done"), m.sem("z_mean_done"), m.sem("z_var_done")
        z_rstd_done, zn_done, zg_done = m.sem("z_rstd_done"), m.sem("zn_done"), m.sem("zg_done")
        xb_done, x_done = m.sem("xb_done"), m.sem("x_done")
        be_step = m.sem("be_step")

        block = ctx.enter_context(nc.Block())
        LOADS = 12

        @block.sync
        def _(sp):
            for n, name in enumerate(("Wq", "Wk", "Wv")):
                sp.dma_start(w_in[:, n, :], dram[f"L0_ffn_{name}"].rearrange("h e d -> (h e) d")).then_inc(loaded, DMA)
            sp.dma_start(w_in[:, 3:, :], dram["L0_ffn_We"].rearrange("x e d -> e x d")).then_inc(loaded, DMA)
            sp.dma_start(wsw_in[:, :], dram["L0_ffn_Wsw"]).then_inc(loaded, DMA)
            for to, name in ((bq, "bq"), (bk, "bk")):
                sp.dma_start(to[:, :], dram[f"L0_ffn_{name}"].rearrange("h (e o) -> (h e) o", o=1)).then_inc(loaded, DMA)
            sp.dma_start(bv[:, :], dram["L0_ffn_bv"].rearrange("h e -> (h e)").partition_broadcast(P)).then_inc(loaded, DMA)
            for to, name in ((gamma, "gamma"), (beta, "beta"), (bsw, "bsw")):
                sp.dma_start(to[:, :], dram[f"L0_ffn_{name}"].partition_broadcast(P)).then_inc(loaded, DMA)
            flat_be = dram["L0_ffn_be"].rearrange("(o x) d -> o (x d)", o=1)
            sp.dma_start(be[0:1, :], flat_be).then_inc(loaded, DMA)

        @block.tensor
        def _(pe):
            pe.wait_ge(loaded, LOADS * DMA)
            for n in range(3 + EXPERTS):
                if n >= 4 and n % 4 == 0:
                    pe.wait_ge(w_done, n // 4)
                last = pe.transpose(small_ps[:, n % 4 * P:n % 4 * P + P], w_in[:, n, :], ident[:, :])
                if n % 4 == 3 or n == 2 + EXPERTS:
                    last.then_inc(w_turned, 1)
            pe.wait_ge(w_done, 3)
            pe.transpose(small_ps[:, 0:EXPERTS], wsw_in[:, :], ident[0:EXPERTS, 0:EXPERTS]).then_inc(w_turned, 1)
            pe.wait_ge(w_done, 4)
            pe.wait_ge(masks_done, 6)
            pe.wait_ge(be_step, 11)

            def scores(t):
                pe.wait_ge(q_block_done, 2 * t.index + 2)
                wait(pe, masked, t.index)
                for b in range(PER_TILE):
                    for c in range(CHUNKS):
                        for h in range(2):
                            last = pe.matmul(score_ps[h * SEQ:(h + 1) * SEQ, b, c * SEQ:(c + 1) * SEQ],
                                             q_block[:, t.odd, b, 2 * c + h, :],
                                             qk[:, t.odd, 1, b * SEQ:(b + 1) * SEQ], start=True, stop=True)
                last.then_inc(scored, 1)

            def turn_prob(t):
                pe.wait_ge(exp_done, t.index + 1)
                wait(pe, hid_raw_done, t.index)
                for b in range(PER_TILE):
                    for c in range(PAIRS):
                        h = b * CHUNKS + 2 * c
                        last = pe.transpose(turn_ps[:, b, c * P:(c + 1) * P], expo[:, t.odd, h:h + 2, :], ident[:, :])
                last.then_inc(prob_turned, 1)

            def mix(t):
                pe.wait_ge(prob_t_done, t.index + 1)
                pe.wait_ge(v_done, t.index + 1)
                for b in range(PER_TILE):
                    for c in range(PAIRS):
                        at = (b * PAIRS + c) * 2 * VCOL
                        last = pe.matmul(turn_ps[:, 0, at:at + 2 * VCOL], prob_t[:, t.odd, b, c, :],
                                         v_block[:, t.odd, b, c, :, :], start=True, stop=True)
                last.then_inc(mixed, 1)

            def turn_hidden(t):
                pe.wait_ge(hid_done, t.index + 1)
                wait(pe, order_done, t.index)
                at = t.index + 4
                pe.wait_ge(e_t_done, min(at, TILES) if isinstance(at, int) else at)
                pe.transpose(small_ps[:, P:2 * P], hid[:, t.odd, :], ident[:, :]).then_inc(hid_turned, 1)

            def experts(t, half):
                part = slice(half * 4, half * 4 + 4)
                if half == 0:
                    pe.wait_ge(hid_t_done, t.index + 1)
                    at = t.index + 5
                    pe.wait_ge(e_t_done, min(at, TILES) if isinstance(at, int) else at)
                    pe.matmul(small_ps[:, 256:256 + EXPERTS], hid_t[:, t.odd, :], wsw_t[:, :], start=True,
                              stop=True).then_inc(routed, 1)
                    wait(pe, parts_done, t.index)
                pe.matmul(exp_ps[:, part, :], hid_t[:, t.odd, :], w_t[:, 3 + half * 4:7 + half * 4, :], start=True,
                          stop=False)
                pe.matmul(exp_ps[:, part, :], be_ones[:, :], be_parts[:, half * 512:half * 512 + 512],
                          start=False, stop=True).then_inc(experts_done, 1)

            def count(t):
                pe.wait_ge(chosen_done, t.index + 1)
                wait(pe, seen_done, t.index)
                pe.matmul(small_ps[:, 264:264 + EXPERTS], upto[:, :], chosen_b[:, :], start=True, stop=False)
                pe.matmul(small_ps[:, 264:264 + EXPERTS], ones[:, :], seen[:, :], start=False, stop=True).then_inc(counted, 1)

            def turn_in(t):
                pe.wait_ge(e_done, t.index + 1)
                wait(pe, e_t_done, t.index)
                wait(pe, order_done, t.index - 4)
                pe.transpose(small_ps[:, 0:P], e_now[:, t.odd, :], ident[:, :]).then_inc(e_turned, 1)

            def project_qk(t):
                pe.wait_ge(e_t_done, t.index + 1)
                wait(pe, v_done, t.index)
                pe.matmul(qkv_ps[:, 0, :], w_t[:, 0, :], e_t[:, t.odd, :], start=True, stop=True)
                pe.matmul(qkv_ps[:, 1, :], w_t[:, 1, :], e_t[:, t.odd, :], start=True, stop=True).then_inc(qk_filled, 1)

            def project_v(t):
                pe.wait_ge(qk_done, t.index + 1)
                pe.matmul(qkv_ps[:, 2, :], e_t[:, t.odd, :], w_t[:, 2, :], start=True, stop=True).then_inc(v_filled, 1)

            def step(t):
                now, one, two, three, four = t, t.back(1), t.back(2), t.back(3), t.back(4)
                if one.live:
                    project_qk(one)
                if two.live:
                    scores(two)
                if now.live:
                    turn_in(now)
                if four.live:
                    turn_hidden(four)
                if three.live:
                    turn_prob(three)
                if one.live:
                    project_v(one)
                if four.live:
                    experts(four, 0)
                if three.live:
                    mix(three)
                if four.live:
                    experts(four, 1)
                    count(four)

            over_tiles(pe, step, 4)

        @block.scalar
        def _(act):
            for n in range(3):
                lo, hi = 4 * n, min(4 * n + 4, 3 + EXPERTS)
                act.wait_ge(w_turned, n + 1)
                act.copy(w_t[:, lo:hi, :], small_ps[:, 0:(hi - lo) * P]).then_inc(w_done, 1)
            act.wait_ge(w_turned, 4)
            act.copy(wsw_t[:, :], small_ps[:, 0:EXPERTS]).then_inc(w_done, 1)
            act.wait_ge(loaded, LOADS * DMA)
            act.wait_ge(be_step, 11)

            def bring_hidden(t):
                act.wait_ge(hid_turned, t.index + 1)
                wait(act, experts_done, 2 * t.index - 2)
                act.copy(hid_t[:, t.odd, :], small_ps[:, P:2 * P]).then_inc(hid_t_done, 1)

            def bring_prob(t):
                act.wait_ge(prob_turned, t.index + 1)
                wait(act, mixed, t.index - 1)
                act.copy(prob_t[:, t.odd, :, :, :], turn_ps[:, :, :]).then_inc(prob_t_done, 1)

            def route_exp(t):
                act.wait_ge(less_done, t.index + 1)
                wait(act, route_done, t.index)
                act.activation(e_logit[:, :], logit[:, :], ACT.Exp, bias=less_best[:, :],
                               accum_out=e_sum[:, :]).then_inc(sum_done, 1)

            def exponent(t):
                act.wait_ge(shifted, t.index + 1)
                act.activation(expo[:, t.odd, :, :], expo[:, t.odd, :, :], ACT.Exp, scale=D ** -0.5).then_inc(exp_done, 1)

            def weigh(t):
                act.wait_ge(weight_done, t.index + 1)
                act.wait_ge(experts_done, 2 * t.index + 2)
                wait(act, y_done, t.index)
                for n in range(EXPERTS):
                    last = act.activation(parts[:, n, :], exp_ps[:, n, :], ACT.Copy, scale=weight[:, n:n + 1])
                last.then_inc(parts_done, 1)

            def bring_in(t):
                act.wait_ge(e_turned, t.index + 1)
                wait(act, v_filled, t.index - 1)
                act.copy(e_t[:, t.odd, :], small_ps[:, 0:P]).then_inc(e_t_done, 1)
                act.copy(e_all[:, t.index, :], e_now[:, t.odd, :]).then_inc(e_kept, 1)

            def bring_qk(t):
                act.wait_ge(qk_filled, t.index + 1)
                wait(act, scored, t.index - 1)
                act.activation(qk[:, t.odd, 0, :], qkv_ps[:, 0, :], ACT.Identity, bias=bq[:, :])
                act.activation(qk[:, t.odd, 1, :], qkv_ps[:, 1, :], ACT.Identity, bias=bk[:, :]).then_inc(qk_done, 1)

            def bring_v(t):
                act.wait_ge(v_filled, t.index + 1)
                wait(act, mixed, t.index - 1)
                for b in range(PER_TILE):
                    for p in range(2):
                        frm = qkv_ps[b * SEQ:(b + 1) * SEQ, 2, :].rearrange("k (c p m) -> k c p m", p=2, m=2 * HD)[:, :, p, :]
                        last = act.copy(v_block[p * SEQ:(p + 1) * SEQ, t.odd, b, :, p, 0:2 * HD], frm)
                last.then_inc(v_done, 1)

            def step(t):
                now, one, three, four, five = t, t.back(1), t.back(3), t.back(4), t.back(5)
                if one.live:
                    bring_qk(one)
                if three.live:
                    exponent(three)
                if five.live:
                    weigh(five)
                if four.live:
                    bring_hidden(four)
                if now.live:
                    bring_in(now)
                if three.live:
                    bring_prob(three)
                if four.live:
                    route_exp(four)
                if one.live:
                    bring_v(one)

            over_tiles(act, step, 5)

        @block.vector
        def _(dve):
            dve.wait_ge(loaded, LOADS * DMA)
            dve.memset(be_parts[:, :], 0.0).then_inc(be_step, 1)
            dve.memset(be_ones[:, :], 1.0).then_inc(be_step, 1)
            dve.memset(v_block[:, :, :, :, :, :], 0.0).then_inc(be_step, 1)
            dve.memset(seen[:, :], 0.0).then_inc(be_step, 1)
            dve.wait_ge(be_step, 4)
            for p in range(2):
                dve.memset(v_block[p * SEQ:(p + 1) * SEQ, :, :, :, p, 2 * HD:VCOL], 1.0).then_inc(be_step, 1)
            for n in range(3):
                row = slice(32 * n, 32 * n + 1)
                dve.tensor_copy(be_parts[row, :], be[row, :]).then_inc(be_step, 1)
                dve.wait_ge(be_step, 7 + 2 * n)
                if n < 2:
                    nxt = slice(32 * n + 32, 32 * n + 33)
                    dve.tensor_tensor(be[nxt, :], be[row, :], be_parts[row, :], ALU.subtract).then_inc(be_step, 1)
                    dve.wait_ge(be_step, 8 + 2 * n)

            def moments(t):
                dve.bn_stats(stats[:, t.odd, :], x[:, t.index, :]).then_inc(stats_done, 1)
                dve.wait_ge(stats_done, t.index + 1)
                wait(dve, e_done, t.index - 1)
                apart(dve)
                dve.bn_aggr(mean_var[:, t.odd, :], stats[:, t.odd, :]).then_inc(mean_done, 1)
                dve.wait_ge(mean_done, t.index + 1)
                wait(dve, rstd_done, t.index - 1)
                dve.tensor_scalar(var_eps[:, t.odd:t.odd + 1], mean_var[:, t.odd, 1:2], EPS, None,
                                  ALU.add).then_inc(var_done, 1)

            def normalize(t):
                dve.wait_ge(rstd_done, t.index + 1)
                wait(dve, e_turned, t.index - 1)
                wait(dve, e_kept, t.index - 1)
                dve.tensor_scalar(e_now[:, t.odd, :], x[:, t.index, :], mean_var[:, t.odd, 0:1],
                                  rstd[:, t.odd:t.odd + 1], ALU.subtract, ALU.mult).then_inc(e_done, 1)

            def mask(t):
                dve.wait_ge(scored, t.index + 1)
                wait(dve, shifted, t.index - 1)
                s = score_ps[:, :, :].rearrange("p b (c k) -> p (b c) k", k=SEQ)
                dve.tensor_tensor(score[:, t.odd, :, :], s, many(causal[:, :], HEADS, 1), ALU.mult).then_inc(masked, 1)
                dve.wait_ge(masked, t.index + 1)
                dve.tensor_reduce(top[:, t.odd, :], score[:, t.odd, :, :], AX.X, ALU.max).then_inc(top_done, 1)

            def route(t):
                dve.wait_ge(routed, t.index + 1)
                wait(dve, sum_done, t.index)
                dve.tensor_tensor(logit[:, :], small_ps[:, 256:256 + EXPERTS], bsw[:, :], ALU.add).then_inc(logit_done, 1)
                dve.wait_ge(logit_done, t.index + 1)
                apart(dve)
                dve.max(best[:, :], logit[:, :]).then_inc(best_done, 1)
                dve.wait_ge(best_done, t.index + 1)
                dve.tensor_scalar(less_best[:, :], best[:, 0:1], -1.0, None, ALU.mult).then_inc(less_done, 1)
                apart(dve)
                dve.max_index(place[:, :], best[:, :], logit[:, :]).then_inc(place_done, 1)
                dve.wait_ge(place_done, t.index + 1)
                wait(dve, weight_done, t.index)
                dve.tensor_tensor(chosen[:, :], number[:, :], place[:, 0:1].to_broadcast([P, EXPERTS]),
                                  ALU.is_equal).then_inc(pick_done, 1)
                dve.wait_ge(pick_done, t.index + 1)
                wait(dve, seen_done, t.index)
                dve.tensor_copy(chosen_b[:, :], chosen[:, :]).then_inc(chosen_done, 1)

            def admit(t):
                dve.wait_ge(counted, t.index + 1)
                dve.tensor_tensor(order[:, :], small_ps[:, 264:264 + EXPERTS], chosen[:, :], ALU.mult).then_inc(order_done, 1)
                dve.tensor_tensor(seen[:, :], seen[:, :], chosen_b[:, :], ALU.add).then_inc(seen_done, 1)
                dve.wait_ge(order_done, t.index + 1)
                dve.tensor_reduce(position[:, :], order[:, :], AX.X, ALU.add).then_inc(position_done, 1)
                dve.wait_ge(sum_done, t.index + 1)
                dve.reciprocal(route_prob[:, :], e_sum[:, :]).then_inc(route_done, 1)
                dve.wait_ge(position_done, t.index + 1)
                dve.tensor_scalar(kept[:, :], position[:, :], float(CAPACITY), None, ALU.is_le).then_inc(kept_done, 1)
                dve.wait_ge(kept_done, t.index + 1)
                dve.wait_ge(route_done, t.index + 1)
                dve.tensor_tensor(gate[:, :], kept[:, :], route_prob[:, :], ALU.mult).then_inc(gate_done, 1)
                dve.wait_ge(gate_done, t.index + 1)
                dve.tensor_tensor(pass_on[:, :], route_prob[:, :], gate[:, :], ALU.subtract).then_inc(pass_done, 1)
                wait(dve, parts_done, t.index)
                dve.tensor_scalar(weight[:, :], chosen[:, :], gate[:, :], None, ALU.mult).then_inc(weight_done, 1)

            def take_hidden(t):
                dve.wait_ge(mixed, t.index + 1)
                sums = turn_ps[:, 0, 0:PER_TILE * PAIRS * 2 * VCOL].rearrange("p (b n m) -> p b n m", b=PER_TILE, m=VCOL)
                dve.reciprocal(share[:, t.odd, :, :], sums[:, :, :, 2 * HD:VCOL].rearrange("p b n o -> p b (n o)")).then_inc(share_done, 1)
                dve.wait_ge(share_done, t.index + 1)
                wait(dve, hid_done, t.index - 1)
                for b in range(PER_TILE):
                    for h in range(2):
                        rows = slice(h * SEQ, (h + 1) * SEQ)
                        to = hid_raw[b * SEQ:(b + 1) * SEQ, t.odd, :].rearrange("q (n h d) -> q n h d", h=2, d=HD)[:, :, h, :]
                        last = dve.tensor_tensor(to, sums[rows, b, :, h * HD:(h + 1) * HD],
                                                 many(share[rows, t.odd, b, :], HD), ALU.mult)
                last.then_inc(hid_raw_done, 1)

            def finish(t):
                dve.wait_ge(parts_done, t.index + 1)
                dve.tensor_reduce(y[:, :], parts[:, :, :].rearrange("p x f -> p f x"), AX.X, ALU.add).then_inc(y_done, 1)
                dve.wait_ge(y_done, t.index + 1)
                dve.wait_ge(pass_done, t.index + 1)
                dve.scalar_tensor_tensor(z_pre[:, :], hid[:, t.odd, :], pass_on[:, 0:1], y[:, :], ALU.mult,
                                         ALU.add).then_inc(z_pre_done, 1)
                dve.wait_ge(z_pre_done, t.index + 1)
                dve.wait_ge(e_kept, t.index + 1)
                wait(dve, zn_done, t.index)
                dve.tensor_tensor(z[:, :], z_pre[:, :], e_all[:, t.index, :], ALU.add).then_inc(z_done, 1)
                dve.wait_ge(z_done, t.index + 1)
                dve.bn_stats(z_stats[:, :], z[:, :]).then_inc(z_stats_done, 1)
                dve.wait_ge(z_stats_done, t.index + 1)
                apart(dve)
                dve.bn_aggr(z_mean_var[:, :], z_stats[:, :]).then_inc(z_mean_done, 1)
                dve.wait_ge(z_mean_done, t.index + 1)
                dve.tensor_scalar(z_var_eps[:, :], z_mean_var[:, 1:2], EPS, None, ALU.add).then_inc(z_var_done, 1)

            def finish_scale(t):
                dve.wait_ge(z_rstd_done, t.index + 1)
                wait(dve, zg_done, t.index)
                dve.tensor_scalar(zn[:, :], z[:, :], z_mean_var[:, 0:1], z_rstd[:, 0:1], ALU.subtract,
                                  ALU.mult).then_inc(zn_done, 1)

            def step(t):
                now, two, four, five, six = t, t.back(2), t.back(4), t.back(5), t.back(6)
                if five.live:
                    admit(five)
                if now.live:
                    moments(now)
                if four.live:
                    take_hidden(four)
                if six.live:
                    finish_scale(six)
                if now.live:
                    normalize(now)
                if two.live:
                    mask(two)
                if four.live:
                    route(four)
                if five.live:
                    finish(five)

            over_tiles(dve, step, 6)

        @block.gpsimd
        def _(pool):
            pool.memset(head_of[:, :], 1.0).then_inc(masks_filled, 1)
            pool.memset(causal[:, :], 1.0).then_inc(masks_filled, 1)
            pool.memset(upto[:, :], 1.0).then_inc(masks_filled, 1)
            pool.memset(ones[:, :], 1.0).then_inc(masks_done, 1)
            pool.iota(number[:, :], pattern=[[1, EXPERTS]], base=0, channel_multiplier=0,
                      allow_small_or_imprecise_dtypes=True).then_inc(masks_done, 1)
            pool.wait_ge(masks_filled, 3)
            pool.affine_select(out=head_of[:, :], in_=head_of[:, :], compare_op=ALU.is_ge, fill=0.0, base=0,
                               pattern=[[-HD, HEADS]], channel_multiplier=1).then_inc(masks_filled, 1)
            pool.wait_ge(masks_filled, 4)
            pool.affine_select(out=head_of[:, :], in_=head_of[:, :], compare_op=ALU.is_ge, fill=0.0, base=HD - 1,
                               pattern=[[HD, HEADS]], channel_multiplier=-1).then_inc(masks_done, 1)
            for h in range(2):
                pool.wait_ge(masks_done, 3 + h)
                rows = causal[h * SEQ:(h + 1) * SEQ, :]
                pool.affine_select(out=rows, in_=rows, compare_op=ALU.is_ge, fill=0.0, base=0,
                                   pattern=[[-1, SEQ]], channel_multiplier=1).then_inc(masks_done, 1)
            pool.wait_ge(masks_done, 5)
            pool.affine_select(out=upto[:, :], in_=upto[:, :], compare_op=ALU.is_ge, fill=0.0, base=0,
                               pattern=[[1, P]], channel_multiplier=-1).then_inc(masks_done, 1)
            pool.wait_ge(masks_done, 6)
            pool.wait_ge(loaded, LOADS * DMA)

            def scale_root(t):
                pool.wait_ge(var_done, t.index + 1)
                pool.tensor_tensor(rstd[:, t.odd:t.odd + 1], var_eps[:, t.odd:t.odd + 1], eps_pow[:, :],
                                   ALU.pow).then_inc(rstd_done, 1)

            def shift(t):
                pool.wait_ge(top_done, t.index + 1)
                wait(pool, prob_turned, t.index - 1)
                pool.tensor_tensor(expo[:, t.odd, :, :], score[:, t.odd, :, :], many(top[:, t.odd, :], SEQ),
                                   ALU.subtract).then_inc(shifted, 1)

            def spread_q(t):
                pool.wait_ge(qk_done, t.index + 1)
                wait(pool, scored, t.index - 1)
                for b in range(PER_TILE):
                    pool.tensor_tensor(q_block[:, t.odd, b, :, :], many(qk[:, t.odd, 0, b * SEQ:(b + 1) * SEQ], HEADS, 1),
                                       many(head_of[:, :], SEQ), ALU.mult).then_inc(q_block_done, 1)

            def bias_hidden(t):
                pool.wait_ge(hid_raw_done, t.index + 1)
                wait(pool, z_pre_done, t.index - 1)
                wait(pool, hid_turned, t.index - 1)
                pool.tensor_tensor(hid[:, t.odd, :], hid_raw[:, t.odd, :], bv[:, :], ALU.add).then_inc(hid_done, 1)

            def bias_x(t):
                wait(pool, x_done, t.index)
                pool.tensor_tensor(xb[:, :], x[:, t.index, :], beta[:, :], ALU.add).then_inc(xb_done, 1)

            def scale_z_root(t):
                pool.wait_ge(z_var_done, t.index + 1)
                pool.tensor_tensor(z_rstd[:, :], z_var_eps[:, :], eps_pow[:, :], ALU.pow).then_inc(z_rstd_done, 1)

            def finish(t):
                pool.wait_ge(zn_done, t.index + 1)
                pool.tensor_tensor(zg[:, :], zn[:, :], gamma[:, :], ALU.mult).then_inc(zg_done, 1)
                pool.wait_ge(zg_done, t.index + 1)
                pool.wait_ge(xb_done, t.index + 1)
                apart(pool)
                pool.tensor_tensor(x[:, t.index, :], xb[:, :], zg[:, :], ALU.add).then_inc(x_done, 1)

            def step(t):
                now, one, two, four, five, six = t, t.back(1), t.back(2), t.back(4), t.back(5), t.back(6)
                if now.live:
                    scale_root(now)
                if four.live:
                    bias_hidden(four)
                if six.live:
                    finish(six)
                if one.live:
                    spread_q(one)
                if five.live:
                    bias_x(five)
                if two.live:
                    shift(two)
                if five.live:
                    scale_z_root(five)

            over_tiles(pool, step, 6)


def masked_attention(nc, dram, keep):
    ctx = ExitStack()
    with ctx:
        m = Memory(nc, ctx, "mask")
        x, ident, eps_pow = keep["x"], keep["ident"], keep["eps_pow"]
        w_in = m.sb("w_in", [P, 4, D])
        w_t = m.sb("w_t", [P, 4, D])
        bq = m.sb("bq", [P, 1])
        bk = m.sb("bk", [P, 1])
        bv = m.sb("bv", [P, D])
        bo = m.sb("bo", [P, D])
        head_of = m.sb("head_of", [P, HEADS])
        ctx_in = m.sb("ctx_in", [P, 2, D])
        valid = m.sb("valid", [P, 2, PER_TILE, SEQ])

        stats = m.sb("stats", [P, 2, 6])
        mean_var = m.sb("mean_var", [P, 2, 2])
        var_eps = m.sb("var_eps", [P, 2])
        rstd = m.sb("rstd", [P, 2])
        xn = m.sb("xn", [P, 2, D])
        xc_t = m.sb("xc_t", [P, 2, 2, P])
        qk = m.sb("qk", [P, 2, 2, P])
        q_block = m.sb("q_block", [P, 2, PER_TILE, HEADS, SEQ])
        v_block = m.sb("v_block", [P, 2, PER_TILE, PAIRS, 2, VCOL])
        score = m.sb("score", [P, 2, HEADS, SEQ])
        top = m.sb("top", [P, 2, HEADS])
        expo = m.sb("expo", [P, 2, HEADS, SEQ])
        prob_t = m.sb("prob_t", [P, 2, PER_TILE, PAIRS, P])
        share = m.sb("share", [P, 2, PER_TILE, CHUNKS])
        out_raw = m.sb("out_raw", [P, 2, D])
        out = m.sb("out", [P, 2, D])
        out_t = m.sb("out_t", [P, 2, P])

        turn_in_ps = m.ps("turn_in", [P, 4, P])
        qk_ps = m.ps("qk", [P, 4, P])
        score_ps = m.ps("score", [P, PER_TILE, CHUNKS * SEQ])
        turn_ps = m.ps("turn", [P, PER_TILE, 512])
        v_ps = m.ps("v", [P, 512])
        mix_ps = m.ps("mix", [P, 512])

        loaded, zeroed = m.sem("loaded"), m.sem("zeroed")
        masks_filled, masks_done = m.sem("masks_filled"), m.sem("masks_done")
        ctx_loaded = [m.sem(f"ctx_loaded{i}") for i in range(2)]
        w_turned, w_done, valid_done = m.sem("w_turned"), m.sem("w_done"), m.sem("valid_done")
        stats_done, mean_done, var_done = m.sem("stats_done"), m.sem("mean_done"), m.sem("var_done")
        rstd_done, xn_done, x_biased = m.sem("rstd_done"), m.sem("xn_done"), m.sem("x_biased")
        turned_in, xc_done = m.sem("turned_in"), m.sem("xc_done")
        qk_filled, v_filled = m.sem("qk_filled"), m.sem("v_filled")
        qk_done, v_done = m.sem("qk_done"), m.sem("v_done")
        scored, masked = m.sem("scored"), m.sem("masked")
        q_block_done = [m.sem(f"q_block_done{i}") for i in range(PER_TILE)]
        top_done, shifted, exp_done = m.sem("top_done"), m.sem("shifted"), m.sem("exp_done")
        prob_turned, prob_t_done, mixed = m.sem("prob_turned"), m.sem("prob_t_done"), m.sem("mixed")
        share_done, out_raw_done, out_done = m.sem("share_done"), m.sem("out_raw_done"), m.sem("out_done")
        out_turned, out_t_done, up_done, x_done = m.sem("out_turned"), m.sem("out_t_done"), m.sem("up_done"), m.sem("x_done")

        ctx_tiles = dram["ctx_1024"].rearrange("b s d -> (b s) d").rearrange("(t p) d -> t p d", p=P)
        block = ctx.enter_context(nc.Block())
        LOADS = 8

        @block.sync
        def _(sp):
            for n, name in enumerate(("Wq", "Wk", "Wv", "Wo")):
                sp.dma_start(w_in[:, n, :], dram[f"L1_xattn_{name}"]).then_inc(loaded, DMA)
            for to, name in ((bq, "bq"), (bk, "bk")):
                sp.dma_start(to[:, :], dram[f"L1_xattn_{name}"].rearrange("(e o) -> e o", o=1)).then_inc(loaded, DMA)
            for to, name in ((bv, "bv"), (bo, "bo")):
                sp.dma_start(to[:, :], dram[f"L1_xattn_{name}"].partition_broadcast(P)).then_inc(loaded, DMA)
            sp.dma_start(ctx_in[:, 0, :], ctx_tiles[0]).then_inc(ctx_loaded[0], DMA)
            sp.dma_start(ctx_in[:, 1, :], ctx_tiles[1]).then_inc(ctx_loaded[1], DMA)

            def step(t):
                u = t.back(-2)
                sp.wait_ge(turned_in, t.index + 1)
                sp.dma_start(ctx_in[:, u.odd, :], ctx_tiles[u.index]).then_inc(ctx_loaded[u.odd], DMA)

            with sp.Fori(0, TILES // 2 - 1) as group:
                step(Tile(group, 0))
                step(Tile(group, 1))

        @block.tensor
        def _(pe):
            pe.wait_ge(loaded, LOADS * DMA)
            for n in range(4):
                last = pe.transpose(turn_in_ps[:, n, :], w_in[:, n, :], ident[:, :])
            last.then_inc(w_turned, 1)
            pe.wait_ge(w_done, 1)
            pe.wait_ge(zeroed, 3)

            def scores(t):
                for b in range(PER_TILE):
                    pe.wait_ge(q_block_done[b], t.index + 1)
                wait(pe, masked, 2 * t.index)
                for b in range(PER_TILE):
                    for c in range(CHUNKS):
                        for h in range(2):
                            last = pe.matmul(score_ps[h * SEQ:(h + 1) * SEQ, b, c * SEQ:(c + 1) * SEQ],
                                             q_block[:, t.odd, b, 2 * c + h, :],
                                             qk[:, t.odd, 1, b * SEQ:(b + 1) * SEQ], start=True, stop=True)
                last.then_inc(scored, 1)

            def turn_prob(t):
                pe.wait_ge(exp_done, t.index + 1)
                wait(pe, prob_t_done, t.index)
                for b in range(PER_TILE):
                    for c in range(PAIRS):
                        h = b * CHUNKS + 2 * c
                        last = pe.transpose(turn_ps[:, b, c * P:(c + 1) * P], expo[:, t.odd, h:h + 2, :], ident[:, :])
                last.then_inc(prob_turned, 1)

            def mix(t):
                pe.wait_ge(prob_t_done, t.index + 1)
                pe.wait_ge(v_done, t.index + 1)
                wait(pe, out_raw_done, t.index)
                for b in range(PER_TILE):
                    for c in range(PAIRS):
                        at = (b * PAIRS + c) * 2 * VCOL
                        last = pe.matmul(mix_ps[:, at:at + 2 * VCOL], prob_t[:, t.odd, b, c, :],
                                         v_block[:, t.odd, b, c, :, :], start=True, stop=True)
                last.then_inc(mixed, 1)

            def turn_out(t):
                pe.wait_ge(out_done, t.index + 1)
                wait(pe, x_done, t.index)
                pe.transpose(turn_in_ps[:, 2, :], out[:, t.odd, :], ident[:, :]).then_inc(out_turned, 1)

            def up(t):
                pe.wait_ge(out_t_done, t.index + 1)
                at = t.index + 6
                pe.wait_ge(xc_done, min(at, TILES) if isinstance(at, int) else at)
                pe.matmul(turn_in_ps[:, 3, :], out_t[:, t.odd, :], w_t[:, 3, :], start=True, stop=True).then_inc(up_done, 1)

            def turn_in(t):
                pe.wait_ge(xn_done, t.index + 1)
                pe.wait_ge(ctx_loaded[t.odd], (t.group + 1) * DMA)
                wait(pe, xc_done, t.index)
                wait(pe, x_done, t.index - 5)
                pe.transpose(turn_in_ps[:, 0, :], xn[:, t.odd, :], ident[:, :])
                pe.transpose(turn_in_ps[:, 1, :], ctx_in[:, t.odd, :], ident[:, :]).then_inc(turned_in, 1)

            def project_qk(t):
                pe.wait_ge(xc_done, t.index + 1)
                wait(pe, qk_done, t.index)
                pe.matmul(qk_ps[:, 0, :], w_t[:, 0, :], xc_t[:, t.odd, 0, :], start=True, stop=True)
                pe.matmul(qk_ps[:, 1, :], w_t[:, 1, :], xc_t[:, t.odd, 1, :], start=True, stop=True).then_inc(qk_filled, 1)

            def project_v(t):
                wait(pe, v_done, t.index)
                pe.matmul(v_ps[:, 0:D], xc_t[:, t.odd, 1, :], w_t[:, 2, :], start=True, stop=True).then_inc(v_filled, 1)

            def step(t):
                now, one, two, three, four, five, six = t, t.back(1), t.back(2), t.back(3), t.back(4), t.back(5), t.back(6)
                if one.live:
                    project_qk(one)
                if six.live:
                    up(six)
                if two.live:
                    project_v(two)
                if four.live:
                    mix(four)
                if two.live:
                    scores(two)
                if now.live:
                    turn_in(now)
                if five.live:
                    turn_out(five)
                if three.live:
                    turn_prob(three)

            over_tiles(pe, step, 6)

        @block.scalar
        def _(act):
            act.wait_ge(w_turned, 1)
            act.copy(w_t[:, :, :], turn_in_ps[:, :, :]).then_inc(w_done, 1)
            act.wait_ge(loaded, LOADS * DMA)
            act.wait_ge(zeroed, 3)

            def bring_out(t):
                act.wait_ge(out_turned, t.index + 1)
                wait(act, up_done, t.index - 1)
                act.copy(out_t[:, t.odd, :], turn_in_ps[:, 2, :]).then_inc(out_t_done, 1)

            def bring_prob(t):
                act.wait_ge(prob_turned, t.index + 1)
                wait(act, mixed, t.index - 1)
                act.copy(prob_t[:, t.odd, :, :, :], turn_ps[:, :, :]).then_inc(prob_t_done, 1)

            def exponent(t):
                act.wait_ge(shifted, t.index + 1)
                act.activation(expo[:, t.odd, :, :], expo[:, t.odd, :, :], ACT.Exp, scale=D ** -0.5).then_inc(exp_done, 1)

            def bring_in(t):
                act.wait_ge(turned_in, t.index + 1)
                wait(act, v_filled, t.index - 1)
                act.copy(xc_t[:, t.odd, :, :], turn_in_ps[:, 0:2, :]).then_inc(xc_done, 1)

            def bring_qk(t):
                act.wait_ge(qk_filled, t.index + 1)
                wait(act, scored, t.index - 1)
                for b in range(PER_TILE):
                    wait(act, q_block_done[b], t.index - 1)
                act.activation(qk[:, t.odd, 0, :], qk_ps[:, 0, :], ACT.Identity, bias=bq[:, :])
                act.activation(qk[:, t.odd, 1, :], qk_ps[:, 1, :], ACT.Identity, bias=bk[:, :]).then_inc(qk_done, 1)

            def bring_v(t):
                act.wait_ge(v_filled, t.index + 1)
                wait(act, mixed, t.index - 1)
                for b in range(PER_TILE):
                    for p in range(2):
                        frm = v_ps[b * SEQ:(b + 1) * SEQ, 0:D].rearrange("k (c p m) -> k c p m", p=2, m=2 * HD)[:, :, p, :]
                        last = act.copy(v_block[p * SEQ:(p + 1) * SEQ, t.odd, b, :, p, 0:2 * HD], frm)
                last.then_inc(v_done, 1)

            def step(t):
                now, one, two, three, five = t, t.back(1), t.back(2), t.back(3), t.back(5)
                if one.live:
                    bring_qk(one)
                if two.live:
                    bring_v(two)
                if three.live:
                    exponent(three)
                if five.live:
                    bring_out(five)
                if now.live:
                    bring_in(now)
                if three.live:
                    bring_prob(three)

            over_tiles(act, step, 5)

        @block.vector
        def _(dve):
            dve.memset(v_block[:, :, :, :, :, :], 0.0).then_inc(zeroed, 1)
            dve.wait_ge(zeroed, 1)
            for p in range(2):
                dve.memset(v_block[p * SEQ:(p + 1) * SEQ, :, :, :, p, 2 * HD:VCOL], 1.0).then_inc(zeroed, 1)
            dve.wait_ge(loaded, LOADS * DMA)
            dve.wait_ge(masks_done, 1)
            dve.wait_ge(keep["mask_loaded"], 2 * DMA)

            def moments(t):
                dve.bn_stats(stats[:, t.odd, :], x[:, t.index, :]).then_inc(stats_done, 1)
                dve.wait_ge(stats_done, t.index + 1)
                wait(dve, xn_done, t.index - 1)
                apart(dve)
                dve.bn_aggr(mean_var[:, t.odd, :], stats[:, t.odd, :]).then_inc(mean_done, 1)
                dve.wait_ge(mean_done, t.index + 1)
                wait(dve, rstd_done, t.index - 1)
                dve.tensor_scalar(var_eps[:, t.odd:t.odd + 1], mean_var[:, t.odd, 1:2], EPS, None,
                                  ALU.add).then_inc(var_done, 1)

            def normalize(t):
                dve.wait_ge(rstd_done, t.index + 1)
                wait(dve, turned_in, t.index - 1)
                dve.tensor_scalar(xn[:, t.odd, :], x[:, t.index, :], mean_var[:, t.odd, 0:1],
                                  rstd[:, t.odd:t.odd + 1], ALU.subtract, ALU.mult).then_inc(xn_done, 1)

            def mask(t):
                dve.wait_ge(scored, t.index + 1)
                dve.wait_ge(valid_done, t.index + 1)
                wait(dve, shifted, t.index - 1)
                for b in range(PER_TILE):
                    dve.scalar_tensor_tensor(
                        score[:, t.odd, b * CHUNKS:(b + 1) * CHUNKS, :],
                        score_ps[:, b, :].rearrange("p (c k) -> p c k", k=SEQ), 1e-20,
                        many(valid[:, t.odd, b, :], CHUNKS, 1), ALU.subtract, ALU.mult).then_inc(masked, 1)
                dve.wait_ge(masked, 2 * t.index + 2)
                dve.tensor_reduce(top[:, t.odd, :], score[:, t.odd, :, :], AX.X, ALU.max).then_inc(top_done, 1)

            def take_out(t):
                dve.wait_ge(mixed, t.index + 1)
                sums = mix_ps[:, 0:PER_TILE * PAIRS * 2 * VCOL].rearrange("p (b n m) -> p b n m", b=PER_TILE, m=VCOL)
                dve.reciprocal(share[:, t.odd, :, :], sums[:, :, :, 2 * HD:VCOL].rearrange("p b n o -> p b (n o)")).then_inc(share_done, 1)
                dve.wait_ge(share_done, t.index + 1)
                wait(dve, out_done, t.index - 1)
                for b in range(PER_TILE):
                    for h in range(2):
                        rows = slice(h * SEQ, (h + 1) * SEQ)
                        to = out_raw[b * SEQ:(b + 1) * SEQ, t.odd, :].rearrange("q (n h d) -> q n h d", h=2, d=HD)[:, :, h, :]
                        last = dve.tensor_tensor(to, sums[rows, b, :, h * HD:(h + 1) * HD],
                                                 many(share[rows, t.odd, b, :], HD), ALU.mult)
                last.then_inc(out_raw_done, 1)

            def residual(t):
                dve.wait_ge(up_done, t.index + 1)
                dve.wait_ge(x_biased, t.index + 1)
                dve.tensor_tensor(x[:, t.index, :], turn_in_ps[:, 3, :], x[:, t.index, :], ALU.add).then_inc(x_done, 1)

            def spread_q(t):
                dve.wait_ge(qk_done, t.index + 1)
                wait(dve, scored, t.index - 1)
                dve.tensor_tensor(q_block[:, t.odd, 1, :, :], many(qk[:, t.odd, 0, SEQ:P], HEADS, 1),
                                  many(head_of[:, :], SEQ), ALU.mult).then_inc(q_block_done[1], 1)

            def find_valid(t):
                wait(dve, masked, 2 * t.index - 2)
                dve.tensor_scalar(valid[:, t.odd, :, :].rearrange("p b k -> p (b k)"),
                                  keep["mask"][:, t.index, :], 0, None, ALU.not_equal).then_inc(valid_done, 1)

            def step(t):
                now, one, two, four, six = t, t.back(1), t.back(2), t.back(4), t.back(6)
                if now.live:
                    moments(now)
                if one.live:
                    find_valid(one)
                    spread_q(one)
                if now.live:
                    normalize(now)
                if four.live:
                    take_out(four)
                if six.live:
                    residual(six)
                if two.live:
                    mask(two)

            over_tiles(dve, step, 6)

        @block.gpsimd
        def _(pool):
            pool.memset(head_of[:, :], 1.0).then_inc(masks_filled, 1)
            pool.wait_ge(masks_filled, 1)
            pool.affine_select(out=head_of[:, :], in_=head_of[:, :], compare_op=ALU.is_ge, fill=0.0, base=0,
                               pattern=[[-HD, HEADS]], channel_multiplier=1).then_inc(masks_filled, 1)
            pool.wait_ge(masks_filled, 2)
            pool.affine_select(out=head_of[:, :], in_=head_of[:, :], compare_op=ALU.is_ge, fill=0.0, base=HD - 1,
                               pattern=[[HD, HEADS]], channel_multiplier=-1).then_inc(masks_done, 1)
            pool.wait_ge(masks_done, 1)
            pool.wait_ge(loaded, LOADS * DMA)

            def shift(t):
                pool.wait_ge(top_done, t.index + 1)
                wait(pool, prob_turned, t.index - 1)
                pool.tensor_tensor(expo[:, t.odd, :, :], score[:, t.odd, :, :], many(top[:, t.odd, :], SEQ),
                                   ALU.subtract).then_inc(shifted, 1)

            def spread_q(t):
                pool.wait_ge(qk_done, t.index + 1)
                wait(pool, scored, t.index - 1)
                pool.tensor_tensor(q_block[:, t.odd, 0, :, :], many(qk[:, t.odd, 0, 0:SEQ], HEADS, 1),
                                   many(head_of[:, :], SEQ), ALU.mult).then_inc(q_block_done[0], 1)

            def scale_root(t):
                pool.wait_ge(var_done, t.index + 1)
                pool.tensor_tensor(rstd[:, t.odd:t.odd + 1], var_eps[:, t.odd:t.odd + 1], eps_pow[:, :],
                                   ALU.pow).then_inc(rstd_done, 1)

            def bias_x(t):
                pool.wait_ge(xn_done, t.index + 1)
                pool.tensor_tensor(x[:, t.index, :], x[:, t.index, :], bo[:, :], ALU.add).then_inc(x_biased, 1)

            def bias_out(t):
                pool.wait_ge(out_raw_done, t.index + 1)
                wait(pool, out_turned, t.index - 1)
                pool.tensor_tensor(out[:, t.odd, :], out_raw[:, t.odd, :], bv[:, :], ALU.add).then_inc(out_done, 1)

            def step(t):
                now, one, three, four = t, t.back(1), t.back(3), t.back(4)
                if three.live:
                    shift(three)
                if now.live:
                    scale_root(now)
                if one.live:
                    spread_q(one)
                if now.live:
                    bias_x(now)
                if four.live:
                    bias_out(four)

            over_tiles(pool, step, 4)


def load_mlp(nc, dram, keep):
    with ExitStack() as ctx:
        m = Memory(nc, ctx, "load")
        rows = EXPERTS * BLOCKS + EXPERTS
        bias = m.sb("bias", [rows, P])
        rest = m.sb("rest", [rows, 2, P])
        part = m.sb("part", [rows, 3, P], BF16)
        loaded, split = m.sem("loaded"), m.sem("split")
        block = ctx.enter_context(nc.Block())

        @block.sync
        def _(sp):
            sp.dma_start(bias[0:EXPERTS * BLOCKS, :], dram["L1_ffn_b_in"].rearrange("x (c m) -> (x c) m", m=P)).then_inc(loaded, DMA)
            sp.dma_start(bias[EXPERTS * BLOCKS:rows, :], dram["L1_ffn_b_out"]).then_inc(loaded, DMA)
            sp.wait_ge(split, 6)
            for n in range(3):
                sp.dma_start(keep["b_parts"][32 * n:32 * n + 1, :], part[:, n, :]).then_inc(keep["b_loaded"], DMA)
            sp.wait_ge(keep["b_loaded"], 3 * DMA)

        @block.vector
        def _(dve):
            dve.memset(keep["b_parts"][:, :].bitcast(U32), 0).then_inc(split, 1)
            dve.wait_ge(loaded, 2 * DMA)
            dve.tensor_copy(part[:, 0, :], bias[:, :]).then_inc(split, 1)
            dve.wait_ge(split, 2)
            dve.tensor_tensor(rest[:, 0, :], bias[:, :], part[:, 0, :], ALU.subtract).then_inc(split, 1)
            dve.wait_ge(split, 3)
            dve.tensor_copy(part[:, 1, :], rest[:, 0, :]).then_inc(split, 1)
            dve.wait_ge(split, 4)
            dve.tensor_tensor(rest[:, 1, :], rest[:, 0, :], part[:, 1, :], ALU.subtract).then_inc(split, 1)
            dve.wait_ge(split, 5)
            dve.tensor_copy(part[:, 2, :], rest[:, 1, :]).then_inc(split, 1)

        @block.scalar
        def _(act):
            for n in range(EXPERTS):
                act.dma_start(keep["w_in"][:, n, :], dram["L1_ffn_W_in"][n]).then_inc(keep["w_loaded"], DMA)
                act.dma_start(keep["w_out"][:, n, :, :],
                              dram["L1_ffn_W_out"][n].rearrange("(c m) d -> m c d", m=P)).then_inc(keep["w_loaded"], DMA)


def select_experts(nc, dram, keep):
    ctx = ExitStack()
    with ctx:
        m = Memory(nc, ctx, "sel")
        x, ident, eps_pow = keep["x"], keep["ident"], keep["eps_pow"]
        picked, place, share, table = keep["picked"], keep["place"], keep["share"], keep["table"]
        gate_w = m.sb("gate_w", [P, EXPERTS])
        upto = m.sb("upto", [P, P], BF16)
        ones = m.sb("ones", [P, P], BF16)
        number = m.sb("number", [P, EXPERTS])
        region = m.sb("region", [P, EXPERTS])
        lane = m.sb("lane", [P, 1])
        blank = m.sb("blank", [P, P])
        seen = m.sb("seen", [P, EXPERTS], BF16)

        stats = m.sb("stats", [P, 2, 6])
        mean_var = m.sb("mean_var", [P, 2, 2])
        var_eps = m.sb("var_eps", [P, 2])
        rstd = m.sb("rstd", [P, 2])
        xn = m.sb("xn", [P, 2, D])
        xn_out = m.sb("xn_out", [P, 2, D])
        xn_t = m.sb("xn_t", [P, 2, P])
        logit = m.sb("logit", [P, 2, EXPERTS])
        best = m.sb("best", [P, 2, 8])
        which = m.sb("which", [P, 2, 8], U32)
        less_best = m.sb("less_best", [P, 2, 1])
        second = m.sb("second", [P, 2, 1])
        both = m.sb("both", [P, 2, 1])
        taken = m.sb("taken", [P, 2, EXPERTS], BF16)
        order = m.sb("order", [P, 2, EXPERTS])
        spread = m.sb("spread", [P, 2, TOP, EXPERTS])
        row = m.sb("row", [P, 2, TOP])
        row_i = m.sb("row_i", [P, 2, TOP], I32)
        total = m.sb("total", [P, EXPERTS])
        pad = m.sb("pad", [P, EXPERTS])
        pad_row = m.sb("pad_row", [P, EXPERTS])
        pad_i = m.sb("pad_i", [P, EXPERTS], I32)
        steps = m.sb("steps", [P, TILES])
        over = m.sb("over", [P, EXPERTS, TILES])
        tiles = m.sb("tiles", [P, EXPERTS])
        unit = m.sb("unit", [P, EXPERTS])
        end = m.sb("end", [P, EXPERTS])
        start = m.sb("start", [P, EXPERTS])
        first_row = m.sb("first_row", [P, EXPERTS])
        index = m.sb("index", [P, SORTED])
        past = m.sb("past", [P, SORTED, EXPERTS])
        owner = m.sb("owner", [P, SORTED])
        own = m.sb("own", [P, SORTED, EXPERTS])
        from_row = m.sb("from_row", [P, SORTED])
        real = m.sb("real", [P, SORTED])
        every = m.sb("every", [P, TILES * TOP, EXPERTS])
        every_row = m.sb("every_row", [P, TILES * TOP])
        every_all = m.sb("every_all", [P, TILES * TOP])

        norm_ps = m.ps("norm", [P, 512])
        logit_ps = m.ps("logit", [P, 512])
        count_ps = m.ps("count", [P, 512])

        loaded, filled, ready = m.sem("loaded"), m.sem("filled"), m.sem("ready")
        stats_done, mean_done, var_done = m.sem("stats_done"), m.sem("mean_done"), m.sem("var_done")
        rstd_done, xn_done, turned, xn_t_done = m.sem("rstd_done"), m.sem("xn_done"), m.sem("turned"), m.sem("xn_t_done")
        xn_copied = m.sem("xn_copied")
        gated, logit_done, best_done, which_done = m.sem("gated"), m.sem("logit_done"), m.sem("best_done"), m.sem("which_done")
        less_done, second_done, both_done = m.sem("less_done"), m.sem("second_done"), m.sem("both_done")
        share_first, share_done = m.sem("share_first"), m.sem("share_done")
        picked_done, taken_done, counted = m.sem("picked_done"), m.sem("taken_done"), m.sem("counted")
        order_done, seen_done, spread_done = m.sem("order_done"), m.sem("seen_done"), m.sem("spread_done")
        place_done, row_done, row_i_done = m.sem("place_done"), m.sem("row_done"), m.sem("row_i_done")
        scattered = [m.sem(f"scattered{i}") for i in range(2)]
        totaled, plan, padded = m.sem("totaled"), m.sem("plan"), m.sem("padded")

        block = ctx.enter_context(nc.Block())

        @block.sync
        def _(sp):
            sp.dma_start(gate_w[:, :], dram["L1_ffn_W_gate"]).then_inc(loaded, DMA)

        @block.tensor
        def _(pe):
            pe.wait_ge(loaded, DMA)
            pe.wait_ge(ready, 8)

            def turn(t):
                pe.wait_ge(xn_done, t.index + 1)
                wait(pe, xn_t_done, t.index)
                pe.transpose(norm_ps[:, 0:P], xn[:, t.odd, :], ident[:, :]).then_inc(turned, 1)

            def gate(t):
                pe.wait_ge(xn_t_done, t.index + 1)
                wait(pe, logit_done, t.index)
                pe.matmul(logit_ps[:, 0:EXPERTS], xn_t[:, t.odd, :], gate_w[:, :], start=True, stop=True).then_inc(gated, 1)

            def count(t):
                pe.wait_ge(taken_done, t.index + 1)
                wait(pe, seen_done, t.index)
                wait(pe, order_done, t.index)
                pe.matmul(count_ps[:, 0:EXPERTS], upto[:, :], taken[:, t.odd, :], start=True, stop=False)
                pe.matmul(count_ps[:, 0:EXPERTS], ones[:, :], seen[:, :], start=False, stop=True).then_inc(counted, 1)

            def step(t):
                one, two = t.back(1), t.back(2)
                if two.live:
                    count(two)
                if one.live:
                    gate(one)
                if t.live:
                    turn(t)

            over_tiles(pe, step, 2)
            pe.wait_ge(seen_done, TILES)
            pe.wait_ge(order_done, TILES)
            pe.matmul(count_ps[:, 0:EXPERTS], ones[:, :], seen[:, :], start=True, stop=True).then_inc(totaled, 1)

        @block.scalar
        def _(act):
            def step(t):
                one, two = t.back(1), t.back(2)
                if one.live:
                    act.wait_ge(xn_done, one.index + 1)
                    wait(act, scattered[one.odd], one.group * TOP * DMA)
                    act.copy(xn_out[:, one.odd, :], xn[:, one.odd, :]).then_inc(xn_copied, 1)
                if two.live:
                    act.wait_ge(less_done, two.index + 1)
                    wait(act, share_done, two.index - 1)
                    act.activation(second[:, two.odd, :], best[:, two.odd, 1:2], ACT.Exp,
                                   bias=less_best[:, two.odd, :]).then_inc(second_done, 1)
                if t.live:
                    act.wait_ge(turned, t.index + 1)
                    wait(act, gated, t.index - 1)
                    act.copy(xn_t[:, t.odd, :], norm_ps[:, 0:P]).then_inc(xn_t_done, 1)

            over_tiles(act, step, 2)

        @block.vector
        def _(dve):
            dve.memset(seen[:, :], 0.0).then_inc(ready, 1)
            dve.memset(blank[:, :], 0.0).then_inc(ready, 1)
            dve.memset(unit[:, :], 1.0).then_inc(ready, 1)
            dve.wait_ge(ready, 8)

            def moments(t):
                dve.bn_stats(stats[:, t.odd, :], x[:, t.index, :]).then_inc(stats_done, 1)
                dve.wait_ge(stats_done, t.index + 1)
                wait(dve, xn_done, t.index - 1)
                apart(dve)
                dve.bn_aggr(mean_var[:, t.odd, :], stats[:, t.odd, :]).then_inc(mean_done, 1)
                dve.wait_ge(mean_done, t.index + 1)
                wait(dve, rstd_done, t.index - 1)
                dve.tensor_scalar(var_eps[:, t.odd:t.odd + 1], mean_var[:, t.odd, 1:2], EPS, None,
                                  ALU.add).then_inc(var_done, 1)

            def normalize(t):
                dve.wait_ge(rstd_done, t.index + 1)
                wait(dve, turned, t.index - 1)
                wait(dve, xn_copied, t.index - 1)
                dve.tensor_scalar(xn[:, t.odd, :], x[:, t.index, :], mean_var[:, t.odd, 0:1],
                                  rstd[:, t.odd:t.odd + 1], ALU.subtract, ALU.mult).then_inc(xn_done, 1)

            def choose(t):
                o = t.odd
                dve.wait_ge(gated, t.index + 1)
                dve.tensor_copy(logit[:, o, :], logit_ps[:, 0:EXPERTS]).then_inc(logit_done, 1)
                dve.wait_ge(logit_done, t.index + 1)
                wait(dve, second_done, t.index - 1)
                apart(dve)
                dve.max(best[:, o, :], logit[:, o, :]).then_inc(best_done, 1)
                dve.wait_ge(best_done, t.index + 1)
                apart(dve)
                dve.max_index(which[:, o, :], best[:, o, :], logit[:, o, :]).then_inc(which_done, 1)
                dve.tensor_scalar(less_best[:, o, :], best[:, o, 0:1], -1.0, None, ALU.mult).then_inc(less_done, 1)
                dve.wait_ge(which_done, t.index + 1)
                dve.tensor_tensor(picked[:, t.index, :, :], many(number[:, :], TOP, 1),
                                  many(which[:, o, 0:TOP], EXPERTS), ALU.is_equal).then_inc(picked_done, 1)
                dve.wait_ge(picked_done, t.index + 1)
                wait(dve, counted, t.index - 1)
                dve.tensor_tensor(taken[:, o, :], picked[:, t.index, 0, :], picked[:, t.index, 1, :],
                                  ALU.add).then_inc(taken_done, 1)

            def address(t):
                o = t.odd
                dve.wait_ge(counted, t.index + 1)
                dve.tensor_scalar(order[:, o, :], count_ps[:, 0:EXPERTS], -1.0, None, ALU.add).then_inc(order_done, 1)
                dve.tensor_tensor(seen[:, :], seen[:, :], taken[:, o, :], ALU.add).then_inc(seen_done, 1)
                dve.wait_ge(order_done, t.index + 1)
                dve.tensor_tensor(spread[:, o, :, :], picked[:, t.index, :, :], many(order[:, o, :], TOP, 1),
                                  ALU.mult).then_inc(spread_done, 1)
                dve.wait_ge(spread_done, 2 * t.index + 1)
                dve.tensor_reduce(place[:, t.index, :], spread[:, o, :, :], AX.X, ALU.add).then_inc(place_done, 1)
                dve.wait_ge(place_done, t.index + 1)
                dve.tensor_tensor(spread[:, o, :, :], picked[:, t.index, :, :], many(region[:, :], TOP, 1),
                                  ALU.mult).then_inc(spread_done, 1)
                dve.wait_ge(spread_done, 2 * t.index + 2)
                dve.tensor_reduce(row[:, o, :], spread[:, o, :, :], AX.X, ALU.add).then_inc(row_done, 1)
                dve.wait_ge(row_done, t.index + 1)
                wait(dve, scattered[o], t.group * TOP * DMA)
                dve.tensor_tensor(row_i[:, o, :], row[:, o, :], place[:, t.index, :], ALU.add).then_inc(row_i_done, 1)
                dve.wait_ge(second_done, t.index + 1)
                dve.tensor_scalar(both[:, o, :], second[:, o, :], 1.0, None, ALU.add).then_inc(both_done, 1)
                dve.wait_ge(both_done, t.index + 1)
                dve.reciprocal(share[:, t.index, 0:1], both[:, o, :]).then_inc(share_first, 1)
                dve.wait_ge(share_first, t.index + 1)
                dve.tensor_tensor(share[:, t.index, 1:2], share[:, t.index, 0:1], second[:, o, :],
                                  ALU.mult).then_inc(share_done, 1)

            def step(t):
                one, two = t.back(1), t.back(2)
                if t.live:
                    moments(t)
                if one.live:
                    choose(one)
                if t.live:
                    normalize(t)
                if two.live:
                    address(two)

            over_tiles(dve, step, 2)

            dve.wait_ge(totaled, 1)
            dve.tensor_copy(total[:, :], count_ps[:, 0:EXPERTS]).then_inc(plan, 1)
            dve.wait_ge(plan, 1)
            dve.tensor_tensor(pad[:, :], total[:, :], region[:, :], ALU.add).then_inc(plan, 1)
            dve.wait_ge(plan, 2)
            dve.tensor_scalar(pad_i[:, :], pad[:, :], lane[:, 0:1], None, ALU.add).then_inc(plan, 1)
            dve.tensor_tensor(over[:, :, :], many(total[:, :], TILES), many(steps[:, :], EXPERTS, 1),
                              ALU.is_gt).then_inc(plan, 1)
            dve.wait_ge(plan, 4)
            dve.tensor_reduce(tiles[:, :], over[:, :, :], AX.X, ALU.add).then_inc(plan, 1)
            dve.wait_ge(plan, 5)
            dve.tensor_tensor_scan(end[:, :], unit[:, :], tiles[:, :], 0.0, ALU.mult, ALU.add).then_inc(plan, 1)
            dve.wait_ge(plan, 6)
            dve.tensor_tensor(start[:, :], end[:, :], tiles[:, :], ALU.subtract).then_inc(plan, 1)
            dve.tensor_tensor(past[:, :, :], many(index[:, :], EXPERTS), many(end[:, :], SORTED, 1),
                              ALU.is_ge).then_inc(plan, 1)
            dve.wait_ge(plan, 8)
            dve.tensor_reduce(owner[:, :], past[:, :, :], AX.X, ALU.add).then_inc(plan, 1)
            dve.scalar_tensor_tensor(first_row[:, :], start[:, :], -float(P), region[:, :], ALU.mult,
                                     ALU.add).then_inc(plan, 1)
            dve.wait_ge(plan, 10)
            dve.tensor_tensor(own[:, :, :], many(owner[:, :], EXPERTS), many(number[:, :], SORTED, 1),
                              ALU.is_equal).then_inc(plan, 1)
            dve.wait_ge(plan, 11)
            dve.tensor_tensor(own[:, :, :], own[:, :, :], many(first_row[:, :], SORTED, 1), ALU.mult).then_inc(plan, 1)
            dve.wait_ge(plan, 12)
            dve.tensor_reduce(from_row[:, :], own[:, :, :], AX.X, ALU.add).then_inc(plan, 1)
            dve.tensor_scalar(real[:, :], owner[:, :], float(EXPERTS), None, ALU.is_lt).then_inc(plan, 1)
            dve.tensor_scalar(table[:, 0, :], owner[:, :], float(EXPERTS - 1), None, ALU.min).then_inc(plan, 1)
            dve.wait_ge(plan, 15)
            dve.scalar_tensor_tensor(from_row[:, :], index[:, :], float(P), from_row[:, :], ALU.mult,
                                     ALU.add).then_inc(plan, 1)
            dve.wait_ge(plan, 16)
            dve.tensor_tensor(table[:, 1, :], from_row[:, :], real[:, :], ALU.mult).then_inc(plan, 1)
            dve.tensor_tensor(every[:, :, :], picked[:, :, :, :].rearrange("p t k x -> p (t k) x"),
                              many(start[:, :], TILES * TOP, 1), ALU.mult).then_inc(plan, 1)
            dve.wait_ge(plan, 18)
            dve.tensor_reduce(every_row[:, :], every[:, :, :], AX.X, ALU.add).then_inc(plan, 1)
            dve.wait_ge(plan, 19)
            dve.scalar_tensor_tensor(keep["result_row"][:, :, :].rearrange("p t k -> p (t k)"), every_row[:, :], float(P),
                                     place[:, :, :].rearrange("p t k -> p (t k)"), ALU.mult, ALU.add).then_inc(plan, 1)

        @block.gpsimd
        def _(pool):
            pool.memset(upto[:, :], 1.0).then_inc(filled, 1)
            pool.memset(ones[:, :], 1.0).then_inc(ready, 1)
            pool.iota(number[:, :], pattern=[[1, EXPERTS]], base=0, channel_multiplier=0,
                      allow_small_or_imprecise_dtypes=True).then_inc(filled, 1)
            pool.iota(region[:, :], pattern=[[REGION, EXPERTS]], base=0, channel_multiplier=0,
                      allow_small_or_imprecise_dtypes=True).then_inc(ready, 1)
            pool.iota(lane[:, :], pattern=[[0, 1]], base=0, channel_multiplier=1,
                      allow_small_or_imprecise_dtypes=True).then_inc(ready, 1)
            pool.iota(steps[:, :], pattern=[[P, TILES]], base=0, channel_multiplier=0,
                      allow_small_or_imprecise_dtypes=True).then_inc(ready, 1)
            pool.iota(index[:, :], pattern=[[1, SORTED]], base=0, channel_multiplier=0,
                      allow_small_or_imprecise_dtypes=True).then_inc(filled, 1)
            pool.wait_ge(filled, 3)
            pool.affine_select(out=upto[:, :], in_=upto[:, :], compare_op=ALU.is_ge, fill=0.0, base=0,
                               pattern=[[1, P]], channel_multiplier=-1).then_inc(ready, 1)

            def scatter(t):
                pool.wait_ge(row_i_done, t.index + 1)
                pool.wait_ge(xn_copied, t.index + 1)
                apart(pool)
                for k in range(TOP):
                    pool.indirect_dma_start(keep["sorted"], bass.IndirectOffsetOnAxis(ap=row_i[:, t.odd, k:k + 1], axis=0),
                                            xn_out[:, t.odd, :], None).then_inc(scattered[t.odd], DMA)

            def step(t):
                two = t.back(2)
                if t.live:
                    pool.wait_ge(var_done, t.index + 1)
                    pool.tensor_tensor(rstd[:, t.odd:t.odd + 1], var_eps[:, t.odd:t.odd + 1], eps_pow[:, :],
                                       ALU.pow).then_inc(rstd_done, 1)
                if two.live:
                    scatter(two)

            over_tiles(pool, step, 2)
            pool.wait_ge(plan, 3)
            for n in range(EXPERTS):
                pool.indirect_dma_start(keep["sorted"], bass.IndirectOffsetOnAxis(ap=pad_i[:, n:n + 1], axis=0),
                                        blank[:, :], None).then_inc(padded, DMA)
            pool.wait_ge(padded, EXPERTS * DMA)
            for o in range(2):
                pool.wait_ge(scattered[o], TILES // 2 * TOP * DMA)
            pool.wait_ge(plan, 20)


def run_experts(nc, dram, keep):
    ctx = ExitStack()
    with ctx:
        m = Memory(nc, ctx, "run")
        ident, w_in, w_out, b_parts, table = (keep[n] for n in ("ident", "w_in", "w_out", "b_parts", "table"))
        BUFS = 4
        ones = m.sb("ones", [96, P], BF16)
        xs = m.sb("xs", [P, BUFS, D])
        xs_t = m.sb("xs_t", [P, 2, P])
        hid = m.sb("hid", [P, 2, MLP])
        hid_t = m.sb("hid_t", [P, 2, BLOCKS, P])
        y = m.sb("y", [P, BUFS, D])
        turn_ps = m.ps("turn", [P, 512])
        hid_ps = [m.ps(f"hid{i}", [P, MLP]) for i in range(2)]
        hid_t_ps = [m.ps(f"hid_t{i}", [P, BLOCKS, P]) for i in range(2)]
        y_ps = [m.ps(f"y{i}", [P, 512]) for i in range(2)]

        ready = m.sem("ready")
        xs_loaded = [m.sem(f"xs_loaded{i}") for i in range(BUFS)]
        stored = [m.sem(f"stored{i}") for i in range(BUFS)]
        turned, xs_t_done, hid_summed, hid_done = m.sem("turned"), m.sem("xs_t_done"), m.sem("hid_summed"), m.sem("hid_done")
        hid_turned, hid_t_done, y_summed, y_done = m.sem("hid_turned"), m.sem("hid_t_done"), m.sem("y_summed"), m.sem("y_done")

        sorted_rows, result = keep["sorted"], keep["result"].rearrange("(t p) d -> t p d", p=P)
        block = ctx.enter_context(nc.Block())

        @block.sync
        def _(sp):
            def store(t):
                sp.wait_ge(y_done, t.index + 1)
                sp.dma_start(result[t.index], y[:, t.at, :]).then_inc(stored[t.at], DMA)

            def load(t):
                wait(sp, turned, t.index - BUFS + 1)
                at = sp.value_load(table[0:1, 1, t.index:t.index + 1] if isinstance(t.index, int) else
                                   table[0:1, 1, bass.ds(t.index, 1)], min_val=0, max_val=EXPERTS * REGION - P)
                sp.dma_start(xs[:, t.at, :], sorted_rows[bass.ds(at, P), :]).then_inc(xs_loaded[t.at], DMA)

            def step(t):
                eight = t.back(8)
                if t.live:
                    load(t)
                if eight.live:
                    store(eight)

            over_tiles(sp, step, 8, SORTED, BUFS)
            for i in range(BUFS):
                sp.wait_ge(stored[i], SORTED // BUFS * DMA)

        @block.tensor
        def _(pe):
            pe.wait_ge(keep["w_loaded"], 2 * EXPERTS * DMA)
            pe.wait_ge(ready, 1)

            def owner(t):
                return pe.value_load(table[0:1, 0, bass.ds(t.index, 1)], min_val=0, max_val=EXPERTS - 1)

            def turn(t):
                pe.wait_ge(xs_loaded[t.at], (t.group + 1) * DMA)
                wait(pe, xs_t_done, t.index)
                pe.transpose(turn_ps[:, 0:P], xs[:, t.at, :], ident[:, :]).then_inc(turned, 1)

            def widen(t, n):
                pe.wait_ge(xs_t_done, t.index + 1)
                wait(pe, hid_done, t.index - 1)
                pe.matmul(hid_ps[t.odd][:, :], ones[:, :], b_parts[:, bass.ds(n * MLP, MLP)], start=True, stop=False)
                pe.matmul(hid_ps[t.odd][:, :], xs_t[:, t.odd, :], w_in[:, n, :], start=False, stop=True).then_inc(hid_summed, 1)

            def turn_hidden(t):
                pe.wait_ge(hid_done, t.index + 1)
                wait(pe, hid_t_done, t.index - 1)
                for c in range(BLOCKS):
                    last = pe.transpose(hid_t_ps[t.odd][:, c, :], hid[:, t.odd, c * P:(c + 1) * P], ident[:, :])
                last.then_inc(hid_turned, 1)

            def narrow(t, n):
                pe.wait_ge(hid_t_done, t.index + 1)
                wait(pe, y_done, t.index - 1)
                pe.matmul(y_ps[t.odd][:, 0:D], ones[:, :], b_parts[:, bass.ds(n * D + EXPERTS * MLP, D)], start=True, stop=False)
                for c in range(BLOCKS):
                    last = pe.matmul(y_ps[t.odd][:, 0:D], hid_t[:, t.odd, c, :], w_out[:, n, c, :],
                                     start=False, stop=(c == BLOCKS - 1))
                last.then_inc(y_summed, 1)

            def step(t):
                one, two, three = t.back(1), t.back(2), t.back(3)
                if one.live:
                    widen(one, owner(one))
                if two.live:
                    turn_hidden(two)
                if t.live:
                    turn(t)
                if three.live:
                    narrow(three, owner(three))

            over_tiles(pe, step, 3, SORTED, BUFS)

        @block.scalar
        def _(act):
            def step(t):
                one = t.back(1)
                if one.live:
                    act.wait_ge(hid_summed, one.index + 1)
                    wait(act, hid_turned, one.index - 1)
                    act.activation(hid[:, one.odd, :], hid_ps[one.odd][:, :], ACT.Gelu).then_inc(hid_done, 1)
                if t.live:
                    act.wait_ge(turned, t.index + 1)
                    wait(act, hid_summed, t.index - 1)
                    act.copy(xs_t[:, t.odd, :], turn_ps[:, 0:P]).then_inc(xs_t_done, 1)

            over_tiles(act, step, 1, SORTED, BUFS)

        @block.vector
        def _(dve):
            dve.memset(ones[:, :], 1.0).then_inc(ready, 1)

            def step(t):
                two, three = t.back(2), t.back(3)
                if two.live:
                    dve.wait_ge(hid_turned, two.index + 1)
                    wait(dve, y_summed, two.index - 1)
                    dve.tensor_copy(hid_t[:, two.odd, :, :], hid_t_ps[two.odd][:, :, :]).then_inc(hid_t_done, 1)
                if three.live:
                    dve.wait_ge(y_summed, three.index + 1)
                    wait(dve, stored[three.at], three.group * DMA)
                    dve.tensor_copy(y[:, three.at, :], y_ps[three.odd][:, 0:D]).then_inc(y_done, 1)

            over_tiles(dve, step, 3, SORTED, BUFS)


def combine(nc, dram, keep, out):
    ctx = ExitStack()
    with ctx:
        m = Memory(nc, ctx, "comb")
        x, share = keep["x"], keep["share"]
        BUFS = 4
        got = [m.sb(f"got{i}", [P, TOP, D]) for i in range(BUFS)]
        gathered = [m.sem(f"gathered{i}") for i in range(BUFS)]
        first_done, x_done, written = m.sem("first_done"), m.sem("x_done"), m.sem("written")
        out_tiles = out.rearrange("b s d -> (b s) d").rearrange("(t p) d -> p t d", p=P)
        WRITES = 8
        block = ctx.enter_context(nc.Block())

        @block.gpsimd
        def _(pool):
            def step(r, b):
                wait(pool, x_done, r * BUFS + b + 1 - BUFS)
                for k in range(TOP):
                    pool.indirect_dma_start(
                        got[b][:, k, :], None, keep["result"],
                        bass.IndirectOffsetOnAxis(ap=keep["result_row"][:, r * BUFS + b, k:k + 1], axis=0)).then_inc(gathered[b], DMA)

            for r in range(TILES // BUFS):
                for b in range(BUFS):
                    step(r, b)

        @block.vector
        def _(dve):
            def step(r, b):
                t = r * BUFS + b
                dve.wait_ge(gathered[b], (r + 1) * TOP * DMA)
                dve.scalar_tensor_tensor(x[:, t, :], got[b][:, 0, :], share[:, t, 0:1], x[:, t, :], ALU.mult,
                                         ALU.add).then_inc(first_done, 1)
                dve.wait_ge(first_done, t + 1)
                dve.scalar_tensor_tensor(x[:, t, :], got[b][:, 1, :], share[:, t, 1:2], x[:, t, :], ALU.mult,
                                         ALU.add).then_inc(x_done, 1)

            for r in range(TILES // BUFS):
                for b in range(BUFS):
                    step(r, b)

        @block.sync
        def _(sp):
            for n in range(WRITES):
                part = slice(n * TILES // WRITES, (n + 1) * TILES // WRITES)
                sp.wait_ge(x_done, part.stop)
                sp.dma_start(out_tiles[:, part, :], x[:, part, :]).then_inc(written, DMA)
            sp.wait_ge(keep["mask_loaded"], 2 * DMA)
            sp.wait_ge(written, WRITES * DMA)


def setup(nc, dram, keep):
    x, ident, eps_pow = keep["x"], keep["ident"], keep["eps_pow"]
    x_tiles = dram["x"].rearrange("b s d -> (b s) d").rearrange("(t p) d -> p t d", p=P)
    mask_rows = dram["mask_Bx1xSxS2_ik1"].rearrange("b o q k -> q (b o) k")
    with nc.Block() as block:

        @block.sync
        def _(sp):
            for n in range(4):
                part = slice(n * TILES // 4, (n + 1) * TILES // 4)
                sp.dma_start(x[:, part, :], x_tiles[:, part, :]).then_inc(keep["x_loaded"], DMA)

        @block.scalar
        def _(act):
            for h in range(2):
                act.dma_start(keep["mask"][h * SEQ:(h + 1) * SEQ, :, :].rearrange("q t (b k) -> q (t b) k", b=PER_TILE),
                              mask_rows).then_inc(keep["mask_loaded"], DMA)

        @block.gpsimd
        def _(pool):
            pool.memset(eps_pow[:, :], -0.5).then_inc(keep["ident_ready"], 1)
            pool.memset(ident[:, :], 0.0).then_inc(keep["ident_ready"], 1)
            pool.wait_ge(keep["ident_ready"], 2)
            pool.affine_select(out=ident[:, :], in_=ident[:, :], compare_op=ALU.not_equal, fill=1.0, base=0,
                               pattern=[[-1, P]], channel_multiplier=1).then_inc(keep["ident_ready"], 1)


def network(nc, dram, out):
    ctx = ExitStack()
    with ctx:
        m = Memory(nc, ctx, "net")
        keep = {
            "x": m.sb("x", [P, TILES, D]), "ident": m.sb("ident", [P, P]), "eps_pow": m.sb("eps_pow", [P, 1]),
            "mask": m.sb("mask", [P, TILES, PER_TILE * SEQ], I32), "x_loaded": m.sem("x_loaded"),
            "mask_loaded": m.sem("mask_loaded"), "ident_ready": m.sem("ident_ready"), "ident_count": 3,
            "w_in": m.sb("w_in", [P, EXPERTS, MLP]), "w_out": m.sb("w_out", [P, EXPERTS, BLOCKS, D]),
            "b_parts": m.sb("b_parts", [96, EXPERTS * (MLP + D)], BF16),
            "w_loaded": m.sem("w_loaded"), "b_loaded": m.sem("b_loaded"),
            "picked": m.sb("picked", [P, TILES, TOP, EXPERTS]), "place": m.sb("place", [P, TILES, TOP]),
            "share": m.sb("share", [P, TILES, TOP]), "table": m.sb("table", [P, 2, SORTED], I32),
            "result_row": m.sb("result_row", [P, TILES, TOP], I32),
            "sorted": nc.dram_tensor("sorted_rows", (EXPERTS * REGION, D), F32, kind="Internal").ap(),
            "result": nc.dram_tensor("result_rows", (SORTED * P, D), F32, kind="Internal").ap(),
        }
        setup(nc, dram, keep)
        load_mlp(nc, dram, keep)
        wide_attention(nc, dram, keep)
        routed_attention(nc, dram, keep)
        masked_attention(nc, dram, keep)
        select_experts(nc, dram, keep)
        run_experts(nc, dram, keep)
        combine(nc, dram, keep, out)


_INS = ["x", "ctx_1024", "mask_Bx1xSxS2_ik1"]
_INS += [f"L0_xattn_{n}" for n in ("Wq", "bq", "Wk", "bk", "Wv", "bv", "Wu", "bu")]
_INS += [f"L0_ffn_{n}" for n in ("Wq", "bq", "Wk", "bk", "Wv", "bv", "We", "be", "Wsw", "bsw", "gamma", "beta")]
_INS += [f"L1_xattn_{n}" for n in ("Wv", "bv", "Wk", "bk", "Wq", "bq", "Wo", "bo")]
_INS += [f"L1_ffn_{n}" for n in ("W_gate", "W_in", "b_in", "W_out", "b_out")]


def kernel(**inputs):
    import numpy as np
    from concourse import bacc
    from concourse.bass_utils import run_bass_kernel_spmd

    nc = bacc.Bacc("TRN2", target_bir_lowering=False, num_devices=1)
    arrays, dram = {}, {}
    for name in _INS:
        a = np.ascontiguousarray(inputs[name])
        arrays[f"in_{name}"] = a
        dram[name] = nc.dram_tensor(f"in_{name}", a.shape, mybir.dt.from_np(a.dtype), kind="ExternalInput").ap()
    out = nc.dram_tensor("out_x", inputs["x"].shape, F32, kind="ExternalOutput").ap()
    network(nc, dram, out)
    r = run_bass_kernel_spmd(nc, [arrays], core_ids=[0])
    return r.results[0]["out_x"]
```

```python
from contextlib import ExitStack

import concourse.bass as bass
from concourse import mybir

F32 = mybir.dt.float32
BF16 = mybir.dt.bfloat16
I32 = mybir.dt.int32
U32 = mybir.dt.uint32
ALU = mybir.AluOpType
ACT = mybir.ActivationFunctionType
AX = mybir.AxisListType

P = 128
BATCHES, SEQ, D = 64, 64, 128
TILES = BATCHES * SEQ // P
PER_TILE = P // SEQ
HEADS = 16
CHUNKS = HEADS // 2
PAIRS = CHUNKS // 2
HK = 64
WIDE = HEADS * HK
HD = D // HEADS
EXPERTS = 8
CAPACITY = int(1.2 * BATCHES * SEQ / EXPERTS)
MLP = 512
BLOCKS = MLP // P
EPS = 1e-5
TOP = 2
REGION = BATCHES * SEQ + P
SORTED = BATCHES * SEQ * TOP // P + EXPERTS
VCOL = 2 * HD + 1
ROW = D + 1
LEAST = -3.0e38
W_LOADS = 2 * EXPERTS + 2
BIAS_ROWS = EXPERTS * BLOCKS + EXPERTS
X_PARTS = 4
DMA = 16


class Tile:

    def __init__(self, group, at, count=TILES, size=2):
        self.group, self.at, self.count, self.size = group, at, count, size
        self.odd = at % 2
        self.index = group * size + at if at else group * size

    def back(self, lag):
        at = self.at - lag
        groups = at // self.size
        return Tile(self.group + groups if groups else self.group, at % self.size, self.count, self.size)

    @property
    def live(self):
        return not isinstance(self.group, int) or 0 <= self.index < self.count


def wait(eng, sem, value):
    if not isinstance(value, int) or value > 0:
        eng.wait_ge(sem, value)


def apart(eng):
    eng.nop(nofuse=True)


def over_tiles(eng, step, lag, count=TILES, size=2, before_loop=None):
    first = (lag + 2 * size - 1) // size
    for s in range(first * size):
        step(Tile(s // size, s % size, count, size))
    if before_loop:
        before_loop()
    with eng.Fori(first, count // size) as group:
        for at in range(size):
            step(Tile(group, at, count, size))
    for s in range(count, count + lag):
        step(Tile(s // size, s % size, count, size))


class Memory:

    def __init__(self, nc, ctx, tag):
        self.nc, self.ctx, self.tag = nc, ctx, tag
        self.semaphores = []
        ctx.callback(self.clear)

    def clear(self):
        self.nc.clear_and_free_semaphores(self.semaphores)
        self.nc.all_engine_barrier()

    def sb(self, name, shape, dt=F32):
        return self.ctx.enter_context(self.nc.sbuf_tensor(f"{self.tag}_{name}", shape, dt))

    def ps(self, name, shape, dt=F32):
        return self.ctx.enter_context(self.nc.psum_tensor(f"{self.tag}_{name}_ps", shape, dt))

    def sem(self, name):
        self.semaphores.append(self.nc.alloc_semaphore(name=f"{self.tag}_{name}"))
        return self.semaphores[-1]


def many(ap, n, axis=2):
    ap = ap.unsqueeze(axis)
    shape = list(ap.shape)
    shape[axis] = n
    return ap.to_broadcast(shape)


def wide_attention(nc, dram, keep):
    ctx = ExitStack()
    with ctx:
        m = Memory(nc, ctx, "wide")
        x, ident, eps_pow = keep["x"], keep["ident"], keep["eps_pow"]
        wq = m.sb("wq", [P, CHUNKS, P])
        wk = m.sb("wk", [P, CHUNKS, P])
        wv = m.sb("wv", [P, WIDE])
        wu = m.sb("wu", [P, PAIRS, 2, D])
        bq = m.sb("bq", [P, CHUNKS])
        bk = m.sb("bk", [P, CHUNKS])
        bv = m.sb("bv", [P, HEADS])
        bv_wide = m.sb("bv_wide", [P, PAIRS * 2, P])
        bu = m.sb("bu", [P, D])
        ctx_in = m.sb("ctx_in", [P, 2, D])
        stats = m.sb("stats", [P, 2, 6])
        mean_var = m.sb("mean_var", [P, 2, 2])
        var_eps = m.sb("var_eps", [P, 2])
        rstd = m.sb("rstd", [P, 2])
        xn = m.sb("xn", [P, 2, D])
        xc_t = m.sb("xc_t", [P, 2, 2, P])
        q_block = m.sb("q_block", [P, 2, CHUNKS, PER_TILE, 2, SEQ])
        k_t = m.sb("k_t", [P, 2, CHUNKS, P])
        v_block = m.sb("v_block", [P, 2, PER_TILE, PAIRS, 2, 2, HK])
        top = m.sb("top", [P, 2, HEADS])
        expo = m.sb("expo", [P, 2, HEADS, SEQ])
        total = m.sb("total", [P, 2, HEADS])
        share = m.sb("share", [P, 2, HEADS])
        prob = m.sb("prob", [P, 2, HEADS, SEQ])
        prob_t = m.sb("prob_t", [P, 2, PER_TILE, PAIRS, P])
        out_t = m.sb("out_t", [P, 2, PAIRS, 2, PER_TILE, SEQ])

        proj_ps = [m.ps(f"proj{i}", [P, 4, P]) for i in range(2)]
        score_ps = m.ps("score", [P, PER_TILE, CHUNKS * SEQ])
        turn_ps = m.ps("turn", [P, PER_TILE, 512])
        norm_ps = m.ps("norm", [P, 512])
        up_ps = m.ps("up", [P, 512])

        x_rest = m.sem("x_rest")
        loaded = m.sem("loaded")
        bias_loaded = m.sem("bias_loaded")
        blocks_zero = m.sem("blocks_zero")
        bv_spread = m.sem("bv_spread")
        bu_summed = m.sem("bu_summed")
        bu_ready = m.sem("bu_ready")
        ctx_loaded = [m.sem(f"ctx_loaded{i}") for i in range(2)]
        stats_done = m.sem("stats_done")
        mean_done = m.sem("mean_done")
        var_done = m.sem("var_done")
        rstd_done = m.sem("rstd_done")
        xn_done = m.sem("xn_done")
        x_biased = m.sem("x_biased")
        turned_in = m.sem("turned_in")
        xc_done = m.sem("xc_done")
        q_filled = m.sem("q_filled")
        k_filled = m.sem("k_filled")
        v_filled = m.sem("v_filled")
        q_done = m.sem("q_done")
        k_done = m.sem("k_done")
        v_done = m.sem("v_done")
        scored = m.sem("scored")
        top_done = m.sem("top_done")
        shifted = m.sem("shifted")
        exp_done = m.sem("exp_done")
        total_done = m.sem("total_done")
        share_done = m.sem("share_done")
        prob_done = m.sem("prob_done")
        prob_turned = m.sem("prob_turned")
        prob_t_done = m.sem("prob_t_done")
        mixed = m.sem("mixed")
        out_t_done = m.sem("out_t_done")
        up_done = m.sem("up_done")
        x_done = m.sem("x_done")

        ctx_tiles = dram["ctx_1024"].rearrange("b s d -> (b s) d").rearrange("(t p) d -> t p d", p=P)

        block = ctx.enter_context(nc.Block())
        BIAS_LOADS = 7

        @block.sync
        def _(sp):
            sp.dma_start(ctx_in[:, 0, :], ctx_tiles[0]).then_inc(ctx_loaded[0], DMA)
            sp.dma_start(ctx_in[:, 1, :], ctx_tiles[1]).then_inc(ctx_loaded[1], DMA)
            wu_rows = dram["L0_xattn_Wu"].rearrange("(c p h d) n -> p h d c n", c=PAIRS, p=2, h=2)
            for half in range(2):
                rows = slice(half * HK, half * HK + HK)
                sp.dma_start(bv[rows, :], dram["L0_xattn_bv"].rearrange("(h d) -> d h", d=HK),
                             allow_slow_non_contiguous=True).then_inc(bias_loaded, DMA)
                for h in range(2):
                    sp.dma_start(wu[rows, :, h, :], wu_rows[half, h]).then_inc(bias_loaded, DMA)
            sp.dma_start(bu[:, :], dram["L0_xattn_bu"].partition_broadcast(P)).then_inc(bias_loaded, DMA)
            x_tiles = dram["x"].rearrange("b s d -> (b s) d").rearrange("(t p) d -> p t d", p=P)
            for n in range(1, X_PARTS):
                part = slice(n * TILES // X_PARTS, (n + 1) * TILES // X_PARTS)
                sp.dma_start(x[:, part, :], x_tiles[:, part, :]).then_inc(x_rest, DMA)

            def step(t):
                u = t.back(-2)
                if u.live:
                    wait(sp, turned_in, t.index + 1)
                    sp.dma_start(ctx_in[:, u.odd, :], ctx_tiles[u.index]).then_inc(ctx_loaded[u.odd], DMA)

            with sp.Fori(0, TILES // 2 - 1) as group:
                step(Tile(group, 0))
                step(Tile(group, 1))

        @block.tensor
        def _(pe):
            pe.wait_ge(bv_spread, 2)
            pe.wait_ge(bias_loaded, BIAS_LOADS * DMA)
            for n in range(PAIRS * 2):
                last = pe.matmul(up_ps[:, 0:D], bv_wide[:, n, :], wu[:, n // 2, n % 2, :],
                                 start=(n == 0), stop=(n == PAIRS * 2 - 1))
            last.then_inc(bu_summed, 1)
            pe.wait_ge(loaded, 5 * DMA)
            pe.wait_ge(blocks_zero, 2)
            pe.wait_ge(keep["ident_ready"], keep["ident_count"])

            def turn_in(t):
                pe.wait_ge(xn_done, t.index + 1)
                pe.wait_ge(ctx_loaded[t.odd], (t.group + 1) * DMA)
                wait(pe, xc_done, t.index)
                pe.transpose(norm_ps[:, 0:P], xn[:, t.odd, :], ident[:, :])
                pe.transpose(norm_ps[:, P:2 * P], ctx_in[:, t.odd, :], ident[:, :]).then_inc(turned_in, 1)

            def project_q(t, half):
                pe.wait_ge(xc_done, t.index + 1)
                if half == 0:
                    wait(pe, v_done, t.index * 2 - 1)
                else:
                    pe.wait_ge(q_done, t.index * 2 + 1)
                for c in range(4):
                    last = pe.matmul(proj_ps[0][:, c, :], wq[:, half * 4 + c, :], xc_t[:, t.odd, 0, :],
                                     start=True, stop=True)
                last.then_inc(q_filled, 1)

            def project_k(t, half):
                if half == 0:
                    wait(pe, v_done, t.index * 2)
                else:
                    pe.wait_ge(k_done, t.index * 2 + 1)
                for c in range(4):
                    last = pe.matmul(proj_ps[1][:, c, :], wk[:, half * 4 + c, :], xc_t[:, t.odd, 1, :],
                                     start=True, stop=True)
                last.then_inc(k_filled, 1)

            def project_v(t, half):
                pe.wait_ge(q_done if half == 0 else k_done, t.index * 2 + 2)
                last = pe.matmul(proj_ps[half][:, :, :], xc_t[:, t.odd, 1, :], wv[:, half * 512:half * 512 + 512],
                                 start=True, stop=True)
                last.then_inc(v_filled, 1)

            def scores(t):
                pe.wait_ge(q_done, 2 * t.index + 2)
                pe.wait_ge(k_done, 2 * t.index + 2)
                wait(pe, shifted, t.index)
                for b in range(PER_TILE):
                    for c in range(CHUNKS):
                        last = pe.matmul(score_ps[:, b, c * SEQ:(c + 1) * SEQ], q_block[:, t.odd, c, b, :, :],
                                         k_t[:, t.odd, c, b * SEQ:(b + 1) * SEQ], start=True, stop=True)
                last.then_inc(scored, 1)

            def turn_prob(t):
                pe.wait_ge(prob_done, t.index + 1)
                wait(pe, out_t_done, t.index)
                for b in range(PER_TILE):
                    for c in range(PAIRS):
                        h = b * CHUNKS + 2 * c
                        last = pe.transpose(turn_ps[:, b, c * P:(c + 1) * P], prob[:, t.odd, h:h + 2, :], ident[:, :])
                last.then_inc(prob_turned, 1)

            def mix(t):
                pe.wait_ge(prob_t_done, t.index + 1)
                pe.wait_ge(v_done, 2 * t.index + 2)
                for b in range(PER_TILE):
                    for c in range(PAIRS):
                        for h in range(2):
                            at = (2 * c + h) * SEQ
                            last = pe.matmul(turn_ps[:, b, at:at + SEQ], v_block[:, t.odd, b, c, h, :, :],
                                             prob_t[:, t.odd, b, c, h * SEQ:(h + 1) * SEQ], start=True, stop=True)
                last.then_inc(mixed, 1)

            def up(t):
                pe.wait_ge(out_t_done, t.index + 1)
                wait(pe, x_done, t.index)
                for n in range(PAIRS * 2):
                    last = pe.matmul(up_ps[:, 0:D], out_t[:, t.odd, n // 2, n % 2, :, :], wu[:, n // 2, n % 2, :],
                                     start=(n == 0), stop=(n == PAIRS * 2 - 1))
                last.then_inc(up_done, 1)

            pe.wait_ge(bu_ready, 1)

            def step(t):
                now, one, two, three = t, t.back(1), t.back(2), t.back(3)
                if two.live:
                    scores(two)
                if three.live:
                    turn_prob(three)
                if one.live:
                    project_q(one, 0)
                    project_k(one, 0)
                if three.live:
                    mix(three)
                if one.live:
                    project_q(one, 1)
                    project_k(one, 1)
                    project_v(one, 0)
                if three.live:
                    up(three)
                if one.live:
                    project_v(one, 1)
                if now.live:
                    turn_in(now)

            over_tiles(pe, step, 3)

        @block.scalar
        def _(act):
            act.dma_start(wq[:, :, :], dram["L0_xattn_Wq"].rearrange("d (c m) -> d c m", m=P)).then_inc(loaded, DMA)
            act.dma_start(wk[:, :, :], dram["L0_xattn_Wk"].rearrange("d (c m) -> d c m", m=P)).then_inc(loaded, DMA)
            act.dma_start(bq[:, :], dram["L0_xattn_bq"].rearrange("(c m) -> m c", m=P),
                          allow_slow_non_contiguous=True).then_inc(loaded, DMA)
            act.dma_start(bk[:, :], dram["L0_xattn_bk"].rearrange("(c m) -> m c", m=P),
                          allow_slow_non_contiguous=True).then_inc(loaded, DMA)
            act.dma_start(wv[:, :], dram["L0_xattn_Wv"]).then_inc(loaded, DMA)
            act.wait_ge(loaded, 5 * DMA)
            act.wait_ge(blocks_zero, 2)

            def bring_prob(t):
                act.wait_ge(prob_turned, t.index + 1)
                wait(act, mixed, t.index - 1)
                act.copy(prob_t[:, t.odd, :, :, :], turn_ps[:, :, :]).then_inc(prob_t_done, 1)

            def bring_k(t, half):
                act.wait_ge(k_filled, 2 * t.index + half + 1)
                if half == 0:
                    wait(act, scored, t.index - 1)
                for c in range(4):
                    n = half * 4 + c
                    last = act.activation(k_t[:, t.odd, n, :], proj_ps[1][:, c, :], ACT.Identity,
                                          bias=bk[:, n:n + 1])
                last.then_inc(k_done, 1)

            def bring_v(t, half):
                act.wait_ge(v_filled, 2 * t.index + half + 1)
                if half == 0:
                    wait(act, mixed, t.index - 1)
                for b in range(PER_TILE):
                    for p in range(2):
                        frm = proj_ps[half][b * SEQ:(b + 1) * SEQ, :, :].rearrange(
                            "k (c p) (h d) -> k c p h d", p=2, h=2)[:, :, p, :, :]
                        last = act.copy(
                            v_block[p * SEQ:(p + 1) * SEQ, t.odd, b, 2 * half:2 * half + 2, :, p, :], frm)
                last.then_inc(v_done, 1)

            def exponent(t):
                act.wait_ge(shifted, t.index + 1)
                act.activation(expo[:, t.odd, :, :], expo[:, t.odd, :, :], ACT.Exp, scale=HK ** -0.5).then_inc(exp_done, 1)

            def bring_out(t):
                act.wait_ge(mixed, t.index + 1)
                wait(act, up_done, t.index - 1)
                for b in range(PER_TILE):
                    last = act.copy(out_t[:, t.odd, :, :, b, :],
                                    turn_ps[:, b, :].rearrange("p (c h q) -> p c h q", c=PAIRS, h=2))
                last.then_inc(out_t_done, 1)

            def bring_in(t):
                act.wait_ge(turned_in, t.index + 1)
                wait(act, v_filled, 2 * t.index - 2)
                act.copy(xc_t[:, t.odd, :, :], norm_ps[:, 0:2 * P]).then_inc(xc_done, 1)

            def step(t):
                now, one, two, three = t, t.back(1), t.back(2), t.back(3)
                if three.live:
                    bring_prob(three)
                if one.live:
                    bring_k(one, 0)
                if two.live:
                    exponent(two)
                if three.live:
                    bring_out(three)
                if one.live:
                    bring_k(one, 1)
                    bring_v(one, 0)
                    bring_v(one, 1)
                if now.live:
                    bring_in(now)

            over_tiles(act, step, 3)

        @block.vector
        def _(dve):
            dve.memset(q_block[:, :, :, :, :, :], 0.0).then_inc(blocks_zero, 1)
            dve.wait_ge(bias_loaded, BIAS_LOADS * DMA)
            for half in range(2):
                rows = slice(half * HK, half * HK + HK)
                of_half = bv[rows, :].rearrange("d (c p h) -> d c p h", p=2, h=2)[:, :, half, :]
                dve.tensor_copy(bv_wide[rows, :, :].rearrange("d (c h) m -> d c h m", h=2),
                                many(of_half, P, 3)).then_inc(bv_spread, 1)
            dve.wait_ge(bu_summed, 1)
            dve.tensor_tensor(bu[:, :], up_ps[:, 0:D], bu[:, :], ALU.add).then_inc(bu_ready, 1)
            dve.wait_ge(loaded, 5 * DMA)

            def moments(t):
                dve.bn_stats(stats[:, t.odd, :], x[:, t.index, :]).then_inc(stats_done, 1)
                dve.wait_ge(stats_done, t.index + 1)
                wait(dve, xn_done, t.index - 1)
                apart(dve)
                dve.bn_aggr(mean_var[:, t.odd, :], stats[:, t.odd, :]).then_inc(mean_done, 1)
                dve.wait_ge(mean_done, t.index + 1)
                wait(dve, rstd_done, t.index - 1)
                dve.tensor_scalar(var_eps[:, t.odd:t.odd + 1], mean_var[:, t.odd, 1:2], EPS, None,
                                  ALU.add).then_inc(var_done, 1)

            def normalize(t):
                dve.wait_ge(rstd_done, t.index + 1)
                wait(dve, turned_in, t.index - 1)
                dve.tensor_scalar(xn[:, t.odd, :], x[:, t.index, :], mean_var[:, t.odd, 0:1],
                                  rstd[:, t.odd:t.odd + 1], ALU.subtract, ALU.mult).then_inc(xn_done, 1)

            def bring_q(t, half):
                dve.wait_ge(q_filled, 2 * t.index + half + 1)
                if half == 0:
                    wait(dve, scored, t.index - 1)
                for p in range(2):
                    rows = slice(p * HK, (p + 1) * HK)
                    cs = slice(half * 4, half * 4 + 4)
                    last = dve.tensor_tensor(
                        q_block[rows, t.odd, cs, :, p, :],
                        proj_ps[0][rows, :, :].rearrange("p c (b q) -> p c b q", b=PER_TILE),
                        many(bq[rows, cs], P).rearrange("p c (b q) -> p c b q", b=PER_TILE), ALU.add)
                last.then_inc(q_done, 1)

            def shift(t):
                dve.wait_ge(scored, t.index + 1)
                s = score_ps[:, :, :].rearrange("p b (c k) -> p (b c) k", k=SEQ)
                dve.tensor_reduce(top[:, t.odd, :], s, AX.X, ALU.max).then_inc(top_done, 1)
                dve.wait_ge(top_done, t.index + 1)
                wait(dve, prob_done, t.index - 1)
                dve.tensor_tensor(expo[:, t.odd, :, :], s, many(top[:, t.odd, :], SEQ), ALU.subtract).then_inc(shifted, 1)

            def totals(t):
                dve.wait_ge(exp_done, t.index + 1)
                dve.tensor_reduce(total[:, t.odd, :], expo[:, t.odd, :, :], AX.X, ALU.add).then_inc(total_done, 1)
                dve.wait_ge(total_done, t.index + 1)
                dve.reciprocal(share[:, t.odd, :], total[:, t.odd, :]).then_inc(share_done, 1)

            def residual(t):
                dve.wait_ge(up_done, t.index + 1)
                dve.wait_ge(x_biased, t.index + 1)
                dve.tensor_tensor(x[:, t.index, :], up_ps[:, 0:D], x[:, t.index, :], ALU.add).then_inc(x_done, 1)

            def step(t):
                now, one, two, three = t, t.back(1), t.back(2), t.back(3)
                if two.live:
                    shift(two)
                if now.live:
                    moments(now)
                if one.live:
                    bring_q(one, 0)
                if two.live:
                    totals(two)
                if now.live:
                    normalize(now)
                if one.live:
                    bring_q(one, 1)
                if three.live:
                    residual(three)

            dve.wait_ge(keep["x_loaded"], DMA)
            dve.wait_ge(blocks_zero, 2)
            over_tiles(dve, step, 3, before_loop=lambda: dve.wait_ge(x_rest, (X_PARTS - 1) * DMA))

        @block.gpsimd
        def _(pool):
            pool.wait_ge(keep["ident_ready"], keep["ident_count"])
            pool.memset(v_block[:, :, :, :, :, :, :], 0.0).then_inc(blocks_zero, 1)
            pool.wait_ge(bu_ready, 1)

            def step(t):
                now, two = t, t.back(2)
                if now.live:
                    pool.wait_ge(var_done, now.index + 1)
                    pool.tensor_tensor(rstd[:, now.odd:now.odd + 1], var_eps[:, now.odd:now.odd + 1],
                                       eps_pow[:, :], ALU.pow).then_inc(rstd_done, 1)
                if two.live:
                    pool.wait_ge(share_done, two.index + 1)
                    wait(pool, prob_turned, two.index - 1)
                    pool.tensor_tensor(prob[:, two.odd, :, :], expo[:, two.odd, :, :],
                                       many(share[:, two.odd, :], SEQ), ALU.mult).then_inc(prob_done, 1)
                if now.live:
                    pool.wait_ge(xn_done, now.index + 1)
                    pool.tensor_tensor(x[:, now.index, :], x[:, now.index, :], bu[:, :], ALU.add).then_inc(x_biased, 1)

            over_tiles(pool, step, 2)


def start_later_loads(sp, dram, keep):
    mask_rows = dram["mask_Bx1xSxS2_ik1"].rearrange("b o q k -> q (b o) k")
    for h in range(2):
        sp.dma_start(keep["mask"][h * SEQ:(h + 1) * SEQ, :, :].rearrange("q t (b k) -> q (t b) k", b=PER_TILE),
                     mask_rows).then_inc(keep["mask_loaded"], DMA)
    for n in range(EXPERTS):
        sp.dma_start(keep["w_in"][:, n, :], dram["L1_ffn_W_in"][n]).then_inc(keep["w_loaded"], DMA)
        sp.dma_start(keep["w_out"][:, n, :, :],
                     dram["L1_ffn_W_out"][n].rearrange("(c m) d -> m c d", m=P)).then_inc(keep["w_loaded"], DMA)
    sp.dma_start(keep["b_rows"][0:EXPERTS * BLOCKS, :],
                 dram["L1_ffn_b_in"].rearrange("x (c m) -> (x c) m", m=P)).then_inc(keep["w_loaded"], DMA)
    sp.dma_start(keep["b_rows"][EXPERTS * BLOCKS:, :], dram["L1_ffn_b_out"]).then_inc(keep["w_loaded"], DMA)


def routed_attention(nc, dram, keep):
    ctx = ExitStack()
    with ctx:
        m = Memory(nc, ctx, "rout")
        x, ident, eps_pow = keep["x"], keep["ident"], keep["eps_pow"]
        w_in = m.sb("w_in", [P, 3 + EXPERTS, D])
        w_t = m.sb("w_t", [P, 3 + EXPERTS, D])
        wsw_in = m.sb("wsw_in", [EXPERTS, D])
        wsw_t = m.sb("wsw_t", [P, EXPERTS])
        bq = m.sb("bq", [P, 1])
        bk = m.sb("bk", [P, 1])
        bv = m.sb("bv", [P, D])
        gamma = m.sb("gamma", [P, D])
        beta = m.sb("beta", [P, D])
        bsw = m.sb("bsw", [P, EXPERTS])
        be = m.sb("be", [P, EXPERTS * D])
        be_parts = m.sb("be_parts", [96, EXPERTS * D], BF16)
        be_ones = m.sb("be_ones", [96, P], BF16)
        head_of = m.sb("head_of", [P, HEADS])
        causal = m.sb("causal", [P, SEQ])
        upto = m.sb("upto", [P, P], BF16)
        ones = m.sb("ones", [P, P], BF16)
        number = m.sb("number", [P, EXPERTS])
        seen = m.sb("seen", [P, EXPERTS], BF16)

        stats = m.sb("stats", [P, 2, 6])
        mean_var = m.sb("mean_var", [P, 2, 2])
        var_eps = m.sb("var_eps", [P, 2])
        rstd = m.sb("rstd", [P, 2])
        e_now = m.sb("e_now", [P, 2, D])
        e_all = m.sb("e_all", [P, TILES, D])
        e_t = m.sb("e_t", [P, 2, P])
        qk = m.sb("qk", [P, 2, 2, P])
        q_block = m.sb("q_block", [P, 2, PER_TILE, HEADS, SEQ])
        v_block = m.sb("v_block", [P, 2, PER_TILE, PAIRS, 2, VCOL])
        score = m.sb("score", [P, 2, HEADS, SEQ])
        top = m.sb("top", [P, 2, HEADS])
        expo = m.sb("expo", [P, 2, HEADS, SEQ])
        prob_t = m.sb("prob_t", [P, 2, PER_TILE, PAIRS, P])
        share = m.sb("share", [P, 2, PER_TILE, CHUNKS])
        hid_raw = m.sb("hid_raw", [P, 2, D])
        hid = m.sb("hid", [P, 2, D])
        hid_t = m.sb("hid_t", [P, 2, P])
        logit = m.sb("logit", [P, EXPERTS])
        best = m.sb("best", [P, 8])
        place = m.sb("place", [P, 8], U32)
        less_best = m.sb("less_best", [P, 1])
        e_logit = m.sb("e_logit", [P, EXPERTS])
        e_sum = m.sb("e_sum", [P, 1])
        route_prob = m.sb("route_prob", [P, 1])
        chosen = m.sb("chosen", [P, EXPERTS])
        chosen_b = m.sb("chosen_b", [P, EXPERTS], BF16)
        order = m.sb("order", [P, EXPERTS])
        position = m.sb("position", [P, 1])
        kept = m.sb("kept", [P, 1])
        gate = m.sb("gate", [P, 1])
        pass_on = m.sb("pass_on", [P, 1])
        weight = m.sb("weight", [P, EXPERTS])
        parts = m.sb("parts", [P, EXPERTS, D])
        y = m.sb("y", [P, D])
        z = m.sb("z", [P, D])
        z_pre = m.sb("z_pre", [P, D])
        z_stats = m.sb("z_stats", [P, 6])
        z_mean_var = m.sb("z_mean_var", [P, 2])
        z_var_eps = m.sb("z_var_eps", [P, 1])
        z_rstd = m.sb("z_rstd", [P, 1])
        zn = m.sb("zn", [P, D])
        zg = m.sb("zg", [P, D])
        xb = m.sb("xb", [P, D])

        small_ps = m.ps("small", [P, 512])
        qkv_ps = m.ps("qkv", [P, 4, P])
        score_ps = m.ps("score", [P, PER_TILE, CHUNKS * SEQ])
        turn_ps = m.ps("turn", [P, PER_TILE, 512])
        exp_ps = m.ps("exp", [P, EXPERTS, D])

        loaded = m.sem("loaded")
        masks_filled = m.sem("masks_filled")
        masks_done = m.sem("masks_done")
        w_turned = m.sem("w_turned")
        w_done = m.sem("w_done")
        stats_done, mean_done, var_done = m.sem("stats_done"), m.sem("mean_done"), m.sem("var_done")
        rstd_done, e_done, e_kept = m.sem("rstd_done"), m.sem("e_done"), m.sem("e_kept")
        e_turned, e_t_done = m.sem("e_turned"), m.sem("e_t_done")
        qk_filled, v_filled = m.sem("qk_filled"), m.sem("v_filled")
        qk_done, v_done = m.sem("qk_done"), m.sem("v_done")
        q_block_done, scored, masked = m.sem("q_block_done"), m.sem("scored"), m.sem("masked")
        top_done, shifted, exp_done = m.sem("top_done"), m.sem("shifted"), m.sem("exp_done")
        prob_turned, prob_t_done, mixed = m.sem("prob_turned"), m.sem("prob_t_done"), m.sem("mixed")
        share_done, hid_raw_done, hid_done = m.sem("share_done"), m.sem("hid_raw_done"), m.sem("hid_done")
        hid_turned, hid_t_done, routed = m.sem("hid_turned"), m.sem("hid_t_done"), m.sem("routed")
        experts_done, parts_done = m.sem("experts_done"), m.sem("parts_done")
        logit_done, best_done, place_done = m.sem("logit_done"), m.sem("best_done"), m.sem("place_done")
        less_done, sum_done, chosen_done = m.sem("less_done"), m.sem("sum_done"), m.sem("chosen_done")
        counted, order_done, position_done = m.sem("counted"), m.sem("order_done"), m.sem("position_done")
        kept_done, route_done, gate_done = m.sem("kept_done"), m.sem("route_done"), m.sem("gate_done")
        pick_done, pass_done = m.sem("pick_done"), m.sem("pass_done")
        weight_done, seen_done = m.sem("weight_done"), m.sem("seen_done")
        y_done, z_pre_done, z_done = m.sem("y_done"), m.sem("z_pre_done"), m.sem("z_done")
        z_stats_done, z_mean_done, z_var_done = m.sem("z_stats_done"), m.sem("z_mean_done"), m.sem("z_var_done")
        z_rstd_done, zn_done, zg_done = m.sem("z_rstd_done"), m.sem("zn_done"), m.sem("zg_done")
        xb_done, x_done = m.sem("xb_done"), m.sem("x_done")
        be_step = m.sem("be_step")

        block = ctx.enter_context(nc.Block())
        LOADS = 12

        @block.sync
        def _(sp):
            for n, name in enumerate(("Wq", "Wk", "Wv")):
                sp.dma_start(w_in[:, n, :], dram[f"L0_ffn_{name}"].rearrange("h e d -> (h e) d")).then_inc(loaded, DMA)
            sp.dma_start(w_in[:, 3:, :], dram["L0_ffn_We"].rearrange("x e d -> e x d")).then_inc(loaded, DMA)
            sp.dma_start(wsw_in[:, :], dram["L0_ffn_Wsw"]).then_inc(loaded, DMA)
            for to, name in ((bq, "bq"), (bk, "bk")):
                sp.dma_start(to[:, :], dram[f"L0_ffn_{name}"].rearrange("h (e o) -> (h e) o", o=1)).then_inc(loaded, DMA)
            sp.dma_start(bv[:, :], dram["L0_ffn_bv"].rearrange("h e -> (h e)").partition_broadcast(P)).then_inc(loaded, DMA)
            for to, name in ((gamma, "gamma"), (beta, "beta"), (bsw, "bsw")):
                sp.dma_start(to[:, :], dram[f"L0_ffn_{name}"].partition_broadcast(P)).then_inc(loaded, DMA)
            flat_be = dram["L0_ffn_be"].rearrange("(o x) d -> o (x d)", o=1)
            sp.dma_start(be[0:1, :], flat_be).then_inc(loaded, DMA)
            start_later_loads(sp, dram, keep)

        @block.tensor
        def _(pe):
            pe.wait_ge(loaded, LOADS * DMA)
            for n in range(3 + EXPERTS):
                if n >= 4 and n % 4 == 0:
                    pe.wait_ge(w_done, n // 4)
                last = pe.transpose(small_ps[:, n % 4 * P:n % 4 * P + P], w_in[:, n, :], ident[:, :])
                if n % 4 == 3 or n == 2 + EXPERTS:
                    last.then_inc(w_turned, 1)
            pe.wait_ge(w_done, 3)
            pe.transpose(small_ps[:, 0:EXPERTS], wsw_in[:, :], ident[0:EXPERTS, 0:EXPERTS]).then_inc(w_turned, 1)
            pe.wait_ge(w_done, 4)
            pe.wait_ge(masks_done, 6)
            pe.wait_ge(be_step, 11)

            def scores(t):
                pe.wait_ge(q_block_done, 2 * t.index + 2)
                wait(pe, masked, t.index)
                for b in range(PER_TILE):
                    for c in range(CHUNKS):
                        for h in range(2):
                            last = pe.matmul(score_ps[h * SEQ:(h + 1) * SEQ, b, c * SEQ:(c + 1) * SEQ],
                                             q_block[:, t.odd, b, 2 * c + h, :],
                                             qk[:, t.odd, 1, b * SEQ:(b + 1) * SEQ], start=True, stop=True)
                last.then_inc(scored, 1)

            def turn_prob(t):
                pe.wait_ge(exp_done, t.index + 1)
                wait(pe, hid_raw_done, t.index)
                for b in range(PER_TILE):
                    for c in range(PAIRS):
                        h = b * CHUNKS + 2 * c
                        last = pe.transpose(turn_ps[:, b, c * P:(c + 1) * P], expo[:, t.odd, h:h + 2, :], ident[:, :])
                last.then_inc(prob_turned, 1)

            def mix(t):
                pe.wait_ge(prob_t_done, t.index + 1)
                pe.wait_ge(v_done, t.index + 1)
                for b in range(PER_TILE):
                    for c in range(PAIRS):
                        at = (b * PAIRS + c) * 2 * VCOL
                        last = pe.matmul(turn_ps[:, 0, at:at + 2 * VCOL], prob_t[:, t.odd, b, c, :],
                                         v_block[:, t.odd, b, c, :, :], start=True, stop=True)
                last.then_inc(mixed, 1)

            def turn_hidden(t):
                pe.wait_ge(hid_done, t.index + 1)
                wait(pe, order_done, t.index)
                at = t.index + 4
                pe.wait_ge(e_t_done, min(at, TILES) if isinstance(at, int) else at)
                pe.transpose(small_ps[:, P:2 * P], hid[:, t.odd, :], ident[:, :]).then_inc(hid_turned, 1)

            def experts(t, half):
                part = slice(half * 4, half * 4 + 4)
                if half == 0:
                    pe.wait_ge(hid_t_done, t.index + 1)
                    at = t.index + 5
                    pe.wait_ge(e_t_done, min(at, TILES) if isinstance(at, int) else at)
                    pe.matmul(small_ps[:, 256:256 + EXPERTS], hid_t[:, t.odd, :], wsw_t[:, :], start=True,
                              stop=True).then_inc(routed, 1)
                    wait(pe, parts_done, t.index)
                pe.matmul(exp_ps[:, part, :], hid_t[:, t.odd, :], w_t[:, 3 + half * 4:7 + half * 4, :], start=True,
                          stop=False)
                pe.matmul(exp_ps[:, part, :], be_ones[:, :], be_parts[:, half * 512:half * 512 + 512],
                          start=False, stop=True).then_inc(experts_done, 1)

            def count(t):
                pe.wait_ge(chosen_done, t.index + 1)
                wait(pe, seen_done, t.index)
                pe.matmul(small_ps[:, 264:264 + EXPERTS], upto[:, :], chosen_b[:, :], start=True, stop=False)
                pe.matmul(small_ps[:, 264:264 + EXPERTS], ones[:, :], seen[:, :], start=False, stop=True).then_inc(counted, 1)

            def turn_in(t):
                pe.wait_ge(e_done, t.index + 1)
                wait(pe, e_t_done, t.index)
                wait(pe, order_done, t.index - 4)
                pe.transpose(small_ps[:, 0:P], e_now[:, t.odd, :], ident[:, :]).then_inc(e_turned, 1)

            def project_qk(t):
                pe.wait_ge(e_t_done, t.index + 1)
                wait(pe, v_done, t.index)
                pe.matmul(qkv_ps[:, 0, :], w_t[:, 0, :], e_t[:, t.odd, :], start=True, stop=True)
                pe.matmul(qkv_ps[:, 1, :], w_t[:, 1, :], e_t[:, t.odd, :], start=True, stop=True).then_inc(qk_filled, 1)

            def project_v(t):
                pe.wait_ge(qk_done, t.index + 1)
                pe.matmul(qkv_ps[:, 2, :], e_t[:, t.odd, :], w_t[:, 2, :], start=True, stop=True).then_inc(v_filled, 1)

            def step(t):
                now, one, two, three, four = t, t.back(1), t.back(2), t.back(3), t.back(4)
                if one.live:
                    project_qk(one)
                if two.live:
                    scores(two)
                if now.live:
                    turn_in(now)
                if four.live:
                    turn_hidden(four)
                if three.live:
                    turn_prob(three)
                if one.live:
                    project_v(one)
                if four.live:
                    experts(four, 0)
                if three.live:
                    mix(three)
                if four.live:
                    experts(four, 1)
                    count(four)

            over_tiles(pe, step, 4)

        @block.scalar
        def _(act):
            for n in range(3):
                lo, hi = 4 * n, min(4 * n + 4, 3 + EXPERTS)
                act.wait_ge(w_turned, n + 1)
                act.copy(w_t[:, lo:hi, :], small_ps[:, 0:(hi - lo) * P]).then_inc(w_done, 1)
            act.wait_ge(w_turned, 4)
            act.copy(wsw_t[:, :], small_ps[:, 0:EXPERTS]).then_inc(w_done, 1)
            act.wait_ge(loaded, LOADS * DMA)
            act.wait_ge(be_step, 11)

            def bring_hidden(t):
                act.wait_ge(hid_turned, t.index + 1)
                wait(act, experts_done, 2 * t.index - 2)
                act.copy(hid_t[:, t.odd, :], small_ps[:, P:2 * P]).then_inc(hid_t_done, 1)

            def bring_prob(t):
                act.wait_ge(prob_turned, t.index + 1)
                wait(act, mixed, t.index - 1)
                act.copy(prob_t[:, t.odd, :, :, :], turn_ps[:, :, :]).then_inc(prob_t_done, 1)

            def route_exp(t):
                act.wait_ge(less_done, t.index + 1)
                wait(act, route_done, t.index)
                act.activation(e_logit[:, :], logit[:, :], ACT.Exp, bias=less_best[:, :],
                               accum_out=e_sum[:, :]).then_inc(sum_done, 1)

            def exponent(t):
                act.wait_ge(shifted, t.index + 1)
                act.activation(expo[:, t.odd, :, :], expo[:, t.odd, :, :], ACT.Exp, scale=D ** -0.5).then_inc(exp_done, 1)

            def weigh(t):
                act.wait_ge(weight_done, t.index + 1)
                act.wait_ge(experts_done, 2 * t.index + 2)
                wait(act, y_done, t.index)
                for n in range(EXPERTS):
                    last = act.activation(parts[:, n, :], exp_ps[:, n, :], ACT.Copy, scale=weight[:, n:n + 1])
                last.then_inc(parts_done, 1)

            def bring_in(t):
                act.wait_ge(e_turned, t.index + 1)
                wait(act, v_filled, t.index - 1)
                act.copy(e_t[:, t.odd, :], small_ps[:, 0:P]).then_inc(e_t_done, 1)
                act.copy(e_all[:, t.index, :], e_now[:, t.odd, :]).then_inc(e_kept, 1)

            def bring_qk(t):
                act.wait_ge(qk_filled, t.index + 1)
                wait(act, scored, t.index - 1)
                act.activation(qk[:, t.odd, 0, :], qkv_ps[:, 0, :], ACT.Identity, bias=bq[:, :])
                act.activation(qk[:, t.odd, 1, :], qkv_ps[:, 1, :], ACT.Identity, bias=bk[:, :]).then_inc(qk_done, 1)

            def bring_v(t):
                act.wait_ge(v_filled, t.index + 1)
                wait(act, mixed, t.index - 1)
                for b in range(PER_TILE):
                    for p in range(2):
                        frm = qkv_ps[b * SEQ:(b + 1) * SEQ, 2, :].rearrange("k (c p m) -> k c p m", p=2, m=2 * HD)[:, :, p, :]
                        last = act.copy(v_block[p * SEQ:(p + 1) * SEQ, t.odd, b, :, p, 0:2 * HD], frm)
                last.then_inc(v_done, 1)

            def step(t):
                now, one, three, four, five = t, t.back(1), t.back(3), t.back(4), t.back(5)
                if one.live:
                    bring_qk(one)
                if three.live:
                    exponent(three)
                if five.live:
                    weigh(five)
                if four.live:
                    bring_hidden(four)
                if now.live:
                    bring_in(now)
                if three.live:
                    bring_prob(three)
                if four.live:
                    route_exp(four)
                if one.live:
                    bring_v(one)

            over_tiles(act, step, 5)

        @block.vector
        def _(dve):
            dve.wait_ge(loaded, LOADS * DMA)
            dve.memset(be_parts[:, :], 0.0).then_inc(be_step, 1)
            dve.memset(be_ones[:, :], 1.0).then_inc(be_step, 1)
            dve.memset(v_block[:, :, :, :, :, :], 0.0).then_inc(be_step, 1)
            dve.memset(seen[:, :], 0.0).then_inc(be_step, 1)
            dve.wait_ge(be_step, 4)
            for p in range(2):
                dve.memset(v_block[p * SEQ:(p + 1) * SEQ, :, :, :, p, 2 * HD:VCOL], 1.0).then_inc(be_step, 1)
            for n in range(3):
                row = slice(32 * n, 32 * n + 1)
                dve.tensor_copy(be_parts[row, :], be[row, :]).then_inc(be_step, 1)
                dve.wait_ge(be_step, 7 + 2 * n)
                if n < 2:
                    nxt = slice(32 * n + 32, 32 * n + 33)
                    dve.tensor_tensor(be[nxt, :], be[row, :], be_parts[row, :], ALU.subtract).then_inc(be_step, 1)
                    dve.wait_ge(be_step, 8 + 2 * n)

            def moments(t):
                dve.bn_stats(stats[:, t.odd, :], x[:, t.index, :]).then_inc(stats_done, 1)
                dve.wait_ge(stats_done, t.index + 1)
                wait(dve, e_done, t.index - 1)
                apart(dve)
                dve.bn_aggr(mean_var[:, t.odd, :], stats[:, t.odd, :]).then_inc(mean_done, 1)
                dve.wait_ge(mean_done, t.index + 1)
                wait(dve, rstd_done, t.index - 1)
                dve.tensor_scalar(var_eps[:, t.odd:t.odd + 1], mean_var[:, t.odd, 1:2], EPS, None,
                                  ALU.add).then_inc(var_done, 1)

            def normalize(t):
                dve.wait_ge(rstd_done, t.index + 1)
                wait(dve, e_turned, t.index - 1)
                wait(dve, e_kept, t.index - 1)
                dve.tensor_scalar(e_now[:, t.odd, :], x[:, t.index, :], mean_var[:, t.odd, 0:1],
                                  rstd[:, t.odd:t.odd + 1], ALU.subtract, ALU.mult).then_inc(e_done, 1)

            def mask(t):
                dve.wait_ge(scored, t.index + 1)
                wait(dve, shifted, t.index - 1)
                s = score_ps[:, :, :].rearrange("p b (c k) -> p (b c) k", k=SEQ)
                dve.tensor_tensor(score[:, t.odd, :, :], s, many(causal[:, :], HEADS, 1), ALU.mult).then_inc(masked, 1)
                dve.wait_ge(masked, t.index + 1)
                dve.tensor_reduce(top[:, t.odd, :], score[:, t.odd, :, :], AX.X, ALU.max).then_inc(top_done, 1)

            def route(t):
                dve.wait_ge(routed, t.index + 1)
                wait(dve, sum_done, t.index)
                dve.tensor_tensor(logit[:, :], small_ps[:, 256:256 + EXPERTS], bsw[:, :], ALU.add).then_inc(logit_done, 1)
                dve.wait_ge(logit_done, t.index + 1)
                apart(dve)
                dve.max(best[:, :], logit[:, :]).then_inc(best_done, 1)
                dve.wait_ge(best_done, t.index + 1)
                dve.tensor_scalar(less_best[:, :], best[:, 0:1], -1.0, None, ALU.mult).then_inc(less_done, 1)
                apart(dve)
                dve.max_index(place[:, :], best[:, :], logit[:, :]).then_inc(place_done, 1)
                dve.wait_ge(place_done, t.index + 1)
                wait(dve, weight_done, t.index)
                dve.tensor_tensor(chosen[:, :], number[:, :], place[:, 0:1].to_broadcast([P, EXPERTS]),
                                  ALU.is_equal).then_inc(pick_done, 1)
                dve.wait_ge(pick_done, t.index + 1)
                wait(dve, seen_done, t.index)
                dve.tensor_copy(chosen_b[:, :], chosen[:, :]).then_inc(chosen_done, 1)

            def admit(t):
                dve.wait_ge(counted, t.index + 1)
                dve.tensor_tensor(order[:, :], small_ps[:, 264:264 + EXPERTS], chosen[:, :], ALU.mult).then_inc(order_done, 1)
                dve.tensor_tensor(seen[:, :], seen[:, :], chosen_b[:, :], ALU.add).then_inc(seen_done, 1)
                dve.wait_ge(order_done, t.index + 1)
                dve.tensor_reduce(position[:, :], order[:, :], AX.X, ALU.add).then_inc(position_done, 1)
                dve.wait_ge(sum_done, t.index + 1)
                dve.reciprocal(route_prob[:, :], e_sum[:, :]).then_inc(route_done, 1)
                dve.wait_ge(position_done, t.index + 1)
                dve.tensor_scalar(kept[:, :], position[:, :], float(CAPACITY), None, ALU.is_le).then_inc(kept_done, 1)
                dve.wait_ge(kept_done, t.index + 1)
                dve.wait_ge(route_done, t.index + 1)
                dve.tensor_tensor(gate[:, :], kept[:, :], route_prob[:, :], ALU.mult).then_inc(gate_done, 1)
                dve.wait_ge(gate_done, t.index + 1)
                dve.tensor_tensor(pass_on[:, :], route_prob[:, :], gate[:, :], ALU.subtract).then_inc(pass_done, 1)
                wait(dve, parts_done, t.index)
                dve.tensor_scalar(weight[:, :], chosen[:, :], gate[:, :], None, ALU.mult).then_inc(weight_done, 1)

            def take_hidden(t):
                dve.wait_ge(mixed, t.index + 1)
                sums = turn_ps[:, 0, 0:PER_TILE * PAIRS * 2 * VCOL].rearrange("p (b n m) -> p b n m", b=PER_TILE, m=VCOL)
                dve.reciprocal(share[:, t.odd, :, :], sums[:, :, :, 2 * HD:VCOL].rearrange("p b n o -> p b (n o)")).then_inc(share_done, 1)
                dve.wait_ge(share_done, t.index + 1)
                wait(dve, hid_done, t.index - 1)
                for b in range(PER_TILE):
                    for h in range(2):
                        rows = slice(h * SEQ, (h + 1) * SEQ)
                        to = hid_raw[b * SEQ:(b + 1) * SEQ, t.odd, :].rearrange("q (n h d) -> q n h d", h=2, d=HD)[:, :, h, :]
                        last = dve.tensor_tensor(to, sums[rows, b, :, h * HD:(h + 1) * HD],
                                                 many(share[rows, t.odd, b, :], HD), ALU.mult)
                last.then_inc(hid_raw_done, 1)

            def finish(t):
                dve.wait_ge(parts_done, t.index + 1)
                dve.tensor_reduce(y[:, :], parts[:, :, :].rearrange("p x f -> p f x"), AX.X, ALU.add).then_inc(y_done, 1)
                dve.wait_ge(y_done, t.index + 1)
                dve.wait_ge(pass_done, t.index + 1)
                dve.scalar_tensor_tensor(z_pre[:, :], hid[:, t.odd, :], pass_on[:, 0:1], y[:, :], ALU.mult,
                                         ALU.add).then_inc(z_pre_done, 1)
                dve.wait_ge(z_pre_done, t.index + 1)
                dve.wait_ge(e_kept, t.index + 1)
                wait(dve, zn_done, t.index)
                dve.tensor_tensor(z[:, :], z_pre[:, :], e_all[:, t.index, :], ALU.add).then_inc(z_done, 1)
                dve.wait_ge(z_done, t.index + 1)
                dve.bn_stats(z_stats[:, :], z[:, :]).then_inc(z_stats_done, 1)
                dve.wait_ge(z_stats_done, t.index + 1)
                apart(dve)
                dve.bn_aggr(z_mean_var[:, :], z_stats[:, :]).then_inc(z_mean_done, 1)
                dve.wait_ge(z_mean_done, t.index + 1)
                dve.tensor_scalar(z_var_eps[:, :], z_mean_var[:, 1:2], EPS, None, ALU.add).then_inc(z_var_done, 1)

            def finish_scale(t):
                dve.wait_ge(z_rstd_done, t.index + 1)
                wait(dve, zg_done, t.index)
                dve.tensor_scalar(zn[:, :], z[:, :], z_mean_var[:, 0:1], z_rstd[:, 0:1], ALU.subtract,
                                  ALU.mult).then_inc(zn_done, 1)

            def step(t):
                now, two, four, five, six = t, t.back(2), t.back(4), t.back(5), t.back(6)
                if now.live:
                    moments(now)
                if five.live:
                    admit(five)
                if four.live:
                    take_hidden(four)
                if now.live:
                    normalize(now)
                if six.live:
                    finish_scale(six)
                if two.live:
                    mask(two)
                if four.live:
                    route(four)
                if five.live:
                    finish(five)

            over_tiles(dve, step, 6)

        @block.gpsimd
        def _(pool):
            pool.memset(head_of[:, :], 1.0).then_inc(masks_filled, 1)
            pool.memset(causal[:, :], 1.0).then_inc(masks_filled, 1)
            pool.memset(upto[:, :], 1.0).then_inc(masks_filled, 1)
            pool.memset(ones[:, :], 1.0).then_inc(masks_done, 1)
            pool.iota(number[:, :], pattern=[[1, EXPERTS]], base=0, channel_multiplier=0,
                      allow_small_or_imprecise_dtypes=True).then_inc(masks_done, 1)
            pool.wait_ge(masks_filled, 3)
            pool.affine_select(out=head_of[:, :], in_=head_of[:, :], compare_op=ALU.is_ge, fill=0.0, base=0,
                               pattern=[[-HD, HEADS]], channel_multiplier=1).then_inc(masks_filled, 1)
            pool.wait_ge(masks_filled, 4)
            pool.affine_select(out=head_of[:, :], in_=head_of[:, :], compare_op=ALU.is_ge, fill=0.0, base=HD - 1,
                               pattern=[[HD, HEADS]], channel_multiplier=-1).then_inc(masks_done, 1)
            for h in range(2):
                pool.wait_ge(masks_done, 3 + h)
                rows = causal[h * SEQ:(h + 1) * SEQ, :]
                pool.affine_select(out=rows, in_=rows, compare_op=ALU.is_ge, fill=0.0, base=0,
                                   pattern=[[-1, SEQ]], channel_multiplier=1).then_inc(masks_done, 1)
            pool.wait_ge(masks_done, 5)
            pool.affine_select(out=upto[:, :], in_=upto[:, :], compare_op=ALU.is_ge, fill=0.0, base=0,
                               pattern=[[1, P]], channel_multiplier=-1).then_inc(masks_done, 1)
            pool.wait_ge(masks_done, 6)
            pool.wait_ge(loaded, LOADS * DMA)

            def scale_root(t):
                pool.wait_ge(var_done, t.index + 1)
                pool.tensor_tensor(rstd[:, t.odd:t.odd + 1], var_eps[:, t.odd:t.odd + 1], eps_pow[:, :],
                                   ALU.pow).then_inc(rstd_done, 1)

            def shift(t):
                pool.wait_ge(top_done, t.index + 1)
                wait(pool, prob_turned, t.index - 1)
                pool.tensor_tensor(expo[:, t.odd, :, :], score[:, t.odd, :, :], many(top[:, t.odd, :], SEQ),
                                   ALU.subtract).then_inc(shifted, 1)

            def spread_q(t, b):
                pool.wait_ge(qk_done, t.index + 1)
                wait(pool, scored, t.index - 1)
                pool.tensor_tensor(q_block[:, t.odd, b, :, :], many(qk[:, t.odd, 0, b * SEQ:(b + 1) * SEQ], HEADS, 1),
                                   many(head_of[:, :], SEQ), ALU.mult).then_inc(q_block_done, 1)

            def bias_hidden(t):
                pool.wait_ge(hid_raw_done, t.index + 1)
                wait(pool, z_pre_done, t.index - 1)
                wait(pool, hid_turned, t.index - 1)
                pool.tensor_tensor(hid[:, t.odd, :], hid_raw[:, t.odd, :], bv[:, :], ALU.add).then_inc(hid_done, 1)

            def bias_x(t):
                wait(pool, x_done, t.index)
                pool.tensor_tensor(xb[:, :], x[:, t.index, :], beta[:, :], ALU.add).then_inc(xb_done, 1)

            def scale_z_root(t):
                pool.wait_ge(z_var_done, t.index + 1)
                pool.tensor_tensor(z_rstd[:, :], z_var_eps[:, :], eps_pow[:, :], ALU.pow).then_inc(z_rstd_done, 1)

            def finish(t):
                pool.wait_ge(zn_done, t.index + 1)
                pool.tensor_tensor(zg[:, :], zn[:, :], gamma[:, :], ALU.mult).then_inc(zg_done, 1)
                pool.wait_ge(zg_done, t.index + 1)
                pool.wait_ge(xb_done, t.index + 1)
                apart(pool)
                pool.tensor_tensor(x[:, t.index, :], xb[:, :], zg[:, :], ALU.add).then_inc(x_done, 1)

            def step(t):
                now, one, two, four, five, six = t, t.back(1), t.back(2), t.back(4), t.back(5), t.back(6)
                if now.live:
                    scale_root(now)
                if one.live:
                    spread_q(one, 0)
                if four.live:
                    bias_hidden(four)
                if six.live:
                    finish(six)
                if one.live:
                    spread_q(one, 1)
                if five.live:
                    bias_x(five)
                if two.live:
                    shift(two)
                if five.live:
                    scale_z_root(five)

            over_tiles(pool, step, 6)


def masked_attention(nc, dram, keep):
    ctx = ExitStack()
    with ctx:
        m = Memory(nc, ctx, "mask")
        x, ident, eps_pow = keep["x"], keep["ident"], keep["eps_pow"]
        w_in = m.sb("w_in", [P, 4, D])
        w_t = m.sb("w_t", [P, 4, D])
        bq = m.sb("bq", [P, 1])
        bk = m.sb("bk", [P, 1])
        bv = m.sb("bv", [P, D])
        bo = m.sb("bo", [P, D])
        head_of = m.sb("head_of", [P, HEADS])
        ctx_in = m.sb("ctx_in", [P, 2, D])
        valid = m.sb("valid", [P, 2, PER_TILE, SEQ])

        stats = m.sb("stats", [P, 2, 6])
        mean_var = m.sb("mean_var", [P, 2, 2])
        var_eps = m.sb("var_eps", [P, 2])
        rstd = m.sb("rstd", [P, 2])
        xn = m.sb("xn", [P, 2, D])
        xc_t = m.sb("xc_t", [P, 2, 2, P])
        qk = m.sb("qk", [P, 2, 2, P])
        q_block = m.sb("q_block", [P, 2, PER_TILE, HEADS, SEQ])
        v_block = m.sb("v_block", [P, 2, PER_TILE, PAIRS, 2, VCOL])
        score = m.sb("score", [P, 2, HEADS, SEQ])
        top = m.sb("top", [P, 2, HEADS])
        expo = m.sb("expo", [P, 2, HEADS, SEQ])
        prob_t = m.sb("prob_t", [P, 2, PER_TILE, PAIRS, P])
        share = m.sb("share", [P, 2, PER_TILE, CHUNKS])
        out_raw = m.sb("out_raw", [P, 2, D])
        out = m.sb("out", [P, 2, D])
        out_t = m.sb("out_t", [P, 2, P])

        turn_in_ps = m.ps("turn_in", [P, 4, P])
        qk_ps = m.ps("qk", [P, 4, P])
        score_ps = m.ps("score", [P, PER_TILE, CHUNKS * SEQ])
        turn_ps = m.ps("turn", [P, PER_TILE, 512])
        v_ps = m.ps("v", [P, 512])
        mix_ps = m.ps("mix", [P, 512])

        loaded, zeroed = m.sem("loaded"), m.sem("zeroed")
        masks_filled, masks_done = m.sem("masks_filled"), m.sem("masks_done")
        ctx_loaded = [m.sem(f"ctx_loaded{i}") for i in range(2)]
        w_turned, w_done, valid_done = m.sem("w_turned"), m.sem("w_done"), m.sem("valid_done")
        stats_done, mean_done, var_done = m.sem("stats_done"), m.sem("mean_done"), m.sem("var_done")
        rstd_done, xn_done, x_biased = m.sem("rstd_done"), m.sem("xn_done"), m.sem("x_biased")
        turned_in, xc_done = m.sem("turned_in"), m.sem("xc_done")
        qk_filled, v_filled = m.sem("qk_filled"), m.sem("v_filled")
        qk_done, v_done = m.sem("qk_done"), m.sem("v_done")
        scored, masked = m.sem("scored"), m.sem("masked")
        q_block_done = [m.sem(f"q_block_done{i}") for i in range(PER_TILE)]
        top_done, shifted, exp_done = m.sem("top_done"), m.sem("shifted"), m.sem("exp_done")
        prob_turned, prob_t_done, mixed = m.sem("prob_turned"), m.sem("prob_t_done"), m.sem("mixed")
        share_done, out_raw_done, out_done = m.sem("share_done"), m.sem("out_raw_done"), m.sem("out_done")
        out_turned, out_t_done, up_done, x_done = m.sem("out_turned"), m.sem("out_t_done"), m.sem("up_done"), m.sem("x_done")

        ctx_tiles = dram["ctx_1024"].rearrange("b s d -> (b s) d").rearrange("(t p) d -> t p d", p=P)
        block = ctx.enter_context(nc.Block())
        LOADS = 8

        @block.sync
        def _(sp):
            for n, name in enumerate(("Wq", "Wk", "Wv", "Wo")):
                sp.dma_start(w_in[:, n, :], dram[f"L1_xattn_{name}"]).then_inc(loaded, DMA)
            for to, name in ((bq, "bq"), (bk, "bk")):
                sp.dma_start(to[:, :], dram[f"L1_xattn_{name}"].rearrange("(e o) -> e o", o=1)).then_inc(loaded, DMA)
            for to, name in ((bv, "bv"), (bo, "bo")):
                sp.dma_start(to[:, :], dram[f"L1_xattn_{name}"].partition_broadcast(P)).then_inc(loaded, DMA)
            sp.dma_start(ctx_in[:, 0, :], ctx_tiles[0]).then_inc(ctx_loaded[0], DMA)
            sp.dma_start(ctx_in[:, 1, :], ctx_tiles[1]).then_inc(ctx_loaded[1], DMA)

            def step(t):
                u = t.back(-2)
                sp.wait_ge(turned_in, t.index + 1)
                sp.dma_start(ctx_in[:, u.odd, :], ctx_tiles[u.index]).then_inc(ctx_loaded[u.odd], DMA)

            with sp.Fori(0, TILES // 2 - 1) as group:
                step(Tile(group, 0))
                step(Tile(group, 1))

        @block.tensor
        def _(pe):
            pe.wait_ge(loaded, LOADS * DMA)
            for n in range(4):
                last = pe.transpose(turn_in_ps[:, n, :], w_in[:, n, :], ident[:, :])
            last.then_inc(w_turned, 1)
            pe.wait_ge(w_done, 1)
            pe.wait_ge(zeroed, 3)

            def scores(t):
                for b in range(PER_TILE):
                    pe.wait_ge(q_block_done[b], t.index + 1)
                wait(pe, masked, 2 * t.index)
                for b in range(PER_TILE):
                    for c in range(CHUNKS):
                        for h in range(2):
                            last = pe.matmul(score_ps[h * SEQ:(h + 1) * SEQ, b, c * SEQ:(c + 1) * SEQ],
                                             q_block[:, t.odd, b, 2 * c + h, :],
                                             qk[:, t.odd, 1, b * SEQ:(b + 1) * SEQ], start=True, stop=True)
                last.then_inc(scored, 1)

            def turn_prob(t):
                pe.wait_ge(exp_done, t.index + 1)
                wait(pe, prob_t_done, t.index)
                for b in range(PER_TILE):
                    for c in range(PAIRS):
                        h = b * CHUNKS + 2 * c
                        last = pe.transpose(turn_ps[:, b, c * P:(c + 1) * P], expo[:, t.odd, h:h + 2, :], ident[:, :])
                last.then_inc(prob_turned, 1)

            def mix(t):
                pe.wait_ge(prob_t_done, t.index + 1)
                pe.wait_ge(v_done, t.index + 1)
                wait(pe, out_raw_done, t.index)
                for b in range(PER_TILE):
                    for c in range(PAIRS):
                        at = (b * PAIRS + c) * 2 * VCOL
                        last = pe.matmul(mix_ps[:, at:at + 2 * VCOL], prob_t[:, t.odd, b, c, :],
                                         v_block[:, t.odd, b, c, :, :], start=True, stop=True)
                last.then_inc(mixed, 1)

            def turn_out(t):
                pe.wait_ge(out_done, t.index + 1)
                wait(pe, x_done, t.index)
                pe.transpose(turn_in_ps[:, 2, :], out[:, t.odd, :], ident[:, :]).then_inc(out_turned, 1)

            def up(t):
                pe.wait_ge(out_t_done, t.index + 1)
                at = t.index + 6
                pe.wait_ge(xc_done, min(at, TILES) if isinstance(at, int) else at)
                pe.matmul(turn_in_ps[:, 3, :], out_t[:, t.odd, :], w_t[:, 3, :], start=True, stop=True).then_inc(up_done, 1)

            def turn_in(t):
                pe.wait_ge(xn_done, t.index + 1)
                pe.wait_ge(ctx_loaded[t.odd], (t.group + 1) * DMA)
                wait(pe, xc_done, t.index)
                wait(pe, x_done, t.index - 5)
                pe.transpose(turn_in_ps[:, 0, :], xn[:, t.odd, :], ident[:, :])
                pe.transpose(turn_in_ps[:, 1, :], ctx_in[:, t.odd, :], ident[:, :]).then_inc(turned_in, 1)

            def project_qk(t):
                pe.wait_ge(xc_done, t.index + 1)
                wait(pe, qk_done, t.index)
                pe.matmul(qk_ps[:, 0, :], w_t[:, 0, :], xc_t[:, t.odd, 0, :], start=True, stop=True)
                pe.matmul(qk_ps[:, 1, :], w_t[:, 1, :], xc_t[:, t.odd, 1, :], start=True, stop=True).then_inc(qk_filled, 1)

            def project_v(t):
                wait(pe, v_done, t.index)
                pe.matmul(v_ps[:, 0:D], xc_t[:, t.odd, 1, :], w_t[:, 2, :], start=True, stop=True).then_inc(v_filled, 1)

            def step(t):
                now, one, two, three, four, five, six = t, t.back(1), t.back(2), t.back(3), t.back(4), t.back(5), t.back(6)
                if one.live:
                    project_qk(one)
                if six.live:
                    up(six)
                if two.live:
                    project_v(two)
                if four.live:
                    mix(four)
                if two.live:
                    scores(two)
                if now.live:
                    turn_in(now)
                if five.live:
                    turn_out(five)
                if three.live:
                    turn_prob(three)

            over_tiles(pe, step, 6)

        @block.scalar
        def _(act):
            act.wait_ge(w_turned, 1)
            act.copy(w_t[:, :, :], turn_in_ps[:, :, :]).then_inc(w_done, 1)
            act.wait_ge(loaded, LOADS * DMA)
            act.wait_ge(zeroed, 3)

            def bring_out(t):
                act.wait_ge(out_turned, t.index + 1)
                wait(act, up_done, t.index - 1)
                act.copy(out_t[:, t.odd, :], turn_in_ps[:, 2, :]).then_inc(out_t_done, 1)

            def bring_prob(t):
                act.wait_ge(prob_turned, t.index + 1)
                wait(act, mixed, t.index - 1)
                act.copy(prob_t[:, t.odd, :, :, :], turn_ps[:, :, :]).then_inc(prob_t_done, 1)

            def exponent(t):
                act.wait_ge(shifted, t.index + 1)
                act.activation(expo[:, t.odd, :, :], expo[:, t.odd, :, :], ACT.Exp, scale=D ** -0.5).then_inc(exp_done, 1)

            def bring_in(t):
                act.wait_ge(turned_in, t.index + 1)
                wait(act, v_filled, t.index - 1)
                act.copy(xc_t[:, t.odd, :, :], turn_in_ps[:, 0:2, :]).then_inc(xc_done, 1)

            def bring_qk(t):
                act.wait_ge(qk_filled, t.index + 1)
                wait(act, scored, t.index - 1)
                for b in range(PER_TILE):
                    wait(act, q_block_done[b], t.index - 1)
                act.activation(qk[:, t.odd, 0, :], qk_ps[:, 0, :], ACT.Identity, bias=bq[:, :])
                act.activation(qk[:, t.odd, 1, :], qk_ps[:, 1, :], ACT.Identity, bias=bk[:, :]).then_inc(qk_done, 1)

            def bring_v(t):
                act.wait_ge(v_filled, t.index + 1)
                wait(act, mixed, t.index - 1)
                for b in range(PER_TILE):
                    for p in range(2):
                        frm = v_ps[b * SEQ:(b + 1) * SEQ, 0:D].rearrange("k (c p m) -> k c p m", p=2, m=2 * HD)[:, :, p, :]
                        last = act.copy(v_block[p * SEQ:(p + 1) * SEQ, t.odd, b, :, p, 0:2 * HD], frm)
                last.then_inc(v_done, 1)

            def step(t):
                now, one, two, three, five = t, t.back(1), t.back(2), t.back(3), t.back(5)
                if one.live:
                    bring_qk(one)
                if two.live:
                    bring_v(two)
                if three.live:
                    exponent(three)
                if five.live:
                    bring_out(five)
                if now.live:
                    bring_in(now)
                if three.live:
                    bring_prob(three)

            over_tiles(act, step, 5)

        @block.vector
        def _(dve):
            dve.memset(v_block[:, :, :, :, :, :], 0.0).then_inc(zeroed, 1)
            dve.wait_ge(zeroed, 1)
            for p in range(2):
                dve.memset(v_block[p * SEQ:(p + 1) * SEQ, :, :, :, p, 2 * HD:VCOL], 1.0).then_inc(zeroed, 1)
            dve.wait_ge(loaded, LOADS * DMA)
            dve.wait_ge(masks_done, 1)
            dve.wait_ge(keep["mask_loaded"], 2 * DMA)

            def moments(t):
                dve.bn_stats(stats[:, t.odd, :], x[:, t.index, :]).then_inc(stats_done, 1)
                dve.wait_ge(stats_done, t.index + 1)
                wait(dve, xn_done, t.index - 1)
                apart(dve)
                dve.bn_aggr(mean_var[:, t.odd, :], stats[:, t.odd, :]).then_inc(mean_done, 1)
                dve.wait_ge(mean_done, t.index + 1)
                wait(dve, rstd_done, t.index - 1)
                dve.tensor_scalar(var_eps[:, t.odd:t.odd + 1], mean_var[:, t.odd, 1:2], EPS, None,
                                  ALU.add).then_inc(var_done, 1)

            def normalize(t):
                dve.wait_ge(rstd_done, t.index + 1)
                wait(dve, turned_in, t.index - 1)
                dve.tensor_scalar(xn[:, t.odd, :], x[:, t.index, :], mean_var[:, t.odd, 0:1],
                                  rstd[:, t.odd:t.odd + 1], ALU.subtract, ALU.mult).then_inc(xn_done, 1)

            def mask(t):
                dve.wait_ge(scored, t.index + 1)
                dve.wait_ge(valid_done, t.index + 1)
                wait(dve, shifted, t.index - 1)
                for b in range(PER_TILE):
                    dve.scalar_tensor_tensor(
                        score[:, t.odd, b * CHUNKS:(b + 1) * CHUNKS, :],
                        score_ps[:, b, :].rearrange("p (c k) -> p c k", k=SEQ), 1e-20,
                        many(valid[:, t.odd, b, :], CHUNKS, 1), ALU.subtract, ALU.mult).then_inc(masked, 1)
                dve.wait_ge(masked, 2 * t.index + 2)
                dve.tensor_reduce(top[:, t.odd, :], score[:, t.odd, :, :], AX.X, ALU.max).then_inc(top_done, 1)

            def take_out(t):
                dve.wait_ge(mixed, t.index + 1)
                sums = mix_ps[:, 0:PER_TILE * PAIRS * 2 * VCOL].rearrange("p (b n m) -> p b n m", b=PER_TILE, m=VCOL)
                dve.reciprocal(share[:, t.odd, :, :], sums[:, :, :, 2 * HD:VCOL].rearrange("p b n o -> p b (n o)")).then_inc(share_done, 1)
                dve.wait_ge(share_done, t.index + 1)
                wait(dve, out_done, t.index - 1)
                for b in range(PER_TILE):
                    for h in range(2):
                        rows = slice(h * SEQ, (h + 1) * SEQ)
                        to = out_raw[b * SEQ:(b + 1) * SEQ, t.odd, :].rearrange("q (n h d) -> q n h d", h=2, d=HD)[:, :, h, :]
                        last = dve.tensor_tensor(to, sums[rows, b, :, h * HD:(h + 1) * HD],
                                                 many(share[rows, t.odd, b, :], HD), ALU.mult)
                last.then_inc(out_raw_done, 1)

            def residual(t):
                dve.wait_ge(up_done, t.index + 1)
                dve.wait_ge(x_biased, t.index + 1)
                dve.tensor_tensor(x[:, t.index, :], turn_in_ps[:, 3, :], x[:, t.index, :], ALU.add).then_inc(x_done, 1)

            def spread_q(t):
                dve.wait_ge(qk_done, t.index + 1)
                wait(dve, scored, t.index - 1)
                dve.tensor_tensor(q_block[:, t.odd, 1, :, :], many(qk[:, t.odd, 0, SEQ:P], HEADS, 1),
                                  many(head_of[:, :], SEQ), ALU.mult).then_inc(q_block_done[1], 1)

            def find_valid(t):
                wait(dve, masked, 2 * t.index - 2)
                dve.tensor_scalar(valid[:, t.odd, :, :].rearrange("p b k -> p (b k)"),
                                  keep["mask"][:, t.index, :], 0, None, ALU.not_equal).then_inc(valid_done, 1)

            def step(t):
                now, one, two, four, six = t, t.back(1), t.back(2), t.back(4), t.back(6)
                if now.live:
                    moments(now)
                if one.live:
                    find_valid(one)
                    spread_q(one)
                if now.live:
                    normalize(now)
                if four.live:
                    take_out(four)
                if six.live:
                    residual(six)
                if two.live:
                    mask(two)

            over_tiles(dve, step, 6)

        @block.gpsimd
        def _(pool):
            pool.memset(head_of[:, :], 1.0).then_inc(masks_filled, 1)
            pool.wait_ge(masks_filled, 1)
            pool.affine_select(out=head_of[:, :], in_=head_of[:, :], compare_op=ALU.is_ge, fill=0.0, base=0,
                               pattern=[[-HD, HEADS]], channel_multiplier=1).then_inc(masks_filled, 1)
            pool.wait_ge(masks_filled, 2)
            pool.affine_select(out=head_of[:, :], in_=head_of[:, :], compare_op=ALU.is_ge, fill=0.0, base=HD - 1,
                               pattern=[[HD, HEADS]], channel_multiplier=-1).then_inc(masks_done, 1)
            pool.wait_ge(masks_done, 1)
            pool.wait_ge(loaded, LOADS * DMA)

            def shift(t):
                pool.wait_ge(top_done, t.index + 1)
                wait(pool, prob_turned, t.index - 1)
                pool.tensor_tensor(expo[:, t.odd, :, :], score[:, t.odd, :, :], many(top[:, t.odd, :], SEQ),
                                   ALU.subtract).then_inc(shifted, 1)

            def spread_q(t):
                pool.wait_ge(qk_done, t.index + 1)
                wait(pool, scored, t.index - 1)
                pool.tensor_tensor(q_block[:, t.odd, 0, :, :], many(qk[:, t.odd, 0, 0:SEQ], HEADS, 1),
                                   many(head_of[:, :], SEQ), ALU.mult).then_inc(q_block_done[0], 1)

            def scale_root(t):
                pool.wait_ge(var_done, t.index + 1)
                pool.tensor_tensor(rstd[:, t.odd:t.odd + 1], var_eps[:, t.odd:t.odd + 1], eps_pow[:, :],
                                   ALU.pow).then_inc(rstd_done, 1)

            def bias_x(t):
                pool.wait_ge(xn_done, t.index + 1)
                pool.tensor_tensor(x[:, t.index, :], x[:, t.index, :], bo[:, :], ALU.add).then_inc(x_biased, 1)

            def bias_out(t):
                pool.wait_ge(out_raw_done, t.index + 1)
                wait(pool, out_turned, t.index - 1)
                pool.tensor_tensor(out[:, t.odd, :], out_raw[:, t.odd, :], bv[:, :], ALU.add).then_inc(out_done, 1)

            def step(t):
                now, one, three, four = t, t.back(1), t.back(3), t.back(4)
                if three.live:
                    shift(three)
                if now.live:
                    scale_root(now)
                if one.live:
                    spread_q(one)
                if now.live:
                    bias_x(now)
                if four.live:
                    bias_out(four)

            over_tiles(pool, step, 4)


def select_experts(nc, dram, keep):
    ctx = ExitStack()
    with ctx:
        m = Memory(nc, ctx, "sel")
        x, ident, eps_pow = keep["x"], keep["ident"], keep["eps_pow"]
        share, table, b_parts = keep["share"], keep["table"], keep["b_parts"]
        GROUP = 4
        GROUPS = TILES // GROUP
        PICKS = TILES * EXPERTS
        gate_w = m.sb("gate_w", [P, EXPERTS])
        upto = m.sb("upto", [P, P], BF16)
        ones = m.sb("ones", [P, P], BF16)
        number = m.sb("number", [P, EXPERTS])
        number_up = m.sb("number_up", [P, EXPERTS])
        region = m.sb("region", [P, EXPERTS])
        lane = m.sb("lane", [P, 1])
        token = m.sb("token", [P, TILES, TOP], I32)
        blank = m.sb("blank", [P, 2 * EXPERTS, ROW])
        not_first = m.sb("not_first", [P, EXPERTS, TILES])

        stats = m.sb("stats", [P, TILES, 6])
        mean_var = m.sb("mean_var", [P, TILES, 2])
        var_eps = m.sb("var_eps", [P, TILES])
        rstd = m.sb("rstd", [P, TILES])
        xn = m.sb("xn", [P, TILES, D])
        xn_now = m.sb("xn_now", [P, 2, GROUP, D])
        xn_t = m.sb("xn_t", [P, 2, GROUP, P])
        logit = m.sb("logit", [P, TOP, TILES, EXPERTS])
        best = m.sb("best", [P, TOP, TILES])
        even = m.sb("even", [P, TILES, EXPERTS])
        which = m.sb("which", [P, TILES])
        picked = m.sb("picked", [P, TOP, TILES, EXPERTS])
        less = m.sb("less", [P, TILES])
        second = m.sb("second", [P, TILES])
        both = m.sb("both", [P, TILES])
        taken = m.sb("taken", [P, TILES, EXPERTS], BF16)
        in_tile = m.sb("in_tile", [P, TILES, EXPERTS])
        up_to_tile = m.sb("up_to_tile", [P, EXPERTS, TILES])
        before = m.sb("before", [P, TILES, EXPERTS])
        order = m.sb("order", [P, TILES, EXPERTS])
        spread = m.sb("spread", [P, TILES, EXPERTS])
        row = m.sb("row", [P, TILES, TOP])
        rows_out = m.sb("rows_out", [P, 2, TOP, ROW])
        row_now = m.sb("row_now", [P, 2, TOP], I32)
        pad = m.sb("pad", [P, EXPERTS])
        pad_i = m.sb("pad_i", [P, EXPERTS], I32)
        steps = m.sb("steps", [P, TILES])
        over = m.sb("over", [P, EXPERTS, TILES])
        tiles = m.sb("tiles", [P, EXPERTS])
        unit = m.sb("unit", [P, EXPERTS])
        end = m.sb("end", [P, EXPERTS])
        start = m.sb("start", [P, EXPERTS])
        first_row = m.sb("first_row", [P, EXPERTS])
        index = m.sb("index", [P, SORTED])
        past = m.sb("past", [P, SORTED, EXPERTS])
        owner = m.sb("owner", [P, SORTED])
        own = m.sb("own", [P, SORTED, EXPERTS])
        from_row = m.sb("from_row", [P, SORTED])
        spare = m.sb("spare", [P, SORTED])
        blank_first = m.sb("blank_first", [P, 1])
        bias_rest = m.sb("bias_rest", [BIAS_ROWS, 2, P])
        bias_part = m.sb("bias_part", [BIAS_ROWS, 3, P], BF16)

        turn_ps = [m.ps(f"turn{i}", [P, GROUP, P]) for i in range(2)]
        logit_ps = m.ps("logit", [P, GROUPS, GROUP, EXPERTS])
        in_tile_ps = m.ps("in_tile", [P, PICKS])
        tile_ps = m.ps("tile", [P, PICKS])

        loaded, filled, ready = m.sem("loaded"), m.sem("filled"), m.sem("ready")
        stats_done, mean_done, var_done = m.sem("stats_done"), m.sem("mean_done"), m.sem("var_done")
        rstd_done, centered, xn_done = m.sem("rstd_done"), m.sem("centered"), m.sem("xn_done")
        xn_copied, turned, xn_t_done, gated = m.sem("xn_copied"), m.sem("turned"), m.sem("xn_t_done"), m.sem("gated")
        chosen, taken_done, counted = m.sem("chosen"), m.sem("taken_done"), m.sem("counted")
        second_done, shared, placed = m.sem("second_done"), m.sem("shared"), m.sem("placed")
        rows_filled, targets_filled = m.sem("rows_filled"), m.sem("targets_filled")
        scattered = [m.sem(f"scattered{i}") for i in range(2)]
        plan, padded, blank_written = m.sem("plan"), m.sem("padded"), m.sem("blank_written")
        zeroed, split, bias_loaded = m.sem("zeroed"), m.sem("split"), m.sem("bias_loaded")

        block = ctx.enter_context(nc.Block())

        @block.sync
        def _(sp):
            sp.dma_start(gate_w[:, :], dram["L1_ffn_W_gate"]).then_inc(loaded, DMA)
            sp.wait_ge(ready, 10)
            sp.dma_start(keep["sorted"][EXPERTS * REGION:, :].rearrange("(n p) d -> p n d", p=P),
                         blank[:, EXPERTS:, :]).then_inc(blank_written, DMA)
            sp.wait_ge(zeroed, 1)
            sp.wait_ge(split, 5)
            for n in range(3):
                sp.dma_start(b_parts[32 * n:32 * n + 1, :], bias_part[:, n, :]).then_inc(bias_loaded, DMA)
            sp.wait_ge(bias_loaded, 3 * DMA)
            sp.wait_ge(blank_written, DMA)

        @block.tensor
        def _(pe):
            pe.wait_ge(loaded, DMA)

            def turn(g):
                pe.wait_ge(xn_copied, g.index + 1)
                wait(pe, xn_t_done, g.index - 1)
                for n in range(GROUP):
                    last = pe.transpose(turn_ps[g.odd][:, n, :], xn_now[:, g.odd, n, :], ident[:, :])
                last.then_inc(turned, 1)

            def gate(g):
                pe.wait_ge(xn_t_done, g.index + 1)
                for n in range(GROUP):
                    last = pe.matmul(logit_ps[:, g.index, n, :], xn_t[:, g.odd, n, :], gate_w[:, :], start=True, stop=True)
                last.then_inc(gated, 1)

            def step(g):
                one = g.back(1)
                if g.live:
                    turn(g)
                if one.live:
                    gate(one)

            over_tiles(pe, step, 1, GROUPS)
            pe.wait_ge(ready, 10)
            pe.wait_ge(taken_done, 1)
            picks = taken[:, :, :].rearrange("p t x -> p (t x)")
            pe.matmul(in_tile_ps[:, :], upto[:, :], picks, start=True, stop=True)
            pe.matmul(tile_ps[:, :], ones[:, :], picks, start=True, stop=True).then_inc(counted, 1)

        @block.scalar
        def _(act):
            def bring(g):
                act.wait_ge(turned, g.index + 1)
                wait(act, gated, g.index - 1)
                act.copy(xn_t[:, g.odd, :, :], turn_ps[g.odd][:, :, :]).then_inc(xn_t_done, 1)

            def copy_xn(g):
                act.wait_ge(xn_done, g.index + 1)
                wait(act, turned, g.index - 1)
                act.copy(xn_now[:, g.odd, :, :], xn_groups[:, g.index, :, :]).then_inc(xn_copied, 1)

            xn_groups = xn[:, :, :].rearrange("p (g n) d -> p g n d", n=GROUP)

            def group_step(g):
                one = g.back(1)
                if g.live:
                    copy_xn(g)
                if one.live:
                    bring(one)

            over_tiles(act, group_step, 1, GROUPS)

            act.wait_ge(chosen, 13)
            act.activation(second[:, :], less[:, :], ACT.Exp).then_inc(second_done, 1)

            def fill(t):
                wait(act, scattered[t.odd], t.group * TOP * DMA)
                act.copy(rows_out[:, t.odd, :, 0:D], many(xn[:, t.index, :], TOP, 1)).then_inc(rows_filled, 1)

            over_tiles(act, fill, 0)

        @block.vector
        def _(dve):
            def moments(t):
                dve.bn_stats(stats[:, t.index, :], x[:, t.index, :]).then_inc(stats_done, 1)

            def step(t):
                if t.live:
                    moments(t)

            over_tiles(dve, step, 0)
            dve.wait_ge(stats_done, TILES)
            for t in range(TILES):
                last = dve.bn_aggr(mean_var[:, t, :], stats[:, t, :])
            last.then_inc(mean_done, 1)
            dve.wait_ge(mean_done, 1)
            dve.tensor_scalar(var_eps[:, :], mean_var[:, :, 1], EPS, None, ALU.add).then_inc(var_done, 1)
            dve.wait_ge(rstd_done, 1)
            for g in range(GROUPS):
                part = slice(g * GROUP, (g + 1) * GROUP)
                dve.tensor_tensor(xn[:, part, :], x[:, part, :], many(mean_var[:, part, 0], D), ALU.subtract).then_inc(centered, 1)
                dve.wait_ge(centered, g + 1)
                dve.tensor_tensor(xn[:, part, :], xn[:, part, :], many(rstd[:, part], D), ALU.mult).then_inc(xn_done, 1)

            bias = keep["b_rows"]
            dve.wait_ge(keep["w_loaded"], W_LOADS * DMA)
            dve.tensor_copy(bias_part[:, 0, :], bias[:, :]).then_inc(split, 1)
            dve.wait_ge(split, 1)
            dve.tensor_tensor(bias_rest[:, 0, :], bias[:, :], bias_part[:, 0, :], ALU.subtract).then_inc(split, 1)
            dve.wait_ge(split, 2)
            dve.tensor_copy(bias_part[:, 1, :], bias_rest[:, 0, :]).then_inc(split, 1)
            dve.wait_ge(split, 3)
            dve.tensor_tensor(bias_rest[:, 1, :], bias_rest[:, 0, :], bias_part[:, 1, :], ALU.subtract).then_inc(split, 1)
            dve.wait_ge(split, 4)
            dve.tensor_copy(bias_part[:, 2, :], bias_rest[:, 1, :]).then_inc(split, 1)

            dve.wait_ge(ready, 10)
            dve.wait_ge(gated, GROUPS)
            dve.tensor_copy(logit[:, 0, :, :], logit_ps[:, :, :, :].rearrange("p g n x -> p (g n) x")).then_inc(chosen, 1)
            for k in range(TOP):
                dve.wait_ge(chosen, 6 * k + 1)
                dve.tensor_reduce(best[:, k, :], logit[:, k, :, :], AX.X, ALU.max).then_inc(chosen, 1)
                dve.wait_ge(chosen, 6 * k + 2)
                dve.tensor_tensor(even[:, :, :], logit[:, k, :, :], many(best[:, k, :], EXPERTS), ALU.is_equal).then_inc(chosen, 1)
                dve.wait_ge(chosen, 6 * k + 3)
                dve.scalar_tensor_tensor(even[:, :, :], even[:, :, :], -float(EXPERTS), many(number_up[:, :], TILES, 1),
                                         ALU.mult, ALU.add).then_inc(chosen, 1)
                dve.wait_ge(chosen, 6 * k + 4)
                dve.tensor_reduce(which[:, :], even[:, :, :], AX.X, ALU.min).then_inc(chosen, 1)
                dve.wait_ge(chosen, 6 * k + 5)
                dve.tensor_tensor(picked[:, k, :, :], many(number[:, :], TILES, 1), many(which[:, :], EXPERTS),
                                  ALU.is_equal).then_inc(chosen, 1)
                if k == 0:
                    dve.wait_ge(chosen, 6)
                    dve.scalar_tensor_tensor(logit[:, 1, :, :], picked[:, 0, :, :], LEAST, logit[:, 0, :, :], ALU.mult,
                                             ALU.add).then_inc(chosen, 1)
            dve.wait_ge(chosen, 12)
            dve.tensor_tensor(taken[:, :, :], picked[:, 0, :, :], picked[:, 1, :, :], ALU.add).then_inc(taken_done, 1)
            dve.tensor_tensor(less[:, :], best[:, 1, :], best[:, 0, :], ALU.subtract).then_inc(chosen, 1)
            dve.wait_ge(counted, 1)
            dve.tensor_copy(over[:, :, :], tile_ps[:, :].rearrange("p (t x) -> p x t", x=EXPERTS)).then_inc(placed, 1)
            dve.tensor_copy(in_tile[:, :, :], in_tile_ps[:, :].rearrange("p (t x) -> p t x", x=EXPERTS)).then_inc(placed, 1)
            dve.wait_ge(placed, 2)
            dve.tensor_tensor_scan(up_to_tile[:, :, :].rearrange("p x t -> p (x t)"), not_first[:, :, :].rearrange("p x t -> p (x t)"),
                                   over[:, :, :].rearrange("p x t -> p (x t)"), 0.0, ALU.mult, ALU.add).then_inc(placed, 1)
            dve.wait_ge(placed, 3)
            dve.tensor_tensor(before[:, :, :].rearrange("p t x -> p x t"), up_to_tile[:, :, :], over[:, :, :],
                              ALU.subtract).then_inc(placed, 1)
            dve.wait_ge(placed, 4)
            dve.scalar_tensor_tensor(order[:, :, :], before[:, :, :], -1.0, in_tile[:, :, :], ALU.add, ALU.add).then_inc(placed, 1)
            dve.wait_ge(placed, 5)
            dve.tensor_tensor(order[:, :, :], order[:, :, :], many(region[:, :], TILES, 1), ALU.add).then_inc(placed, 1)
            dve.wait_ge(placed, 6)
            for k in range(TOP):
                dve.tensor_tensor(spread[:, :, :], picked[:, k, :, :], order[:, :, :], ALU.mult).then_inc(placed, 1)
                dve.wait_ge(placed, 7 + 2 * k)
                dve.tensor_reduce(row[:, :, k], spread[:, :, :], AX.X, ALU.add).then_inc(placed, 1)
                dve.wait_ge(placed, 8 + 2 * k)

            def fill(t):
                wait(dve, scattered[t.odd], t.group * TOP * DMA)
                dve.tensor_copy(rows_out[:, t.odd, :, D:ROW].rearrange("p k o -> p (k o)").bitcast(I32), token[:, t.index, :])
                dve.tensor_copy(row_now[:, t.odd, :], row[:, t.index, :]).then_inc(targets_filled, 1)

            for t in range(2):
                fill(Tile(0, t))

            dve.wait_ge(second_done, 1)
            dve.tensor_scalar(both[:, :], second[:, :], 1.0, None, ALU.add).then_inc(shared, 1)
            dve.wait_ge(shared, 1)
            dve.reciprocal(share[:, :, 0], both[:, :]).then_inc(shared, 1)
            dve.wait_ge(shared, 2)
            dve.tensor_tensor(share[:, :, 1], share[:, :, 0], second[:, :], ALU.mult).then_inc(shared, 1)

            total = up_to_tile[:, :, TILES - 1]
            dve.tensor_tensor(pad[:, :], total, region[:, :], ALU.add).then_inc(plan, 1)
            dve.wait_ge(plan, 1)
            dve.tensor_scalar(pad_i[:, :], pad[:, :], lane[:, 0:1], None, ALU.add).then_inc(plan, 1)
            dve.tensor_tensor(over[:, :, :], many(total, TILES), many(steps[:, :], EXPERTS, 1), ALU.is_gt).then_inc(plan, 1)
            dve.wait_ge(plan, 3)
            dve.tensor_reduce(tiles[:, :], over[:, :, :], AX.X, ALU.add).then_inc(plan, 1)
            dve.wait_ge(plan, 4)
            dve.tensor_tensor_scan(end[:, :], unit[:, :], tiles[:, :], 0.0, ALU.mult, ALU.add).then_inc(plan, 1)
            dve.wait_ge(plan, 5)
            dve.tensor_tensor(start[:, :], end[:, :], tiles[:, :], ALU.subtract).then_inc(plan, 1)
            dve.tensor_tensor(past[:, :, :], many(index[:, :], EXPERTS), many(end[:, :], SORTED, 1), ALU.is_ge).then_inc(plan, 1)
            dve.wait_ge(plan, 7)
            dve.tensor_reduce(owner[:, :], past[:, :, :], AX.X, ALU.add).then_inc(plan, 1)
            dve.scalar_tensor_tensor(first_row[:, :], start[:, :], -float(P), region[:, :], ALU.mult, ALU.add).then_inc(plan, 1)
            dve.wait_ge(plan, 9)
            dve.tensor_tensor(own[:, :, :], many(owner[:, :], EXPERTS), many(number[:, :], SORTED, 1),
                              ALU.is_equal).then_inc(plan, 1)
            dve.wait_ge(plan, 10)
            dve.tensor_tensor(own[:, :, :], own[:, :, :], many(first_row[:, :], SORTED, 1), ALU.mult).then_inc(plan, 1)
            dve.wait_ge(plan, 11)
            dve.tensor_reduce(from_row[:, :], own[:, :, :], AX.X, ALU.add).then_inc(plan, 1)
            dve.tensor_scalar(spare[:, :], owner[:, :], float(EXPERTS), None, ALU.is_ge).then_inc(plan, 1)
            dve.tensor_scalar(table[:, 0, :], owner[:, :], float(EXPERTS - 1), None, ALU.min).then_inc(plan, 1)
            dve.tensor_scalar(blank_first[:, :], end[:, EXPERTS - 1:EXPERTS], -float(P), float(EXPERTS * REGION),
                              ALU.mult, ALU.add).then_inc(plan, 1)
            dve.wait_ge(plan, 15)
            dve.scalar_tensor_tensor(from_row[:, :], index[:, :], float(P), from_row[:, :], ALU.mult, ALU.add).then_inc(plan, 1)
            dve.wait_ge(plan, 16)
            dve.scalar_tensor_tensor(table[:, 1, :], spare[:, :], blank_first[:, 0:1], from_row[:, :], ALU.mult,
                                     ALU.add).then_inc(plan, 1)

            def later(t):
                if t.live and (not isinstance(t.group, int) or t.index >= 2):
                    fill(t)

            over_tiles(dve, later, 0)

        @block.gpsimd
        def _(pool):
            pool.memset(b_parts[:, :].bitcast(U32), 0).then_inc(zeroed, 1)
            pool.memset(upto[:, :], 1.0).then_inc(filled, 1)
            pool.memset(not_first[:, :, :], 1.0).then_inc(filled, 1)
            pool.memset(blank[:, :, :], 0.0).then_inc(filled, 1)
            pool.memset(ones[:, :], 1.0).then_inc(ready, 1)
            pool.memset(unit[:, :], 1.0).then_inc(ready, 1)
            pool.iota(number[:, :], pattern=[[1, EXPERTS]], base=0, channel_multiplier=0,
                      allow_small_or_imprecise_dtypes=True).then_inc(ready, 1)
            pool.iota(number_up[:, :], pattern=[[1, EXPERTS]], base=EXPERTS, channel_multiplier=0,
                      allow_small_or_imprecise_dtypes=True).then_inc(ready, 1)
            pool.iota(region[:, :], pattern=[[REGION, EXPERTS]], base=0, channel_multiplier=0,
                      allow_small_or_imprecise_dtypes=True).then_inc(ready, 1)
            pool.iota(lane[:, :], pattern=[[0, 1]], base=0, channel_multiplier=1,
                      allow_small_or_imprecise_dtypes=True).then_inc(ready, 1)
            pool.iota(steps[:, :], pattern=[[P, TILES]], base=0, channel_multiplier=0,
                      allow_small_or_imprecise_dtypes=True).then_inc(ready, 1)
            pool.iota(index[:, :], pattern=[[1, SORTED]], base=0, channel_multiplier=0,
                      allow_small_or_imprecise_dtypes=True).then_inc(filled, 1)
            pool.iota(token[:, :, :], pattern=[[P * TOP, TILES], [1, TOP]], base=0, channel_multiplier=TOP).then_inc(filled, 1)
            pool.wait_ge(filled, 5)
            pool.affine_select(out=upto[:, :], in_=upto[:, :], compare_op=ALU.is_ge, fill=0.0, base=0,
                               pattern=[[1, P]], channel_multiplier=-1).then_inc(ready, 1)
            pool.affine_select(out=not_first[:, :, :], in_=not_first[:, :, :], compare_op=ALU.not_equal, fill=0.0, base=0,
                               pattern=[[0, EXPERTS], [1, TILES]], channel_multiplier=0).then_inc(ready, 1)
            pool.iota(blank[:, :, D:ROW].rearrange("p n o -> p (n o)").bitcast(I32), pattern=[[P, 2 * EXPERTS]],
                      base=TILES * P * TOP, channel_multiplier=1).then_inc(ready, 1)
            pool.wait_ge(ready, 10)
            pool.wait_ge(var_done, 1)
            pool.tensor_tensor(rstd[:, :], var_eps[:, :], eps_pow[:, 0:1].to_broadcast([P, TILES]), ALU.pow).then_inc(rstd_done, 1)

            def scatter(t):
                pool.wait_ge(rows_filled, t.index + 1)
                pool.wait_ge(targets_filled, t.index + 1)
                apart(pool)
                for k in range(TOP):
                    pool.indirect_dma_start(keep["sorted"], bass.IndirectOffsetOnAxis(ap=row_now[:, t.odd, k:k + 1], axis=0),
                                            rows_out[:, t.odd, k, :], None).then_inc(scattered[t.odd], DMA)

            over_tiles(pool, scatter, 0)
            pool.wait_ge(plan, 2)
            for n in range(EXPERTS):
                pool.indirect_dma_start(keep["sorted"], bass.IndirectOffsetOnAxis(ap=pad_i[:, n:n + 1], axis=0),
                                        blank[:, n, :], None).then_inc(padded, DMA)
            pool.wait_ge(padded, EXPERTS * DMA)
            for o in range(2):
                pool.wait_ge(scattered[o], TILES // 2 * TOP * DMA)
            pool.wait_ge(plan, 17)


def run_experts(nc, dram, keep):
    ctx = ExitStack()
    with ctx:
        m = Memory(nc, ctx, "run")
        ident, w_in, w_out, b_parts, table = (keep[n] for n in ("ident", "w_in", "w_out", "b_parts", "table"))
        BUFS = 4
        ones = m.sb("ones", [96, P], BF16)
        xs = m.sb("xs", [P, BUFS, ROW])
        target_new = m.sb("target_new", [P, BUFS], I32)
        target = m.sb("target", [P, BUFS], I32)
        xs_t = m.sb("xs_t", [P, 2, P])
        hid = m.sb("hid", [P, 2, MLP])
        hid_t = m.sb("hid_t", [P, 2, BLOCKS, P])
        y = m.sb("y", [P, BUFS, D])
        turn_ps = m.ps("turn", [P, 512])
        hid_ps = [m.ps(f"hid{i}", [P, MLP]) for i in range(2)]
        hid_t_ps = [m.ps(f"hid_t{i}", [P, BLOCKS, P]) for i in range(2)]
        y_ps = [m.ps(f"y{i}", [P, 512]) for i in range(2)]

        ready = m.sem("ready")
        xs_loaded = [m.sem(f"xs_loaded{i}") for i in range(BUFS)]
        stored = [m.sem(f"stored{i}") for i in range(BUFS)]
        turned, xs_t_done, hid_summed, hid_done = m.sem("turned"), m.sem("xs_t_done"), m.sem("hid_summed"), m.sem("hid_done")
        hid_turned, hid_t_done, y_summed, y_done = m.sem("hid_turned"), m.sem("hid_t_done"), m.sem("y_summed"), m.sem("y_done")

        target_taken, target_done = m.sem("target_taken"), m.sem("target_done")
        sorted_rows = keep["sorted"]
        block = ctx.enter_context(nc.Block())

        @block.sync
        def _(sp):
            def load(t):
                wait(sp, turned, t.index - BUFS + 1)
                wait(sp, target_taken, t.index - BUFS + 1)
                at = sp.value_load(table[0:1, 1, t.index:t.index + 1] if isinstance(t.index, int) else
                                   table[0:1, 1, bass.ds(t.index, 1)], min_val=0, max_val=EXPERTS * (REGION + P) - P)
                sp.dma_start(xs[:, t.at, :], sorted_rows[bass.ds(at, P), :]).then_inc(xs_loaded[t.at], DMA)

            over_tiles(sp, load, 0, SORTED, BUFS)

        @block.tensor
        def _(pe):
            pe.wait_ge(keep["w_loaded"], W_LOADS * DMA)
            pe.wait_ge(ready, 1)

            def owner(t):
                return pe.value_load(table[0:1, 0, bass.ds(t.index, 1)], min_val=0, max_val=EXPERTS - 1)

            def turn(t):
                pe.wait_ge(xs_loaded[t.at], (t.group + 1) * DMA)
                wait(pe, xs_t_done, t.index)
                pe.transpose(turn_ps[:, 0:P], xs[:, t.at, 0:D], ident[:, :]).then_inc(turned, 1)

            def widen(t, n):
                pe.wait_ge(xs_t_done, t.index + 1)
                wait(pe, hid_done, t.index - 1)
                pe.matmul(hid_ps[t.odd][:, :], ones[:, :], b_parts[:, bass.ds(n * MLP, MLP)], start=True, stop=False)
                pe.matmul(hid_ps[t.odd][:, :], xs_t[:, t.odd, :], w_in[:, n, :], start=False, stop=True).then_inc(hid_summed, 1)

            def turn_hidden(t):
                pe.wait_ge(hid_done, t.index + 1)
                wait(pe, hid_t_done, t.index - 1)
                for c in range(BLOCKS):
                    last = pe.transpose(hid_t_ps[t.odd][:, c, :], hid[:, t.odd, c * P:(c + 1) * P], ident[:, :])
                last.then_inc(hid_turned, 1)

            def narrow(t, n):
                pe.wait_ge(hid_t_done, t.index + 1)
                wait(pe, y_done, t.index - 1)
                pe.matmul(y_ps[t.odd][:, 0:D], ones[:, :], b_parts[:, bass.ds(n * D + EXPERTS * MLP, D)], start=True, stop=False)
                for c in range(BLOCKS):
                    last = pe.matmul(y_ps[t.odd][:, 0:D], hid_t[:, t.odd, c, :], w_out[:, n, c, :],
                                     start=False, stop=(c == BLOCKS - 1))
                last.then_inc(y_summed, 1)

            def step(t):
                one, three, four = t.back(1), t.back(3), t.back(4)
                last = owner(four) if four.live else None
                first = owner(one) if one.live else None
                if three.live:
                    turn_hidden(three)
                if t.live:
                    turn(t)
                if four.live:
                    narrow(four, last)
                if one.live:
                    widen(one, first)

            over_tiles(pe, step, 4, SORTED, BUFS)

        @block.scalar
        def _(act):
            def step(t):
                one = t.back(1)
                if t.live:
                    act.wait_ge(turned, t.index + 1)
                    wait(act, hid_summed, t.index - 1)
                    act.copy(xs_t[:, t.odd, :], turn_ps[:, 0:P]).then_inc(xs_t_done, 1)
                if one.live:
                    act.wait_ge(hid_summed, one.index + 1)
                    wait(act, hid_turned, one.index - 1)
                    act.activation(hid[:, one.odd, :], hid_ps[one.odd][:, :], ACT.Gelu).then_inc(hid_done, 1)

            over_tiles(act, step, 1, SORTED, BUFS)

        @block.vector
        def _(dve):
            dve.memset(ones[:, :], 1.0).then_inc(ready, 1)

            def step(t):
                three, four = t.back(3), t.back(4)
                if t.live:
                    dve.wait_ge(xs_loaded[t.at], (t.group + 1) * DMA)
                    wait(dve, target_done, t.index - BUFS + 1)
                    dve.tensor_copy(target_new[:, t.at:t.at + 1], xs[:, t.at, D:ROW].bitcast(I32)).then_inc(target_taken, 1)
                if three.live:
                    dve.wait_ge(hid_turned, three.index + 1)
                    wait(dve, y_summed, three.index - 1)
                    dve.tensor_copy(hid_t[:, three.odd, :, :], hid_t_ps[three.odd][:, :, :]).then_inc(hid_t_done, 1)
                    dve.wait_ge(target_taken, three.index + 1)
                    wait(dve, stored[three.at], three.group * DMA)
                    dve.tensor_copy(target[:, three.at:three.at + 1], target_new[:, three.at:three.at + 1]).then_inc(target_done, 1)
                if four.live:
                    dve.wait_ge(y_summed, four.index + 1)
                    wait(dve, stored[four.at], four.group * DMA)
                    dve.tensor_copy(y[:, four.at, :], y_ps[four.odd][:, 0:D]).then_inc(y_done, 1)

            over_tiles(dve, step, 4, SORTED, BUFS)

        @block.gpsimd
        def _(pool):
            def store(t):
                pool.wait_ge(y_done, t.index + 1)
                pool.wait_ge(target_done, t.index + 1)
                apart(pool)
                pool.indirect_dma_start(keep["result"], bass.IndirectOffsetOnAxis(ap=target[:, t.at:t.at + 1], axis=0),
                                        y[:, t.at, :], None).then_inc(stored[t.at], DMA)

            over_tiles(pool, store, 0, SORTED, BUFS)
            for i in range(BUFS):
                pool.wait_ge(stored[i], SORTED // BUFS * DMA)


def combine(nc, dram, keep, out):
    ctx = ExitStack()
    with ctx:
        m = Memory(nc, ctx, "comb")
        x, share = keep["x"], keep["share"]
        GROUP, BUFS = 4, 4
        GROUPS = TILES // GROUP
        got = [m.sb(f"got{i}", [P, GROUP, TOP, D]) for i in range(BUFS)]
        gathered = [m.sem(f"gathered{i}") for i in range(BUFS)]
        weighed, first_done, x_done, written = m.sem("weighed"), m.sem("first_done"), m.sem("x_done"), m.sem("written")
        out_tiles = out.rearrange("b s d -> (b s) d").rearrange("(t p) d -> p t d", p=P)
        result = keep["result"][0:TILES * P * TOP, :].rearrange("(t p k) d -> p t k d", p=P, k=TOP)
        block = ctx.enter_context(nc.Block())

        @block.sync
        def _(sp):
            for g in range(GROUPS):
                part = slice(g * GROUP, (g + 1) * GROUP)
                if g >= BUFS:
                    sp.wait_ge(x_done, g - BUFS + 1)
                sp.dma_start(got[g % BUFS][:, :, :, :], result[:, part, :, :]).then_inc(gathered[g % BUFS], DMA)

        @block.vector
        def _(dve):
            for g in range(GROUPS):
                part, now = slice(g * GROUP, (g + 1) * GROUP), got[g % BUFS]
                dve.wait_ge(gathered[g % BUFS], (g // BUFS + 1) * DMA)
                dve.tensor_tensor(now[:, :, :, :], now[:, :, :, :], many(share[:, part, :], D, 3), ALU.mult).then_inc(weighed, 1)
                dve.wait_ge(weighed, g + 1)
                dve.tensor_tensor(x[:, part, :], x[:, part, :], now[:, :, 0, :], ALU.add).then_inc(first_done, 1)
                dve.wait_ge(first_done, g + 1)
                dve.tensor_tensor(x[:, part, :], x[:, part, :], now[:, :, 1, :], ALU.add).then_inc(x_done, 1)

        @block.scalar
        def _(act):
            for g in range(GROUPS):
                part = slice(g * GROUP, (g + 1) * GROUP)
                act.wait_ge(x_done, g + 1)
                act.dma_start(out_tiles[:, part, :], x[:, part, :]).then_inc(written, DMA)
            act.wait_ge(keep["mask_loaded"], 2 * DMA)
            act.wait_ge(written, GROUPS * DMA)




def setup(nc, dram, keep):
    x, ident, eps_pow = keep["x"], keep["ident"], keep["eps_pow"]
    x_tiles = dram["x"].rearrange("b s d -> (b s) d").rearrange("(t p) d -> p t d", p=P)
    with nc.Block() as block:

        @block.sync
        def _(sp):
            part = slice(0, TILES // X_PARTS)
            sp.dma_start(x[:, part, :], x_tiles[:, part, :]).then_inc(keep["x_loaded"], DMA)

        @block.gpsimd
        def _(pool):
            pool.memset(eps_pow[:, :], -0.5).then_inc(keep["ident_ready"], 1)
            pool.memset(ident[:, :], 0.0).then_inc(keep["ident_ready"], 1)
            pool.wait_ge(keep["ident_ready"], 2)
            pool.affine_select(out=ident[:, :], in_=ident[:, :], compare_op=ALU.not_equal, fill=1.0, base=0,
                               pattern=[[-1, P]], channel_multiplier=1).then_inc(keep["ident_ready"], 1)


def network(nc, dram, out):
    ctx = ExitStack()
    with ctx:
        m = Memory(nc, ctx, "net")
        keep = {
            "x": m.sb("x", [P, TILES, D]), "ident": m.sb("ident", [P, P]), "eps_pow": m.sb("eps_pow", [P, 1]),
            "mask": m.sb("mask", [P, TILES, PER_TILE * SEQ], I32), "x_loaded": m.sem("x_loaded"),
            "mask_loaded": m.sem("mask_loaded"), "ident_ready": m.sem("ident_ready"), "ident_count": 3,
            "w_in": m.sb("w_in", [P, EXPERTS, MLP]), "w_out": m.sb("w_out", [P, EXPERTS, BLOCKS, D]),
            "b_parts": m.sb("b_parts", [96, EXPERTS * (MLP + D)], BF16),
            "b_rows": m.sb("b_rows", [BIAS_ROWS, P]), "w_loaded": m.sem("w_loaded"),
            "share": m.sb("share", [P, TILES, TOP]), "table": m.sb("table", [P, 2, SORTED], I32),
            "sorted": nc.dram_tensor("sorted_rows", (EXPERTS * (REGION + P), ROW), F32, kind="Internal").ap(),
            "result": nc.dram_tensor("result_rows", ((TILES * TOP + 2 * EXPERTS) * P, D), F32, kind="Internal").ap(),
        }
        setup(nc, dram, keep)
        wide_attention(nc, dram, keep)
        routed_attention(nc, dram, keep)
        masked_attention(nc, dram, keep)
        select_experts(nc, dram, keep)
        run_experts(nc, dram, keep)
        combine(nc, dram, keep, out)


_INS = ["x", "ctx_1024", "mask_Bx1xSxS2_ik1"]
_INS += [f"L0_xattn_{n}" for n in ("Wq", "bq", "Wk", "bk", "Wv", "bv", "Wu", "bu")]
_INS += [f"L0_ffn_{n}" for n in ("Wq", "bq", "Wk", "bk", "Wv", "bv", "We", "be", "Wsw", "bsw", "gamma", "beta")]
_INS += [f"L1_xattn_{n}" for n in ("Wv", "bv", "Wk", "bk", "Wq", "bq", "Wo", "bo")]
_INS += [f"L1_ffn_{n}" for n in ("W_gate", "W_in", "b_in", "W_out", "b_out")]


def kernel(**inputs):
    import numpy as np
    from concourse import bacc
    from concourse.bass_utils import run_bass_kernel_spmd

    nc = bacc.Bacc("TRN2", target_bir_lowering=False, num_devices=1)
    arrays, dram = {}, {}
    for name in _INS:
        a = np.ascontiguousarray(inputs[name])
        arrays[f"in_{name}"] = a
        dram[name] = nc.dram_tensor(f"in_{name}", a.shape, mybir.dt.from_np(a.dtype), kind="ExternalInput").ap()
    out = nc.dram_tensor("out_x", inputs["x"].shape, F32, kind="ExternalOutput").ap()
    network(nc, dram, out)
    r = run_bass_kernel_spmd(nc, [arrays], core_ids=[0])
    return r.results[0]["out_x"]
```

```python
from contextlib import ExitStack

import concourse.bass as bass
from concourse import mybir

F32 = mybir.dt.float32
BF16 = mybir.dt.bfloat16
I32 = mybir.dt.int32
U32 = mybir.dt.uint32
ALU = mybir.AluOpType
ACT = mybir.ActivationFunctionType
AX = mybir.AxisListType

P = 128
BATCHES, SEQ, D = 64, 64, 128
TILES = BATCHES * SEQ // P
PER_TILE = P // SEQ
HEADS = 16
CHUNKS = HEADS // 2
PAIRS = CHUNKS // 2
HK = 64
WIDE = HEADS * HK
HD = D // HEADS
EXPERTS = 8
CAPACITY = int(1.2 * BATCHES * SEQ / EXPERTS)
MLP = 512
BLOCKS = MLP // P
EPS = 1e-5
TOP = 2
REGION = BATCHES * SEQ + P
SORTED = BATCHES * SEQ * TOP // P + EXPERTS
VCOL = 2 * HD + 1
ROW = D + 1
LEAST = -3.0e38
LAYER_LOADS = 20
W_LOADS = 2 * EXPERTS + 2
FIRST_ROOTS = 3
X_PARTS = 4
DMA = 16


class Tile:

    def __init__(self, group, at, count=TILES, size=2):
        self.group, self.at, self.count, self.size = group, at, count, size
        self.odd = at % 2
        self.index = group * size + at if at else group * size

    def back(self, lag):
        at = self.at - lag
        groups = at // self.size
        return Tile(self.group + groups if groups else self.group, at % self.size, self.count, self.size)

    @property
    def live(self):
        return not isinstance(self.group, int) or 0 <= self.index < self.count


def scalar_at(buf, t):
    return buf[:, t.index:t.index + 1] if isinstance(t.index, int) else buf[:, bass.ds(t.index, 1)]


def wait(eng, sem, value):
    if not isinstance(value, int) or value > 0:
        eng.wait_ge(sem, value)


def apart(eng):
    eng.nop(nofuse=True)


def over_tiles(eng, step, lag, count=TILES, size=2, before_loop=None):
    first = (lag + 2 * size - 1) // size
    for s in range(first * size):
        step(Tile(s // size, s % size, count, size))
    if before_loop:
        before_loop()
    with eng.Fori(first, count // size) as group:
        for at in range(size):
            step(Tile(group, at, count, size))
    for s in range(count, count + lag):
        step(Tile(s // size, s % size, count, size))


class Memory:

    def __init__(self, nc, ctx, tag):
        self.nc, self.ctx, self.tag = nc, ctx, tag
        self.semaphores = []
        ctx.callback(self.clear)

    def clear(self):
        self.nc.clear_and_free_semaphores(self.semaphores)
        self.nc.all_engine_barrier()

    def sb(self, name, shape, dt=F32):
        return self.ctx.enter_context(self.nc.sbuf_tensor(f"{self.tag}_{name}", shape, dt))

    def ps(self, name, shape, dt=F32):
        return self.ctx.enter_context(self.nc.psum_tensor(f"{self.tag}_{name}_ps", shape, dt))

    def sem(self, name):
        self.semaphores.append(self.nc.alloc_semaphore(name=f"{self.tag}_{name}"))
        return self.semaphores[-1]


def many(ap, n, axis=2):
    ap = ap.unsqueeze(axis)
    shape = list(ap.shape)
    shape[axis] = n
    return ap.to_broadcast(shape)


def wide_attention(nc, dram, keep):
    ctx = ExitStack()
    with ctx:
        m = Memory(nc, ctx, "wide")
        x, ident, eps_pow = keep["x"], keep["ident"], keep["eps_pow"]
        wq = m.sb("wq", [P, CHUNKS, P])
        wk = m.sb("wk", [P, CHUNKS, P])
        wv = m.sb("wv", [P, WIDE])
        wu = m.sb("wu", [P, PAIRS, 2, D])
        bq = m.sb("bq", [P, CHUNKS])
        bk = m.sb("bk", [P, CHUNKS])
        bv = m.sb("bv", [P, HEADS])
        bv_wide = m.sb("bv_wide", [P, PAIRS * 2, P])
        bu = m.sb("bu", [P, D])
        ctx_in = m.sb("ctx_in", [P, 2, D])
        stats = m.sb("stats", [P, 2, 6])
        mean_var = m.sb("mean_var", [P, 2, 2])
        var_eps = m.sb("var_eps", [P, 2])
        rstd = m.sb("rstd", [P, 2])
        xn = m.sb("xn", [P, 2, D])
        xc_t = m.sb("xc_t", [P, 2, 2, P])
        q_block = m.sb("q_block", [P, 2, CHUNKS, PER_TILE, 2, SEQ])
        k_t = m.sb("k_t", [P, 2, CHUNKS, P])
        v_block = m.sb("v_block", [P, 2, PER_TILE, PAIRS, 2, 2, HK])
        top = m.sb("top", [P, 2, HEADS])
        expo = m.sb("expo", [P, 2, HEADS, SEQ])
        total = m.sb("total", [P, 2, HEADS])
        share = m.sb("share", [P, 2, HEADS])
        prob = m.sb("prob", [P, 2, HEADS, SEQ])
        prob_t = m.sb("prob_t", [P, 2, PER_TILE, PAIRS, P])
        out_t = m.sb("out_t", [P, 2, PAIRS, 2, PER_TILE, SEQ])

        proj_ps = [m.ps(f"proj{i}", [P, 4, P]) for i in range(2)]
        score_ps = m.ps("score", [P, PER_TILE, CHUNKS * SEQ])
        turn_ps = m.ps("turn", [P, PER_TILE, 512])
        norm_ps = m.ps("norm", [P, 512])
        up_ps = m.ps("up", [P, 512])

        x_rest = m.sem("x_rest")
        loaded = m.sem("loaded")
        bias_loaded = m.sem("bias_loaded")
        blocks_zero = m.sem("blocks_zero")
        bv_spread = m.sem("bv_spread")
        bu_summed = m.sem("bu_summed")
        bu_ready = m.sem("bu_ready")
        ctx_loaded = [m.sem(f"ctx_loaded{i}") for i in range(2)]
        stats_done = m.sem("stats_done")
        next_stats_done = m.sem("next_stats_done")
        mean_done = m.sem("mean_done")
        var_done = m.sem("var_done")
        rstd_done = m.sem("rstd_done")
        xn_done = m.sem("xn_done")
        x_biased = m.sem("x_biased")
        turned_in = m.sem("turned_in")
        xc_done = m.sem("xc_done")
        q_filled = m.sem("q_filled")
        k_filled = m.sem("k_filled")
        v_filled = m.sem("v_filled")
        q_done = m.sem("q_done")
        k_done = m.sem("k_done")
        v_done = m.sem("v_done")
        scored = m.sem("scored")
        top_done = m.sem("top_done")
        shifted = m.sem("shifted")
        exp_done = m.sem("exp_done")
        total_done = m.sem("total_done")
        share_done = m.sem("share_done")
        prob_done = m.sem("prob_done")
        prob_turned = m.sem("prob_turned")
        prob_t_done = m.sem("prob_t_done")
        mixed = m.sem("mixed")
        out_t_done = m.sem("out_t_done")
        up_done = m.sem("up_done")
        x_done = m.sem("x_done")

        ctx_tiles = dram["ctx_1024"].rearrange("b s d -> (b s) d").rearrange("(t p) d -> t p d", p=P)

        block = ctx.enter_context(nc.Block())
        BIAS_LOADS = 7

        @block.sync
        def _(sp):
            sp.dma_start(ctx_in[:, 0, :], ctx_tiles[0]).then_inc(ctx_loaded[0], DMA)
            sp.dma_start(ctx_in[:, 1, :], ctx_tiles[1]).then_inc(ctx_loaded[1], DMA)
            wu_rows = dram["L0_xattn_Wu"].rearrange("(c p h d) n -> p h d c n", c=PAIRS, p=2, h=2)
            for half in range(2):
                rows = slice(half * HK, half * HK + HK)
                sp.dma_start(bv[rows, :], dram["L0_xattn_bv"].rearrange("(h d) -> d h", d=HK),
                             allow_slow_non_contiguous=True).then_inc(bias_loaded, DMA)
                for h in range(2):
                    sp.dma_start(wu[rows, :, h, :], wu_rows[half, h]).then_inc(bias_loaded, DMA)
            sp.dma_start(bu[:, :], dram["L0_xattn_bu"].partition_broadcast(P)).then_inc(bias_loaded, DMA)
            x_tiles = dram["x"].rearrange("b s d -> (b s) d").rearrange("(t p) d -> p t d", p=P)
            for n in range(1, X_PARTS):
                part = slice(n * TILES // X_PARTS, (n + 1) * TILES // X_PARTS)
                sp.dma_start(x[:, part, :], x_tiles[:, part, :]).then_inc(x_rest, DMA)
            start_weight_loads(sp, dram, keep)

            def step(t):
                u = t.back(-2)
                if u.live:
                    wait(sp, turned_in, t.index + 1)
                    sp.dma_start(ctx_in[:, u.odd, :], ctx_tiles[u.index]).then_inc(ctx_loaded[u.odd], DMA)

            with sp.Fori(0, TILES // 2 - 1) as group:
                step(Tile(group, 0))
                step(Tile(group, 1))

        @block.tensor
        def _(pe):
            pe.wait_ge(bv_spread, 2)
            pe.wait_ge(bias_loaded, BIAS_LOADS * DMA)
            for n in range(PAIRS * 2):
                last = pe.matmul(up_ps[:, 0:D], bv_wide[:, n, :], wu[:, n // 2, n % 2, :],
                                 start=(n == 0), stop=(n == PAIRS * 2 - 1))
            last.then_inc(bu_summed, 1)
            pe.wait_ge(loaded, 5 * DMA)
            pe.wait_ge(blocks_zero, 2)
            pe.wait_ge(keep["ident_ready"], keep["ident_count"])

            def turn_in(t):
                pe.wait_ge(xn_done, t.index + 1)
                pe.wait_ge(ctx_loaded[t.odd], (t.group + 1) * DMA)
                wait(pe, xc_done, t.index)
                pe.transpose(norm_ps[:, 0:P], xn[:, t.odd, :], ident[:, :])
                pe.transpose(norm_ps[:, P:2 * P], ctx_in[:, t.odd, :], ident[:, :]).then_inc(turned_in, 1)

            def project_q(t, half):
                pe.wait_ge(xc_done, t.index + 1)
                if half == 0:
                    wait(pe, v_done, t.index * 2 - 1)
                else:
                    pe.wait_ge(q_done, t.index * 2 + 1)
                for c in range(4):
                    last = pe.matmul(proj_ps[0][:, c, :], wq[:, half * 4 + c, :], xc_t[:, t.odd, 0, :],
                                     start=True, stop=True)
                last.then_inc(q_filled, 1)

            def project_k(t, half):
                if half == 0:
                    wait(pe, v_done, t.index * 2)
                else:
                    pe.wait_ge(k_done, t.index * 2 + 1)
                for c in range(4):
                    last = pe.matmul(proj_ps[1][:, c, :], wk[:, half * 4 + c, :], xc_t[:, t.odd, 1, :],
                                     start=True, stop=True)
                last.then_inc(k_filled, 1)

            def project_v(t, half):
                pe.wait_ge(q_done if half == 0 else k_done, t.index * 2 + 2)
                last = pe.matmul(proj_ps[half][:, :, :], xc_t[:, t.odd, 1, :], wv[:, half * 512:half * 512 + 512],
                                 start=True, stop=True)
                last.then_inc(v_filled, 1)

            def scores(t):
                pe.wait_ge(q_done, 2 * t.index + 2)
                pe.wait_ge(k_done, 2 * t.index + 2)
                wait(pe, shifted, t.index)
                for b in range(PER_TILE):
                    for c in range(CHUNKS):
                        last = pe.matmul(score_ps[:, b, c * SEQ:(c + 1) * SEQ], q_block[:, t.odd, c, b, :, :],
                                         k_t[:, t.odd, c, b * SEQ:(b + 1) * SEQ], start=True, stop=True)
                last.then_inc(scored, 1)

            def turn_prob(t):
                pe.wait_ge(prob_done, t.index + 1)
                wait(pe, out_t_done, t.index)
                for b in range(PER_TILE):
                    for c in range(PAIRS):
                        h = b * CHUNKS + 2 * c
                        last = pe.transpose(turn_ps[:, b, c * P:(c + 1) * P], prob[:, t.odd, h:h + 2, :], ident[:, :])
                last.then_inc(prob_turned, 1)

            def mix(t):
                pe.wait_ge(prob_t_done, t.index + 1)
                pe.wait_ge(v_done, 2 * t.index + 2)
                for b in range(PER_TILE):
                    for c in range(PAIRS):
                        for h in range(2):
                            at = (2 * c + h) * SEQ
                            last = pe.matmul(turn_ps[:, b, at:at + SEQ], v_block[:, t.odd, b, c, h, :, :],
                                             prob_t[:, t.odd, b, c, h * SEQ:(h + 1) * SEQ], start=True, stop=True)
                last.then_inc(mixed, 1)

            def up(t):
                pe.wait_ge(out_t_done, t.index + 1)
                wait(pe, x_done, t.index)
                for n in range(PAIRS * 2):
                    last = pe.matmul(up_ps[:, 0:D], out_t[:, t.odd, n // 2, n % 2, :, :], wu[:, n // 2, n % 2, :],
                                     start=(n == 0), stop=(n == PAIRS * 2 - 1))
                last.then_inc(up_done, 1)

            pe.wait_ge(bu_ready, 1)

            def step(t):
                now, one, two, three = t, t.back(1), t.back(2), t.back(3)
                if two.live:
                    scores(two)
                if three.live:
                    turn_prob(three)
                if one.live:
                    project_q(one, 0)
                    project_k(one, 0)
                if three.live:
                    mix(three)
                if one.live:
                    project_q(one, 1)
                    project_k(one, 1)
                if now.live:
                    turn_in(now)
                if three.live:
                    up(three)
                if one.live:
                    project_v(one, 0)
                    project_v(one, 1)

            over_tiles(pe, step, 3)

        @block.scalar
        def _(act):
            act.dma_start(wq[:, :, :], dram["L0_xattn_Wq"].rearrange("d (c m) -> d c m", m=P)).then_inc(loaded, DMA)
            act.dma_start(wk[:, :, :], dram["L0_xattn_Wk"].rearrange("d (c m) -> d c m", m=P)).then_inc(loaded, DMA)
            act.dma_start(bq[:, :], dram["L0_xattn_bq"].rearrange("(c m) -> m c", m=P),
                          allow_slow_non_contiguous=True).then_inc(loaded, DMA)
            act.dma_start(bk[:, :], dram["L0_xattn_bk"].rearrange("(c m) -> m c", m=P),
                          allow_slow_non_contiguous=True).then_inc(loaded, DMA)
            act.dma_start(wv[:, :], dram["L0_xattn_Wv"]).then_inc(loaded, DMA)
            act.wait_ge(loaded, 5 * DMA)
            act.wait_ge(blocks_zero, 2)

            def bring_prob(t):
                act.wait_ge(prob_turned, t.index + 1)
                wait(act, mixed, t.index - 1)
                act.copy(prob_t[:, t.odd, :, :, :], turn_ps[:, :, :]).then_inc(prob_t_done, 1)

            def bring_k(t, half):
                act.wait_ge(k_filled, 2 * t.index + half + 1)
                if half == 0:
                    wait(act, scored, t.index - 1)
                for c in range(4):
                    n = half * 4 + c
                    last = act.activation(k_t[:, t.odd, n, :], proj_ps[1][:, c, :], ACT.Identity,
                                          bias=bk[:, n:n + 1])
                last.then_inc(k_done, 1)

            def bring_v(t, half):
                act.wait_ge(v_filled, 2 * t.index + half + 1)
                if half == 0:
                    wait(act, mixed, t.index - 1)
                for b in range(PER_TILE):
                    for p in range(2):
                        frm = proj_ps[half][b * SEQ:(b + 1) * SEQ, :, :].rearrange(
                            "k (c p) (h d) -> k c p h d", p=2, h=2)[:, :, p, :, :]
                        last = act.copy(
                            v_block[p * SEQ:(p + 1) * SEQ, t.odd, b, 2 * half:2 * half + 2, :, p, :], frm)
                last.then_inc(v_done, 1)

            def exponent(t):
                act.wait_ge(shifted, t.index + 1)
                act.activation(expo[:, t.odd, :, :], expo[:, t.odd, :, :], ACT.Exp, scale=HK ** -0.5).then_inc(exp_done, 1)

            def bring_out(t):
                act.wait_ge(mixed, t.index + 1)
                wait(act, up_done, t.index - 1)
                for b in range(PER_TILE):
                    last = act.copy(out_t[:, t.odd, :, :, b, :],
                                    turn_ps[:, b, :].rearrange("p (c h q) -> p c h q", c=PAIRS, h=2))
                last.then_inc(out_t_done, 1)

            def bring_in(t):
                act.wait_ge(turned_in, t.index + 1)
                wait(act, v_filled, 2 * t.index - 2)
                act.copy(xc_t[:, t.odd, :, :], norm_ps[:, 0:2 * P]).then_inc(xc_done, 1)

            def step(t):
                now, one, two, three = t, t.back(1), t.back(2), t.back(3)
                if three.live:
                    bring_prob(three)
                if one.live:
                    bring_k(one, 0)
                if two.live:
                    exponent(two)
                if three.live:
                    bring_out(three)
                if one.live:
                    bring_k(one, 1)
                    bring_v(one, 0)
                    bring_v(one, 1)
                if now.live:
                    bring_in(now)

            over_tiles(act, step, 3)

        @block.vector
        def _(dve):
            dve.memset(q_block[:, :, :, :, :, :], 0.0).then_inc(blocks_zero, 1)
            dve.wait_ge(bias_loaded, BIAS_LOADS * DMA)
            for half in range(2):
                rows = slice(half * HK, half * HK + HK)
                of_half = bv[rows, :].rearrange("d (c p h) -> d c p h", p=2, h=2)[:, :, half, :]
                dve.tensor_copy(bv_wide[rows, :, :].rearrange("d (c h) m -> d c h m", h=2),
                                many(of_half, P, 3)).then_inc(bv_spread, 1)
            dve.wait_ge(bu_summed, 1)
            dve.tensor_tensor(bu[:, :], up_ps[:, 0:D], bu[:, :], ALU.add).then_inc(bu_ready, 1)
            dve.wait_ge(loaded, 5 * DMA)

            def moments(t):
                dve.bn_stats(stats[:, t.odd, :], x[:, t.index, :]).then_inc(stats_done, 1)
                dve.wait_ge(stats_done, t.index + 1)
                wait(dve, xn_done, t.index - 1)
                apart(dve)
                dve.bn_aggr(mean_var[:, t.odd, :], stats[:, t.odd, :]).then_inc(mean_done, 1)
                dve.wait_ge(mean_done, t.index + 1)
                wait(dve, rstd_done, t.index - 1)
                dve.tensor_scalar(var_eps[:, t.odd:t.odd + 1], mean_var[:, t.odd, 1:2], EPS, None,
                                  ALU.add).then_inc(var_done, 1)

            def normalize(t):
                dve.wait_ge(rstd_done, t.index + 1)
                wait(dve, turned_in, t.index - 1)
                dve.tensor_scalar(xn[:, t.odd, :], x[:, t.index, :], mean_var[:, t.odd, 0:1],
                                  rstd[:, t.odd:t.odd + 1], ALU.subtract, ALU.mult).then_inc(xn_done, 1)

            def bring_q(t, half):
                dve.wait_ge(q_filled, 2 * t.index + half + 1)
                if half == 0:
                    wait(dve, scored, t.index - 1)
                for p in range(2):
                    rows = slice(p * HK, (p + 1) * HK)
                    cs = slice(half * 4, half * 4 + 4)
                    last = dve.tensor_tensor(
                        q_block[rows, t.odd, cs, :, p, :],
                        proj_ps[0][rows, :, :].rearrange("p c (b q) -> p c b q", b=PER_TILE),
                        many(bq[rows, cs], P).rearrange("p c (b q) -> p c b q", b=PER_TILE), ALU.add)
                last.then_inc(q_done, 1)

            def shift(t):
                dve.wait_ge(scored, t.index + 1)
                s = score_ps[:, :, :].rearrange("p b (c k) -> p (b c) k", k=SEQ)
                dve.tensor_reduce(top[:, t.odd, :], s, AX.X, ALU.max).then_inc(top_done, 1)
                dve.wait_ge(top_done, t.index + 1)
                wait(dve, prob_done, t.index - 1)
                dve.tensor_tensor(expo[:, t.odd, :, :], s, many(top[:, t.odd, :], SEQ), ALU.subtract).then_inc(shifted, 1)

            def totals(t):
                dve.wait_ge(exp_done, t.index + 1)
                dve.tensor_reduce(total[:, t.odd, :], expo[:, t.odd, :, :], AX.X, ALU.add).then_inc(total_done, 1)
                dve.wait_ge(total_done, t.index + 1)
                dve.reciprocal(share[:, t.odd, :], total[:, t.odd, :]).then_inc(share_done, 1)

            def residual(t):
                dve.wait_ge(up_done, t.index + 1)
                dve.wait_ge(x_biased, t.index + 1)
                dve.tensor_tensor(x[:, t.index, :], up_ps[:, 0:D], x[:, t.index, :], ALU.add).then_inc(x_done, 1)

            def next_moments(t):
                dve.wait_ge(x_done, t.index + 1)
                dve.bn_stats(keep["stats"][:, t.index, :], x[:, t.index, :]).then_inc(next_stats_done, 1)

            def step(t):
                now, one, two, three, four = t, t.back(1), t.back(2), t.back(3), t.back(4)
                if two.live:
                    shift(two)
                if now.live:
                    moments(now)
                if one.live:
                    bring_q(one, 0)
                if two.live:
                    totals(two)
                if now.live:
                    normalize(now)
                if one.live:
                    bring_q(one, 1)
                if three.live:
                    residual(three)
                if four.live:
                    next_moments(four)

            over_tiles(dve, step, 4, before_loop=lambda: dve.wait_ge(x_rest, (X_PARTS - 1) * DMA))

        @block.gpsimd
        def _(pool):
            pool.wait_ge(keep["ident_ready"], keep["ident_count"])
            pool.memset(v_block[:, :, :, :, :, :, :], 0.0).then_inc(blocks_zero, 1)
            pool.wait_ge(bu_ready, 1)

            def scale_root(t):
                pool.wait_ge(var_done, t.index + 1)
                pool.tensor_tensor(rstd[:, t.odd:t.odd + 1], var_eps[:, t.odd:t.odd + 1], eps_pow[:, :],
                                   ALU.pow).then_inc(rstd_done, 1)

            def divide(t):
                pool.wait_ge(share_done, t.index + 1)
                wait(pool, prob_turned, t.index - 1)
                pool.tensor_tensor(prob[:, t.odd, :, :], expo[:, t.odd, :, :], many(share[:, t.odd, :], SEQ),
                                   ALU.mult).then_inc(prob_done, 1)

            def bias_x(t):
                pool.wait_ge(xn_done, t.index + 1)
                pool.tensor_tensor(x[:, t.index, :], x[:, t.index, :], bu[:, :], ALU.add).then_inc(x_biased, 1)

            def step(t):
                now, two = t, t.back(2)
                if now.live:
                    scale_root(now)
                    bias_x(now)
                if two.live:
                    divide(two)

            over_tiles(pool, step, 2)


def start_weight_loads(sp, dram, keep):
    ffn, attn, loaded = keep["ffn"], keep["attn"], keep["weights_loaded"]
    for n, name in enumerate(("Wq", "Wk", "Wv")):
        sp.dma_start(ffn["w_in"][:, n, :], dram[f"L0_ffn_{name}"].rearrange("h e d -> (h e) d")).then_inc(loaded, DMA)
    sp.dma_start(ffn["w_in"][:, 3:, :], dram["L0_ffn_We"].rearrange("x e d -> e x d")).then_inc(loaded, DMA)
    sp.dma_start(ffn["wsw_in"][:, :], dram["L0_ffn_Wsw"]).then_inc(loaded, DMA)
    for name in ("bq", "bk"):
        sp.dma_start(ffn[name][:, :], dram[f"L0_ffn_{name}"].rearrange("h (e o) -> (h e) o", o=1)).then_inc(loaded, DMA)
    sp.dma_start(ffn["bv"][:, :], dram["L0_ffn_bv"].rearrange("h e -> (h e)").partition_broadcast(P)).then_inc(loaded, DMA)
    for name in ("gamma", "beta", "bsw"):
        sp.dma_start(ffn[name][:, :], dram[f"L0_ffn_{name}"].partition_broadcast(P)).then_inc(loaded, DMA)
    sp.dma_start(ffn["be"][0:1, :], dram["L0_ffn_be"].rearrange("(o x) d -> o (x d)", o=1)).then_inc(loaded, DMA)
    for n, name in enumerate(("Wq", "Wk", "Wv", "Wo")):
        sp.dma_start(attn["w_in"][:, n, :], dram[f"L1_xattn_{name}"]).then_inc(loaded, DMA)
    for name in ("bq", "bk"):
        sp.dma_start(attn[name][:, :], dram[f"L1_xattn_{name}"].rearrange("(e o) -> e o", o=1)).then_inc(loaded, DMA)
    for name in ("bv", "bo"):
        sp.dma_start(attn[name][:, :], dram[f"L1_xattn_{name}"].partition_broadcast(P)).then_inc(loaded, DMA)


def start_later_loads(sp, dram, keep):
    mask_rows = dram["mask_Bx1xSxS2_ik1"].rearrange("b o q k -> q (b o) k")
    for h in range(2):
        sp.dma_start(keep["mask"][h * SEQ:(h + 1) * SEQ, :, :].rearrange("q t (b k) -> q (t b) k", b=PER_TILE),
                     mask_rows).then_inc(keep["mask_loaded"], DMA)
    for n in range(EXPERTS):
        sp.dma_start(keep["w_in"][:, n, :], dram["L1_ffn_W_in"][n]).then_inc(keep["w_loaded"], DMA)
        sp.dma_start(keep["w_out"][:, n, :, :],
                     dram["L1_ffn_W_out"][n].rearrange("(c m) d -> m c d", m=P)).then_inc(keep["w_loaded"], DMA)
    sp.dma_start(keep["b_in"][:, :],
                 dram["L1_ffn_b_in"].rearrange("x (c m) -> (x c) m", m=P)).then_inc(keep["w_loaded"], DMA)
    sp.dma_start(keep["b_out"][:, :, :].rearrange("p x d -> p (x d)"),
                 dram["L1_ffn_b_out"].rearrange("x d -> (x d)").partition_broadcast(P)).then_inc(keep["w_loaded"], DMA)


def routed_attention(nc, dram, keep):
    ctx = ExitStack()
    with ctx:
        m = Memory(nc, ctx, "rout")
        x, ident, eps_pow = keep["x"], keep["ident"], keep["eps_pow"]
        w_in, wsw_in, bq, bk, bv, gamma, beta, bsw, be = (
            keep["ffn"][n] for n in ("w_in", "wsw_in", "bq", "bk", "bv", "gamma", "beta", "bsw", "be"))
        w_t = m.sb("w_t", [P, 3 + EXPERTS, D])
        wsw_t = m.sb("wsw_t", [P, EXPERTS])
        be_parts = m.sb("be_parts", [96, EXPERTS * D], BF16)
        be_ones = m.sb("be_ones", [96, P], BF16)
        head_of = m.sb("head_of", [P, HEADS])
        causal = m.sb("causal", [P, SEQ])
        upto = m.sb("upto", [P, P], BF16)
        ones = m.sb("ones", [P, P], BF16)
        number = m.sb("number", [P, EXPERTS])
        seen = m.sb("seen", [P, EXPERTS], BF16)

        stats = keep["stats"]
        mean_var = m.sb("mean_var", [P, TILES, 2])
        var_eps = m.sb("var_eps", [P, TILES])
        rstd = m.sb("rstd", [P, TILES])
        e_now = m.sb("e_now", [P, 2, D])
        e_all = m.sb("e_all", [P, TILES, D])
        e_t = m.sb("e_t", [P, 2, P])
        qk = m.sb("qk", [P, 2, 2, P])
        q_block = m.sb("q_block", [P, 2, PER_TILE, HEADS, SEQ])
        v_block = m.sb("v_block", [P, 2, PER_TILE, PAIRS, 2, VCOL])
        score = m.sb("score", [P, 2, HEADS, SEQ])
        top = m.sb("top", [P, 2, HEADS])
        expo = m.sb("expo", [P, 2, HEADS, SEQ])
        prob_t = m.sb("prob_t", [P, 2, PER_TILE, PAIRS, P])
        share = m.sb("share", [P, 2, PER_TILE, CHUNKS])
        hid_raw = m.sb("hid_raw", [P, 2, D])
        hid = m.sb("hid", [P, 2, D])
        hid_t = m.sb("hid_t", [P, 2, P])
        logit = m.sb("logit", [P, EXPERTS])
        best = m.sb("best", [P, 8])
        place = m.sb("place", [P, 8], U32)
        less_best = m.sb("less_best", [P, 1])
        e_logit = m.sb("e_logit", [P, EXPERTS])
        e_sum = m.sb("e_sum", [P, 1])
        route_prob = m.sb("route_prob", [P, 1])
        chosen = m.sb("chosen", [P, EXPERTS])
        chosen_b = m.sb("chosen_b", [P, EXPERTS], BF16)
        order = m.sb("order", [P, EXPERTS])
        position = m.sb("position", [P, 1])
        kept = m.sb("kept", [P, 1])
        gate = m.sb("gate", [P, 1])
        pass_on = m.sb("pass_on", [P, 1])
        weight = m.sb("weight", [P, EXPERTS])
        parts = m.sb("parts", [P, EXPERTS, D])
        y = m.sb("y", [P, D])
        z = m.sb("z", [P, D])
        z_pre = m.sb("z_pre", [P, D])
        z_stats = m.sb("z_stats", [P, 6])
        z_mean_var = m.sb("z_mean_var", [P, 2])
        z_var_eps = m.sb("z_var_eps", [P, 1])
        z_rstd = m.sb("z_rstd", [P, 1])
        zn = m.sb("zn", [P, D])
        zg = m.sb("zg", [P, D])
        xb = m.sb("xb", [P, D])

        small_ps = m.ps("small", [P, 512])
        qkv_ps = m.ps("qkv", [P, 4, P])
        score_ps = m.ps("score", [P, PER_TILE, CHUNKS * SEQ])
        turn_ps = m.ps("turn", [P, PER_TILE, 512])
        exp_ps = m.ps("exp", [P, EXPERTS, D])

        masks_filled = m.sem("masks_filled")
        masks_done = m.sem("masks_done")
        w_turned = m.sem("w_turned")
        w_done = m.sem("w_done")
        mean_done, var_done, next_stats_done = m.sem("mean_done"), m.sem("var_done"), m.sem("next_stats_done")
        rstd_done, e_done, e_kept = m.sem("rstd_done"), m.sem("e_done"), m.sem("e_kept")
        e_turned, e_t_done = m.sem("e_turned"), m.sem("e_t_done")
        qk_filled, v_filled = m.sem("qk_filled"), m.sem("v_filled")
        qk_done, v_done = m.sem("qk_done"), m.sem("v_done")
        q_block_done, scored, masked = m.sem("q_block_done"), m.sem("scored"), m.sem("masked")
        top_done, shifted, exp_done = m.sem("top_done"), m.sem("shifted"), m.sem("exp_done")
        prob_turned, prob_t_done, mixed = m.sem("prob_turned"), m.sem("prob_t_done"), m.sem("mixed")
        share_done, hid_raw_done, hid_done = m.sem("share_done"), m.sem("hid_raw_done"), m.sem("hid_done")
        hid_turned, hid_t_done, routed = m.sem("hid_turned"), m.sem("hid_t_done"), m.sem("routed")
        experts_done, parts_done = m.sem("experts_done"), m.sem("parts_done")
        logit_done, best_done, place_done = m.sem("logit_done"), m.sem("best_done"), m.sem("place_done")
        less_done, sum_done, chosen_done = m.sem("less_done"), m.sem("sum_done"), m.sem("chosen_done")
        counted, order_done, position_done = m.sem("counted"), m.sem("order_done"), m.sem("position_done")
        kept_done, route_done, gate_done = m.sem("kept_done"), m.sem("route_done"), m.sem("gate_done")
        pick_done, pass_done = m.sem("pick_done"), m.sem("pass_done")
        weight_done, seen_done = m.sem("weight_done"), m.sem("seen_done")
        y_done, z_pre_done, z_done = m.sem("y_done"), m.sem("z_pre_done"), m.sem("z_done")
        z_stats_done, z_mean_done, z_var_done = m.sem("z_stats_done"), m.sem("z_mean_done"), m.sem("z_var_done")
        z_rstd_done, zn_done, zg_done = m.sem("z_rstd_done"), m.sem("zn_done"), m.sem("zg_done")
        xb_done, x_done = m.sem("xb_done"), m.sem("x_done")
        be_step, zeroed, v_block_ready = m.sem("be_step"), m.sem("zeroed"), m.sem("v_block_ready")

        block = ctx.enter_context(nc.Block())

        @block.sync
        def _(sp):
            start_later_loads(sp, dram, keep)

        @block.tensor
        def _(pe):
            pe.wait_ge(keep["weights_loaded"], LAYER_LOADS * DMA)
            for n in range(3):
                pe.transpose(small_ps[:, n * P:(n + 1) * P], w_in[:, n, :], ident[:, :])
            pe.transpose(small_ps[:, 3 * P:3 * P + EXPERTS], wsw_in[:, :], ident[0:EXPERTS, 0:EXPERTS]).then_inc(w_turned, 1)
            for n in range(EXPERTS):
                last = pe.transpose(exp_ps[:, n, :], w_in[:, 3 + n, :], ident[:, :])
            last.then_inc(w_turned, 1)
            pe.wait_ge(w_done, 4)
            pe.wait_ge(masks_done, 6)
            pe.wait_ge(v_block_ready, 1)

            def scores(t):
                pe.wait_ge(q_block_done, 2 * t.index + 2)
                wait(pe, masked, t.index)
                for b in range(PER_TILE):
                    for c in range(CHUNKS):
                        for h in range(2):
                            last = pe.matmul(score_ps[h * SEQ:(h + 1) * SEQ, b, c * SEQ:(c + 1) * SEQ],
                                             q_block[:, t.odd, b, 2 * c + h, :],
                                             qk[:, t.odd, 1, b * SEQ:(b + 1) * SEQ], start=True, stop=True)
                last.then_inc(scored, 1)

            def turn_prob(t):
                pe.wait_ge(exp_done, t.index + 1)
                wait(pe, hid_raw_done, t.index)
                for b in range(PER_TILE):
                    for c in range(PAIRS):
                        h = b * CHUNKS + 2 * c
                        last = pe.transpose(turn_ps[:, b, c * P:(c + 1) * P], expo[:, t.odd, h:h + 2, :], ident[:, :])
                last.then_inc(prob_turned, 1)

            def mix(t):
                pe.wait_ge(prob_t_done, t.index + 1)
                pe.wait_ge(v_done, t.index + 1)
                for b in range(PER_TILE):
                    for c in range(PAIRS):
                        at = (b * PAIRS + c) * 2 * VCOL
                        last = pe.matmul(turn_ps[:, 0, at:at + 2 * VCOL], prob_t[:, t.odd, b, c, :],
                                         v_block[:, t.odd, b, c, :, :], start=True, stop=True)
                last.then_inc(mixed, 1)

            def turn_hidden(t):
                pe.wait_ge(hid_done, t.index + 1)
                wait(pe, order_done, t.index)
                at = t.index + 4
                pe.wait_ge(e_t_done, min(at, TILES) if isinstance(at, int) else at)
                pe.transpose(small_ps[:, P:2 * P], hid[:, t.odd, :], ident[:, :]).then_inc(hid_turned, 1)

            def experts(t, half):
                part = slice(half * 4, half * 4 + 4)
                if half == 0:
                    wait(pe, be_step, 7) if isinstance(t.group, int) else None
                    pe.wait_ge(hid_t_done, t.index + 1)
                    at = t.index + 5
                    pe.wait_ge(e_t_done, min(at, TILES) if isinstance(at, int) else at)
                    pe.matmul(small_ps[:, 256:256 + EXPERTS], hid_t[:, t.odd, :], wsw_t[:, :], start=True,
                              stop=True).then_inc(routed, 1)
                    wait(pe, parts_done, t.index)
                pe.matmul(exp_ps[:, part, :], hid_t[:, t.odd, :], w_t[:, 3 + half * 4:7 + half * 4, :], start=True,
                          stop=False)
                pe.matmul(exp_ps[:, part, :], be_ones[:, :], be_parts[:, half * 512:half * 512 + 512],
                          start=False, stop=True).then_inc(experts_done, 1)

            def count(t):
                pe.wait_ge(chosen_done, t.index + 1)
                wait(pe, seen_done, t.index)
                pe.matmul(small_ps[:, 264:264 + EXPERTS], upto[:, :], chosen_b[:, :], start=True, stop=False)
                pe.matmul(small_ps[:, 264:264 + EXPERTS], ones[:, :], seen[:, :], start=False, stop=True).then_inc(counted, 1)

            def turn_in(t):
                pe.wait_ge(e_done, t.index + 1)
                wait(pe, e_t_done, t.index)
                wait(pe, order_done, t.index - 4)
                pe.transpose(small_ps[:, 0:P], e_now[:, t.odd, :], ident[:, :]).then_inc(e_turned, 1)

            def project_qk(t):
                pe.wait_ge(e_t_done, t.index + 1)
                wait(pe, v_done, t.index)
                pe.matmul(qkv_ps[:, 0, :], w_t[:, 0, :], e_t[:, t.odd, :], start=True, stop=True)
                pe.matmul(qkv_ps[:, 1, :], w_t[:, 1, :], e_t[:, t.odd, :], start=True, stop=True).then_inc(qk_filled, 1)

            def project_v(t):
                pe.wait_ge(qk_done, t.index + 1)
                pe.matmul(qkv_ps[:, 2, :], e_t[:, t.odd, :], w_t[:, 2, :], start=True, stop=True).then_inc(v_filled, 1)

            def step(t):
                now, one, two, three, four = t, t.back(1), t.back(2), t.back(3), t.back(4)
                if one.live:
                    project_qk(one)
                if two.live:
                    scores(two)
                if now.live:
                    turn_in(now)
                if four.live:
                    turn_hidden(four)
                if three.live:
                    turn_prob(three)
                if one.live:
                    project_v(one)
                if four.live:
                    experts(four, 0)
                if three.live:
                    mix(three)
                if four.live:
                    count(four)
                    experts(four, 1)

            over_tiles(pe, step, 4)

        @block.scalar
        def _(act):
            act.wait_ge(w_turned, 1)
            act.copy(w_t[:, 0:3, :], small_ps[:, 0:3 * P]).then_inc(w_done, 1)
            act.copy(wsw_t[:, :], small_ps[:, 3 * P:3 * P + EXPERTS]).then_inc(w_done, 1)
            act.wait_ge(w_turned, 2)
            for half in range(2):
                part = slice(half * 4, half * 4 + 4)
                act.copy(w_t[:, 3 + half * 4:7 + half * 4, :], exp_ps[:, part, :]).then_inc(w_done, 1)
            act.wait_ge(keep["weights_loaded"], LAYER_LOADS * DMA)
            act.wait_ge(v_block_ready, 1)

            def bring_hidden(t):
                act.wait_ge(hid_turned, t.index + 1)
                wait(act, experts_done, 2 * t.index - 2)
                act.copy(hid_t[:, t.odd, :], small_ps[:, P:2 * P]).then_inc(hid_t_done, 1)

            def bring_prob(t):
                act.wait_ge(prob_turned, t.index + 1)
                wait(act, mixed, t.index - 1)
                act.copy(prob_t[:, t.odd, :, :, :], turn_ps[:, :, :]).then_inc(prob_t_done, 1)

            def route_exp(t):
                act.wait_ge(less_done, t.index + 1)
                wait(act, route_done, t.index)
                act.activation(e_logit[:, :], logit[:, :], ACT.Exp, bias=less_best[:, :],
                               accum_out=e_sum[:, :]).then_inc(sum_done, 1)

            def exponent(t):
                act.wait_ge(shifted, t.index + 1)
                act.activation(expo[:, t.odd, :, :], expo[:, t.odd, :, :], ACT.Exp, scale=D ** -0.5).then_inc(exp_done, 1)

            def weigh(t):
                act.wait_ge(weight_done, t.index + 1)
                act.wait_ge(experts_done, 2 * t.index + 2)
                wait(act, y_done, t.index)
                for n in range(EXPERTS):
                    last = act.activation(parts[:, n, :], exp_ps[:, n, :], ACT.Copy, scale=weight[:, n:n + 1])
                last.then_inc(parts_done, 1)

            def bring_in(t):
                act.wait_ge(e_turned, t.index + 1)
                wait(act, v_filled, t.index - 1)
                act.copy(e_t[:, t.odd, :], small_ps[:, 0:P]).then_inc(e_t_done, 1)
                act.copy(e_all[:, t.index, :], e_now[:, t.odd, :]).then_inc(e_kept, 1)

            def bring_qk(t):
                act.wait_ge(qk_filled, t.index + 1)
                wait(act, scored, t.index - 1)
                act.activation(qk[:, t.odd, 0, :], qkv_ps[:, 0, :], ACT.Identity, bias=bq[:, :])
                act.activation(qk[:, t.odd, 1, :], qkv_ps[:, 1, :], ACT.Identity, bias=bk[:, :]).then_inc(qk_done, 1)

            def bring_v(t):
                act.wait_ge(v_filled, t.index + 1)
                wait(act, mixed, t.index - 1)
                for b in range(PER_TILE):
                    for p in range(2):
                        frm = qkv_ps[b * SEQ:(b + 1) * SEQ, 2, :].rearrange("k (c p m) -> k c p m", p=2, m=2 * HD)[:, :, p, :]
                        last = act.copy(v_block[p * SEQ:(p + 1) * SEQ, t.odd, b, :, p, 0:2 * HD], frm)
                last.then_inc(v_done, 1)

            def step(t):
                now, one, three, four, five = t, t.back(1), t.back(3), t.back(4), t.back(5)
                if one.live:
                    bring_qk(one)
                if three.live:
                    exponent(three)
                if five.live:
                    weigh(five)
                if four.live:
                    bring_hidden(four)
                if now.live:
                    bring_in(now)
                if three.live:
                    bring_prob(three)
                if four.live:
                    route_exp(four)
                if one.live:
                    bring_v(one)

            over_tiles(act, step, 5)

        @block.vector
        def _(dve):
            for t in range(TILES):
                last = dve.bn_aggr(mean_var[:, t, :], stats[:, t, :])
            last.then_inc(mean_done, 1)
            dve.wait_ge(mean_done, 1)
            dve.tensor_scalar(var_eps[:, :], mean_var[:, :, 1], EPS, None, ALU.add).then_inc(var_done, 1)
            dve.wait_ge(keep["weights_loaded"], LAYER_LOADS * DMA)
            dve.memset(v_block[:, :, :, :, :, :], 0.0).then_inc(zeroed, 1)
            dve.memset(seen[:, :], 0.0).then_inc(zeroed, 1)
            dve.wait_ge(zeroed, 2)
            for p in range(2):
                last = dve.memset(v_block[p * SEQ:(p + 1) * SEQ, :, :, :, p, 2 * HD:VCOL], 1.0)
            last.then_inc(v_block_ready, 1)

            def split_expert_bias(step):
                row, nxt = slice(32 * step, 32 * step + 1), slice(32 * step + 32, 32 * step + 33)
                if step == 0:
                    dve.memset(be_parts[:, :], 0.0).then_inc(be_step, 1)
                    dve.memset(be_ones[:, :], 1.0).then_inc(be_step, 1)
                    dve.wait_ge(be_step, 2)
                else:
                    dve.wait_ge(be_step, 2 + 2 * step)
                dve.tensor_copy(be_parts[row, :], be[row, :]).then_inc(be_step, 1)
                if step < 2:
                    dve.wait_ge(be_step, 3 + 2 * step)
                    dve.tensor_tensor(be[nxt, :], be[row, :], be_parts[row, :], ALU.subtract).then_inc(be_step, 1)

            def normalize(t):
                dve.wait_ge(rstd_done, 1 if isinstance(t.group, int) and t.index < FIRST_ROOTS else 2)
                wait(dve, e_turned, t.index - 1)
                wait(dve, e_kept, t.index - 1)
                dve.tensor_scalar(e_now[:, t.odd, :], x[:, t.index, :], mean_var[:, t.index, 0:1],
                                  scalar_at(rstd, t), ALU.subtract, ALU.mult).then_inc(e_done, 1)

            def mask(t):
                dve.wait_ge(scored, t.index + 1)
                wait(dve, shifted, t.index - 1)
                s = score_ps[:, :, :].rearrange("p b (c k) -> p (b c) k", k=SEQ)
                dve.tensor_tensor(score[:, t.odd, :, :], s, many(causal[:, :], HEADS, 1), ALU.mult).then_inc(masked, 1)
                dve.wait_ge(masked, t.index + 1)
                dve.tensor_reduce(top[:, t.odd, :], score[:, t.odd, :, :], AX.X, ALU.max).then_inc(top_done, 1)

            def route(t):
                dve.wait_ge(routed, t.index + 1)
                wait(dve, sum_done, t.index)
                dve.tensor_tensor(logit[:, :], small_ps[:, 256:256 + EXPERTS], bsw[:, :], ALU.add).then_inc(logit_done, 1)
                dve.wait_ge(logit_done, t.index + 1)
                apart(dve)
                dve.max(best[:, :], logit[:, :]).then_inc(best_done, 1)
                dve.wait_ge(best_done, t.index + 1)
                dve.tensor_scalar(less_best[:, :], best[:, 0:1], -1.0, None, ALU.mult).then_inc(less_done, 1)
                apart(dve)
                dve.max_index(place[:, :], best[:, :], logit[:, :]).then_inc(place_done, 1)
                dve.wait_ge(place_done, t.index + 1)
                wait(dve, weight_done, t.index)
                dve.tensor_tensor(chosen[:, :], number[:, :], place[:, 0:1].to_broadcast([P, EXPERTS]),
                                  ALU.is_equal).then_inc(pick_done, 1)
                dve.wait_ge(pick_done, t.index + 1)
                wait(dve, seen_done, t.index)
                dve.tensor_copy(chosen_b[:, :], chosen[:, :]).then_inc(chosen_done, 1)

            def admit(t):
                dve.wait_ge(counted, t.index + 1)
                dve.tensor_tensor(order[:, :], small_ps[:, 264:264 + EXPERTS], chosen[:, :], ALU.mult).then_inc(order_done, 1)
                dve.tensor_tensor(seen[:, :], seen[:, :], chosen_b[:, :], ALU.add).then_inc(seen_done, 1)
                dve.wait_ge(order_done, t.index + 1)
                dve.tensor_reduce(position[:, :], order[:, :], AX.X, ALU.add).then_inc(position_done, 1)
                dve.wait_ge(sum_done, t.index + 1)
                dve.reciprocal(route_prob[:, :], e_sum[:, :]).then_inc(route_done, 1)
                dve.wait_ge(position_done, t.index + 1)
                dve.tensor_scalar(kept[:, :], position[:, :], float(CAPACITY), None, ALU.is_le).then_inc(kept_done, 1)
                dve.wait_ge(kept_done, t.index + 1)
                dve.wait_ge(route_done, t.index + 1)
                dve.tensor_tensor(gate[:, :], kept[:, :], route_prob[:, :], ALU.mult).then_inc(gate_done, 1)
                dve.wait_ge(gate_done, t.index + 1)
                dve.tensor_tensor(pass_on[:, :], route_prob[:, :], gate[:, :], ALU.subtract).then_inc(pass_done, 1)
                wait(dve, parts_done, t.index)
                dve.tensor_scalar(weight[:, :], chosen[:, :], gate[:, :], None, ALU.mult).then_inc(weight_done, 1)

            def take_hidden(t):
                dve.wait_ge(mixed, t.index + 1)
                sums = turn_ps[:, 0, 0:PER_TILE * PAIRS * 2 * VCOL].rearrange("p (b n m) -> p b n m", b=PER_TILE, m=VCOL)
                dve.reciprocal(share[:, t.odd, :, :], sums[:, :, :, 2 * HD:VCOL].rearrange("p b n o -> p b (n o)")).then_inc(share_done, 1)
                dve.wait_ge(share_done, t.index + 1)
                wait(dve, hid_done, t.index - 1)
                for b in range(PER_TILE):
                    for h in range(2):
                        rows = slice(h * SEQ, (h + 1) * SEQ)
                        to = hid_raw[b * SEQ:(b + 1) * SEQ, t.odd, :].rearrange("q (n h d) -> q n h d", h=2, d=HD)[:, :, h, :]
                        last = dve.tensor_tensor(to, sums[rows, b, :, h * HD:(h + 1) * HD],
                                                 many(share[rows, t.odd, b, :], HD), ALU.mult)
                last.then_inc(hid_raw_done, 1)

            def finish(t):
                dve.wait_ge(parts_done, t.index + 1)
                dve.tensor_reduce(y[:, :], parts[:, :, :].rearrange("p x f -> p f x"), AX.X, ALU.add).then_inc(y_done, 1)
                dve.wait_ge(y_done, t.index + 1)
                dve.wait_ge(pass_done, t.index + 1)
                dve.scalar_tensor_tensor(z_pre[:, :], hid[:, t.odd, :], pass_on[:, 0:1], y[:, :], ALU.mult,
                                         ALU.add).then_inc(z_pre_done, 1)
                dve.wait_ge(z_pre_done, t.index + 1)
                dve.wait_ge(e_kept, t.index + 1)
                wait(dve, zn_done, t.index)
                dve.tensor_tensor(z[:, :], z_pre[:, :], e_all[:, t.index, :], ALU.add).then_inc(z_done, 1)
                dve.wait_ge(z_done, t.index + 1)
                dve.bn_stats(z_stats[:, :], z[:, :]).then_inc(z_stats_done, 1)
                dve.wait_ge(z_stats_done, t.index + 1)
                apart(dve)
                dve.bn_aggr(z_mean_var[:, :], z_stats[:, :]).then_inc(z_mean_done, 1)
                dve.wait_ge(z_mean_done, t.index + 1)
                dve.tensor_scalar(z_var_eps[:, :], z_mean_var[:, 1:2], EPS, None, ALU.add).then_inc(z_var_done, 1)

            def next_moments(t):
                dve.wait_ge(x_done, t.index + 1)
                dve.bn_stats(stats[:, t.index, :], x[:, t.index, :]).then_inc(next_stats_done, 1)

            def finish_scale(t):
                dve.wait_ge(z_rstd_done, t.index + 1)
                wait(dve, zg_done, t.index)
                dve.tensor_scalar(zn[:, :], z[:, :], z_mean_var[:, 0:1], z_rstd[:, 0:1], ALU.subtract,
                                  ALU.mult).then_inc(zn_done, 1)

            def step(t):
                now, two, four, five, six, seven = t, t.back(2), t.back(4), t.back(5), t.back(6), t.back(7)
                if five.live:
                    admit(five)
                if four.live:
                    take_hidden(four)
                if six.live:
                    finish_scale(six)
                if now.live:
                    normalize(now)
                if seven.live:
                    next_moments(seven)
                if two.live:
                    mask(two)
                if four.live:
                    route(four)
                if five.live:
                    finish(five)
                if isinstance(t.group, int) and t.index < 3:
                    split_expert_bias(t.index)

            over_tiles(dve, step, 7)

        @block.gpsimd
        def _(pool):
            pool.memset(head_of[:, :], 1.0).then_inc(masks_filled, 1)
            pool.memset(causal[:, :], 1.0).then_inc(masks_filled, 1)
            pool.memset(upto[:, :], 1.0).then_inc(masks_filled, 1)
            pool.memset(ones[:, :], 1.0).then_inc(masks_done, 1)
            pool.iota(number[:, :], pattern=[[1, EXPERTS]], base=0, channel_multiplier=0,
                      allow_small_or_imprecise_dtypes=True).then_inc(masks_done, 1)
            pool.wait_ge(masks_filled, 3)
            pool.affine_select(out=head_of[:, :], in_=head_of[:, :], compare_op=ALU.is_ge, fill=0.0, base=0,
                               pattern=[[-HD, HEADS]], channel_multiplier=1).then_inc(masks_filled, 1)
            pool.wait_ge(masks_filled, 4)
            pool.affine_select(out=head_of[:, :], in_=head_of[:, :], compare_op=ALU.is_ge, fill=0.0, base=HD - 1,
                               pattern=[[HD, HEADS]], channel_multiplier=-1).then_inc(masks_done, 1)
            for h in range(2):
                pool.wait_ge(masks_done, 3 + h)
                rows = causal[h * SEQ:(h + 1) * SEQ, :]
                pool.affine_select(out=rows, in_=rows, compare_op=ALU.is_ge, fill=0.0, base=0,
                                   pattern=[[-1, SEQ]], channel_multiplier=1).then_inc(masks_done, 1)
            pool.wait_ge(masks_done, 5)
            pool.affine_select(out=upto[:, :], in_=upto[:, :], compare_op=ALU.is_ge, fill=0.0, base=0,
                               pattern=[[1, P]], channel_multiplier=-1).then_inc(masks_done, 1)
            pool.wait_ge(masks_done, 6)
            pool.wait_ge(keep["weights_loaded"], LAYER_LOADS * DMA)
            pool.wait_ge(var_done, 1)

            def scale_roots(first, end):
                pool.tensor_tensor(rstd[:, first:end], var_eps[:, first:end],
                                   eps_pow[:, 0:1].to_broadcast([P, end - first]), ALU.pow).then_inc(rstd_done, 1)

            scale_roots(0, FIRST_ROOTS)

            def shift(t):
                pool.wait_ge(top_done, t.index + 1)
                wait(pool, prob_turned, t.index - 1)
                pool.tensor_tensor(expo[:, t.odd, :, :], score[:, t.odd, :, :], many(top[:, t.odd, :], SEQ),
                                   ALU.subtract).then_inc(shifted, 1)

            def spread_q(t, b):
                pool.wait_ge(qk_done, t.index + 1)
                wait(pool, scored, t.index - 1)
                pool.tensor_tensor(q_block[:, t.odd, b, :, :], many(qk[:, t.odd, 0, b * SEQ:(b + 1) * SEQ], HEADS, 1),
                                   many(head_of[:, :], SEQ), ALU.mult).then_inc(q_block_done, 1)

            def bias_hidden(t):
                pool.wait_ge(hid_raw_done, t.index + 1)
                wait(pool, z_pre_done, t.index - 1)
                wait(pool, hid_turned, t.index - 1)
                pool.tensor_tensor(hid[:, t.odd, :], hid_raw[:, t.odd, :], bv[:, :], ALU.add).then_inc(hid_done, 1)

            def bias_x(t):
                wait(pool, x_done, t.index)
                pool.tensor_tensor(xb[:, :], x[:, t.index, :], beta[:, :], ALU.add).then_inc(xb_done, 1)

            def scale_z_root(t):
                pool.wait_ge(z_var_done, t.index + 1)
                pool.tensor_tensor(z_rstd[:, :], z_var_eps[:, :], eps_pow[:, :], ALU.pow).then_inc(z_rstd_done, 1)

            def finish(t):
                pool.wait_ge(zn_done, t.index + 1)
                pool.tensor_tensor(zg[:, :], zn[:, :], gamma[:, :], ALU.mult).then_inc(zg_done, 1)
                pool.wait_ge(zg_done, t.index + 1)
                pool.wait_ge(xb_done, t.index + 1)
                apart(pool)
                pool.tensor_tensor(x[:, t.index, :], xb[:, :], zg[:, :], ALU.add).then_inc(x_done, 1)

            def step(t):
                one, two, four, five, six = t.back(1), t.back(2), t.back(4), t.back(5), t.back(6)
                if four.live:
                    bias_hidden(four)
                if one.live:
                    spread_q(one, 0)
                    spread_q(one, 1)
                if two.live:
                    shift(two)
                if six.live:
                    finish(six)
                if five.live:
                    bias_x(five)
                    scale_z_root(five)
                if isinstance(t.group, int) and t.index == 2:
                    scale_roots(FIRST_ROOTS, TILES)

            over_tiles(pool, step, 6)


def masked_attention(nc, dram, keep):
    ctx = ExitStack()
    with ctx:
        m = Memory(nc, ctx, "mask")
        x, ident, eps_pow = keep["x"], keep["ident"], keep["eps_pow"]
        w_in, bq, bk, bv, bo = (keep["attn"][n] for n in ("w_in", "bq", "bk", "bv", "bo"))
        w_t = m.sb("w_t", [P, 4, D])
        head_of = m.sb("head_of", [P, HEADS])
        ctx_in = m.sb("ctx_in", [P, 2, D])
        valid = m.sb("valid", [P, 2, PER_TILE, SEQ])

        stats = keep["stats"]
        mean_var = m.sb("mean_var", [P, TILES, 2])
        var_eps = m.sb("var_eps", [P, TILES])
        rstd = m.sb("rstd", [P, TILES])
        xn = m.sb("xn", [P, 2, D])
        xc_t = m.sb("xc_t", [P, 2, 2, P])
        qk = m.sb("qk", [P, 2, 2, P])
        q_block = m.sb("q_block", [P, 2, PER_TILE, HEADS, SEQ])
        v_block = m.sb("v_block", [P, 2, PER_TILE, PAIRS, 2, VCOL])
        score = m.sb("score", [P, 2, HEADS, SEQ])
        top = m.sb("top", [P, 2, HEADS])
        expo = m.sb("expo", [P, 2, HEADS, SEQ])
        prob_t = m.sb("prob_t", [P, 2, PER_TILE, PAIRS, P])
        share = m.sb("share", [P, 2, PER_TILE, CHUNKS])
        out_raw = m.sb("out_raw", [P, 2, D])
        out = m.sb("out", [P, 2, D])
        out_t = m.sb("out_t", [P, 2, P])

        turn_in_ps = m.ps("turn_in", [P, 4, P])
        qk_ps = m.ps("qk", [P, 4, P])
        score_ps = m.ps("score", [P, PER_TILE, CHUNKS * SEQ])
        turn_ps = m.ps("turn", [P, PER_TILE, 512])
        v_ps = m.ps("v", [P, 512])
        mix_ps = m.ps("mix", [P, 512])

        zeroed = m.sem("zeroed")
        masks_filled, masks_done = m.sem("masks_filled"), m.sem("masks_done")
        ctx_loaded = [m.sem(f"ctx_loaded{i}") for i in range(2)]
        w_turned, w_done, valid_done = m.sem("w_turned"), m.sem("w_done"), m.sem("valid_done")
        next_stats_done = m.sem("next_stats_done")
        mean_done, var_done = m.sem("mean_done"), m.sem("var_done")
        rstd_done, xn_done, x_biased = m.sem("rstd_done"), m.sem("xn_done"), m.sem("x_biased")
        turned_in, xc_done = m.sem("turned_in"), m.sem("xc_done")
        qk_filled, v_filled = m.sem("qk_filled"), m.sem("v_filled")
        qk_done, v_done = m.sem("qk_done"), m.sem("v_done")
        scored, masked = m.sem("scored"), m.sem("masked")
        q_block_done = [m.sem(f"q_block_done{i}") for i in range(PER_TILE)]
        top_done, shifted, exp_done = m.sem("top_done"), m.sem("shifted"), m.sem("exp_done")
        prob_turned, prob_t_done, mixed = m.sem("prob_turned"), m.sem("prob_t_done"), m.sem("mixed")
        share_done, out_raw_done, out_done = m.sem("share_done"), m.sem("out_raw_done"), m.sem("out_done")
        out_turned, out_t_done, up_done, x_done = m.sem("out_turned"), m.sem("out_t_done"), m.sem("up_done"), m.sem("x_done")

        ctx_tiles = dram["ctx_1024"].rearrange("b s d -> (b s) d").rearrange("(t p) d -> t p d", p=P)
        block = ctx.enter_context(nc.Block())

        @block.sync
        def _(sp):
            sp.dma_start(ctx_in[:, 0, :], ctx_tiles[0]).then_inc(ctx_loaded[0], DMA)
            sp.dma_start(ctx_in[:, 1, :], ctx_tiles[1]).then_inc(ctx_loaded[1], DMA)

            def step(t):
                u = t.back(-2)
                sp.wait_ge(turned_in, t.index + 1)
                sp.dma_start(ctx_in[:, u.odd, :], ctx_tiles[u.index]).then_inc(ctx_loaded[u.odd], DMA)

            with sp.Fori(0, TILES // 2 - 1) as group:
                step(Tile(group, 0))
                step(Tile(group, 1))

        @block.tensor
        def _(pe):
            for n in range(4):
                last = pe.transpose(turn_in_ps[:, n, :], w_in[:, n, :], ident[:, :])
            last.then_inc(w_turned, 1)
            pe.wait_ge(w_done, 1)
            pe.wait_ge(zeroed, 3)

            def scores(t):
                for b in range(PER_TILE):
                    pe.wait_ge(q_block_done[b], t.index + 1)
                wait(pe, masked, 2 * t.index)
                for b in range(PER_TILE):
                    for c in range(CHUNKS):
                        for h in range(2):
                            last = pe.matmul(score_ps[h * SEQ:(h + 1) * SEQ, b, c * SEQ:(c + 1) * SEQ],
                                             q_block[:, t.odd, b, 2 * c + h, :],
                                             qk[:, t.odd, 1, b * SEQ:(b + 1) * SEQ], start=True, stop=True)
                last.then_inc(scored, 1)

            def turn_prob(t):
                pe.wait_ge(exp_done, t.index + 1)
                wait(pe, prob_t_done, t.index)
                for b in range(PER_TILE):
                    for c in range(PAIRS):
                        h = b * CHUNKS + 2 * c
                        last = pe.transpose(turn_ps[:, b, c * P:(c + 1) * P], expo[:, t.odd, h:h + 2, :], ident[:, :])
                last.then_inc(prob_turned, 1)

            def mix(t):
                pe.wait_ge(prob_t_done, t.index + 1)
                pe.wait_ge(v_done, t.index + 1)
                wait(pe, out_raw_done, t.index)
                for b in range(PER_TILE):
                    for c in range(PAIRS):
                        at = (b * PAIRS + c) * 2 * VCOL
                        last = pe.matmul(mix_ps[:, at:at + 2 * VCOL], prob_t[:, t.odd, b, c, :],
                                         v_block[:, t.odd, b, c, :, :], start=True, stop=True)
                last.then_inc(mixed, 1)

            def turn_out(t):
                pe.wait_ge(out_done, t.index + 1)
                wait(pe, x_done, t.index)
                pe.transpose(turn_in_ps[:, 2, :], out[:, t.odd, :], ident[:, :]).then_inc(out_turned, 1)

            def up(t):
                pe.wait_ge(out_t_done, t.index + 1)
                at = t.index + 6
                pe.wait_ge(xc_done, min(at, TILES) if isinstance(at, int) else at)
                pe.matmul(turn_in_ps[:, 3, :], out_t[:, t.odd, :], w_t[:, 3, :], start=True, stop=True).then_inc(up_done, 1)

            def turn_in(t):
                pe.wait_ge(xn_done, t.index + 1)
                pe.wait_ge(ctx_loaded[t.odd], (t.group + 1) * DMA)
                wait(pe, xc_done, t.index)
                wait(pe, x_done, t.index - 5)
                pe.transpose(turn_in_ps[:, 0, :], xn[:, t.odd, :], ident[:, :])
                pe.transpose(turn_in_ps[:, 1, :], ctx_in[:, t.odd, :], ident[:, :]).then_inc(turned_in, 1)

            def project_qk(t):
                pe.wait_ge(xc_done, t.index + 1)
                wait(pe, qk_done, t.index)
                pe.matmul(qk_ps[:, 0, :], w_t[:, 0, :], xc_t[:, t.odd, 0, :], start=True, stop=True)
                pe.matmul(qk_ps[:, 1, :], w_t[:, 1, :], xc_t[:, t.odd, 1, :], start=True, stop=True).then_inc(qk_filled, 1)

            def project_v(t):
                wait(pe, v_done, t.index)
                pe.matmul(v_ps[:, 0:D], xc_t[:, t.odd, 1, :], w_t[:, 2, :], start=True, stop=True).then_inc(v_filled, 1)

            def step(t):
                now, one, two, three, four, five, six = t, t.back(1), t.back(2), t.back(3), t.back(4), t.back(5), t.back(6)
                if one.live:
                    project_qk(one)
                if six.live:
                    up(six)
                if two.live:
                    scores(two)
                if four.live:
                    mix(four)
                if now.live:
                    turn_in(now)
                if two.live:
                    project_v(two)
                if five.live:
                    turn_out(five)
                if three.live:
                    turn_prob(three)

            over_tiles(pe, step, 6)

        @block.scalar
        def _(act):
            act.wait_ge(w_turned, 1)
            act.copy(w_t[:, :, :], turn_in_ps[:, :, :]).then_inc(w_done, 1)
            act.wait_ge(zeroed, 3)

            def bring_out(t):
                act.wait_ge(out_turned, t.index + 1)
                wait(act, up_done, t.index - 1)
                act.copy(out_t[:, t.odd, :], turn_in_ps[:, 2, :]).then_inc(out_t_done, 1)

            def bring_prob(t):
                act.wait_ge(prob_turned, t.index + 1)
                wait(act, mixed, t.index - 1)
                act.copy(prob_t[:, t.odd, :, :, :], turn_ps[:, :, :]).then_inc(prob_t_done, 1)

            def exponent(t):
                act.wait_ge(shifted, t.index + 1)
                act.activation(expo[:, t.odd, :, :], expo[:, t.odd, :, :], ACT.Exp, scale=D ** -0.5).then_inc(exp_done, 1)

            def bring_in(t):
                act.wait_ge(turned_in, t.index + 1)
                wait(act, v_filled, t.index - 1)
                act.copy(xc_t[:, t.odd, :, :], turn_in_ps[:, 0:2, :]).then_inc(xc_done, 1)

            def bring_qk(t):
                act.wait_ge(qk_filled, t.index + 1)
                wait(act, scored, t.index - 1)
                for b in range(PER_TILE):
                    wait(act, q_block_done[b], t.index - 1)
                act.activation(qk[:, t.odd, 0, :], qk_ps[:, 0, :], ACT.Identity, bias=bq[:, :])
                act.activation(qk[:, t.odd, 1, :], qk_ps[:, 1, :], ACT.Identity, bias=bk[:, :]).then_inc(qk_done, 1)

            def bring_v(t):
                act.wait_ge(v_filled, t.index + 1)
                wait(act, mixed, t.index - 1)
                for b in range(PER_TILE):
                    for p in range(2):
                        frm = v_ps[b * SEQ:(b + 1) * SEQ, 0:D].rearrange("k (c p m) -> k c p m", p=2, m=2 * HD)[:, :, p, :]
                        last = act.copy(v_block[p * SEQ:(p + 1) * SEQ, t.odd, b, :, p, 0:2 * HD], frm)
                last.then_inc(v_done, 1)

            def step(t):
                now, one, two, three, five = t, t.back(1), t.back(2), t.back(3), t.back(5)
                if one.live:
                    bring_qk(one)
                if three.live:
                    exponent(three)
                if five.live:
                    bring_out(five)
                if now.live:
                    bring_in(now)
                if two.live:
                    bring_v(two)
                if three.live:
                    bring_prob(three)

            over_tiles(act, step, 5)

        @block.vector
        def _(dve):
            for t in range(TILES):
                last = dve.bn_aggr(mean_var[:, t, :], stats[:, t, :])
            last.then_inc(mean_done, 1)
            dve.wait_ge(mean_done, 1)
            dve.tensor_scalar(var_eps[:, :], mean_var[:, :, 1], EPS, None, ALU.add).then_inc(var_done, 1)
            dve.memset(v_block[:, :, :, :, :, :], 0.0).then_inc(zeroed, 1)
            dve.wait_ge(zeroed, 1)
            for p in range(2):
                dve.memset(v_block[p * SEQ:(p + 1) * SEQ, :, :, :, p, 2 * HD:VCOL], 1.0).then_inc(zeroed, 1)
            dve.wait_ge(masks_done, 1)
            dve.wait_ge(keep["mask_loaded"], 2 * DMA)

            def normalize(t):
                dve.wait_ge(rstd_done, 1 if isinstance(t.group, int) and t.index < FIRST_ROOTS else 2)
                wait(dve, turned_in, t.index - 1)
                dve.tensor_scalar(xn[:, t.odd, :], x[:, t.index, :], mean_var[:, t.index, 0:1],
                                  scalar_at(rstd, t), ALU.subtract, ALU.mult).then_inc(xn_done, 1)

            def mask(t):
                dve.wait_ge(scored, t.index + 1)
                dve.wait_ge(valid_done, t.index + 1)
                wait(dve, shifted, t.index - 1)
                for b in range(PER_TILE):
                    dve.scalar_tensor_tensor(
                        score[:, t.odd, b * CHUNKS:(b + 1) * CHUNKS, :],
                        score_ps[:, b, :].rearrange("p (c k) -> p c k", k=SEQ), 1e-20,
                        many(valid[:, t.odd, b, :], CHUNKS, 1), ALU.subtract, ALU.mult).then_inc(masked, 1)
                dve.wait_ge(masked, 2 * t.index + 2)
                dve.tensor_reduce(top[:, t.odd, :], score[:, t.odd, :, :], AX.X, ALU.max).then_inc(top_done, 1)

            def take_out(t):
                dve.wait_ge(mixed, t.index + 1)
                sums = mix_ps[:, 0:PER_TILE * PAIRS * 2 * VCOL].rearrange("p (b n m) -> p b n m", b=PER_TILE, m=VCOL)
                dve.reciprocal(share[:, t.odd, :, :], sums[:, :, :, 2 * HD:VCOL].rearrange("p b n o -> p b (n o)")).then_inc(share_done, 1)
                dve.wait_ge(share_done, t.index + 1)
                wait(dve, out_done, t.index - 1)
                for b in range(PER_TILE):
                    for h in range(2):
                        rows = slice(h * SEQ, (h + 1) * SEQ)
                        to = out_raw[b * SEQ:(b + 1) * SEQ, t.odd, :].rearrange("q (n h d) -> q n h d", h=2, d=HD)[:, :, h, :]
                        last = dve.tensor_tensor(to, sums[rows, b, :, h * HD:(h + 1) * HD],
                                                 many(share[rows, t.odd, b, :], HD), ALU.mult)
                last.then_inc(out_raw_done, 1)

            def residual(t):
                dve.wait_ge(up_done, t.index + 1)
                dve.wait_ge(x_biased, t.index + 1)
                dve.tensor_tensor(x[:, t.index, :], turn_in_ps[:, 3, :], x[:, t.index, :], ALU.add).then_inc(x_done, 1)

            def next_moments(t):
                dve.wait_ge(x_done, t.index + 1)
                dve.bn_stats(stats[:, t.index, :], x[:, t.index, :]).then_inc(next_stats_done, 1)

            def spread_q(t):
                dve.wait_ge(qk_done, t.index + 1)
                wait(dve, scored, t.index - 1)
                dve.tensor_tensor(q_block[:, t.odd, 1, :, :], many(qk[:, t.odd, 0, SEQ:P], HEADS, 1),
                                  many(head_of[:, :], SEQ), ALU.mult).then_inc(q_block_done[1], 1)

            def find_valid(t):
                wait(dve, masked, 2 * t.index - 2)
                dve.tensor_scalar(valid[:, t.odd, :, :].rearrange("p b k -> p (b k)"),
                                  keep["mask"][:, t.index, :], 0, None, ALU.not_equal).then_inc(valid_done, 1)

            def step(t):
                now, one, two, four, six, seven = t, t.back(1), t.back(2), t.back(4), t.back(6), t.back(7)
                if one.live:
                    find_valid(one)
                    spread_q(one)
                if now.live:
                    normalize(now)
                if six.live:
                    residual(six)
                if two.live:
                    mask(two)
                if four.live:
                    take_out(four)
                if seven.live:
                    next_moments(seven)

            over_tiles(dve, step, 7)

        @block.gpsimd
        def _(pool):
            pool.memset(head_of[:, :], 1.0).then_inc(masks_filled, 1)
            pool.wait_ge(masks_filled, 1)
            pool.affine_select(out=head_of[:, :], in_=head_of[:, :], compare_op=ALU.is_ge, fill=0.0, base=0,
                               pattern=[[-HD, HEADS]], channel_multiplier=1).then_inc(masks_filled, 1)
            pool.wait_ge(masks_filled, 2)
            pool.affine_select(out=head_of[:, :], in_=head_of[:, :], compare_op=ALU.is_ge, fill=0.0, base=HD - 1,
                               pattern=[[HD, HEADS]], channel_multiplier=-1).then_inc(masks_done, 1)
            pool.wait_ge(masks_done, 1)
            pool.wait_ge(var_done, 1)

            def scale_roots(first, end):
                pool.tensor_tensor(rstd[:, first:end], var_eps[:, first:end],
                                   eps_pow[:, 0:1].to_broadcast([P, end - first]), ALU.pow).then_inc(rstd_done, 1)

            scale_roots(0, FIRST_ROOTS)

            def shift(t):
                pool.wait_ge(top_done, t.index + 1)
                wait(pool, prob_turned, t.index - 1)
                pool.tensor_tensor(expo[:, t.odd, :, :], score[:, t.odd, :, :], many(top[:, t.odd, :], SEQ),
                                   ALU.subtract).then_inc(shifted, 1)

            def spread_q(t):
                pool.wait_ge(qk_done, t.index + 1)
                wait(pool, scored, t.index - 1)
                pool.tensor_tensor(q_block[:, t.odd, 0, :, :], many(qk[:, t.odd, 0, 0:SEQ], HEADS, 1),
                                   many(head_of[:, :], SEQ), ALU.mult).then_inc(q_block_done[0], 1)

            def bias_x(t):
                pool.wait_ge(xn_done, t.index + 1)
                pool.tensor_tensor(x[:, t.index, :], x[:, t.index, :], bo[:, :], ALU.add).then_inc(x_biased, 1)

            def bias_out(t):
                pool.wait_ge(out_raw_done, t.index + 1)
                wait(pool, out_turned, t.index - 1)
                pool.tensor_tensor(out[:, t.odd, :], out_raw[:, t.odd, :], bv[:, :], ALU.add).then_inc(out_done, 1)

            def step(t):
                now, one, three, four = t, t.back(1), t.back(3), t.back(4)
                if three.live:
                    shift(three)
                if one.live:
                    spread_q(one)
                if four.live:
                    bias_out(four)
                if now.live:
                    bias_x(now)
                if isinstance(t.group, int) and t.index == 2:
                    scale_roots(FIRST_ROOTS, TILES)

            over_tiles(pool, step, 4)


def select_experts(nc, dram, keep):
    ctx = ExitStack()
    with ctx:
        m = Memory(nc, ctx, "sel")
        x, ident, eps_pow = keep["x"], keep["ident"], keep["eps_pow"]
        share, table = keep["share"], keep["table"]
        GROUP = 4
        GROUPS = TILES // GROUP
        PICKS = TILES * EXPERTS
        gate_w = m.sb("gate_w", [P, EXPERTS])
        upto = m.sb("upto", [P, P], BF16)
        ones = m.sb("ones", [P, P], BF16)
        number = m.sb("number", [P, EXPERTS])
        number_up = m.sb("number_up", [P, EXPERTS])
        region = m.sb("region", [P, EXPERTS])
        token = m.sb("token", [P, TILES, TOP], I32)
        blank = m.sb("blank", [P, 2 * EXPERTS, ROW])
        not_first = m.sb("not_first", [P, EXPERTS, TILES])

        ROOT_PARTS = ((0, 1), (1, 3), (3, GROUPS))
        stats = keep["stats"]
        mean_var = m.sb("mean_var", [P, TILES, 2])
        var_eps = m.sb("var_eps", [P, TILES])
        rstd = m.sb("rstd", [P, TILES])
        xn = m.sb("xn", [P, TILES, D])
        xn_now = m.sb("xn_now", [P, 2, GROUP, D])
        xn_t = m.sb("xn_t", [P, 2, GROUP, P])
        logit = m.sb("logit", [P, TOP, TILES, EXPERTS])
        best = m.sb("best", [P, TOP, TILES])
        even = m.sb("even", [P, TILES, EXPERTS])
        which = m.sb("which", [P, TILES])
        picked = m.sb("picked", [P, TOP, TILES, EXPERTS])
        less = m.sb("less", [P, TILES])
        second = m.sb("second", [P, TILES])
        both = m.sb("both", [P, TILES])
        taken = m.sb("taken", [P, TILES, EXPERTS], BF16)
        in_tile = m.sb("in_tile", [P, TILES, EXPERTS])
        up_to_tile = m.sb("up_to_tile", [P, EXPERTS, TILES])
        before = m.sb("before", [P, TILES, EXPERTS])
        order = m.sb("order", [P, TILES, EXPERTS])
        spread = m.sb("spread", [P, TILES, EXPERTS])
        row = m.sb("row", [P, TILES, TOP])
        rows_out = m.sb("rows_out", [P, 2, TOP, ROW])
        row_now = m.sb("row_now", [P, 2, TOP], I32)
        pad = m.sb("pad", [P, EXPERTS])
        pad_i = m.sb("pad_i", [P, EXPERTS], I32)
        steps = m.sb("steps", [P, TILES])
        over = m.sb("over", [P, EXPERTS, TILES])
        tiles = m.sb("tiles", [P, EXPERTS])
        unit = m.sb("unit", [P, EXPERTS])
        end = m.sb("end", [P, EXPERTS])
        start = m.sb("start", [P, EXPERTS])
        first_row = m.sb("first_row", [P, EXPERTS])
        index = m.sb("index", [P, SORTED])
        past = m.sb("past", [P, SORTED, EXPERTS])
        owner = m.sb("owner", [P, SORTED])
        own = m.sb("own", [P, SORTED, EXPERTS])
        from_row = m.sb("from_row", [P, SORTED])
        spare = m.sb("spare", [P, SORTED])
        blank_first = m.sb("blank_first", [P, 1])

        turn_ps = [m.ps(f"turn{i}", [P, GROUP, P]) for i in range(2)]
        logit_ps = m.ps("logit", [P, GROUPS, GROUP, EXPERTS])
        in_tile_ps = m.ps("in_tile", [P, PICKS])
        tile_ps = m.ps("tile", [P, PICKS])

        loaded, filled, ready = m.sem("loaded"), m.sem("filled"), m.sem("ready")
        mean_done, var_done = m.sem("mean_done"), m.sem("var_done")
        rstd_done, centered, xn_done = m.sem("rstd_done"), m.sem("centered"), m.sem("xn_done")
        xn_kept, turned, xn_t_done, gated = m.sem("xn_kept"), m.sem("turned"), m.sem("xn_t_done"), m.sem("gated")
        chosen, taken_done, counted = m.sem("chosen"), m.sem("taken_done"), m.sem("counted")
        second_done, shared, placed = m.sem("second_done"), m.sem("shared"), m.sem("placed")
        rows_filled, targets_filled = m.sem("rows_filled"), m.sem("targets_filled")
        scattered = [m.sem(f"scattered{i}") for i in range(2)]
        plan, padded, blank_written = m.sem("plan"), m.sem("padded"), m.sem("blank_written")

        block = ctx.enter_context(nc.Block())

        @block.sync
        def _(sp):
            sp.dma_start(gate_w[:, :], dram["L1_ffn_W_gate"]).then_inc(loaded, DMA)
            sp.wait_ge(ready, 9)
            sp.dma_start(keep["sorted"][EXPERTS * REGION:, :].rearrange("(n p) d -> p n d", p=P),
                         blank[:, EXPERTS:, :]).then_inc(blank_written, DMA)
            sp.wait_ge(plan, 2)
            for n in range(EXPERTS):
                at = sp.value_load(pad_i[0:1, n:n + 1], min_val=n * REGION, max_val=(n + 1) * REGION - P)
                sp.dma_start(keep["sorted"][bass.ds(at, P), :], blank[:, n, :]).then_inc(padded, DMA)
            sp.wait_ge(blank_written, DMA)
            sp.wait_ge(padded, EXPERTS * DMA)

        @block.tensor
        def _(pe):
            pe.wait_ge(loaded, DMA)

            def turn(g):
                pe.wait_ge(xn_done, g.index + 1)
                wait(pe, xn_t_done, g.index - 1)
                for n in range(GROUP):
                    last = pe.transpose(turn_ps[g.odd][:, n, :], xn_now[:, g.odd, n, :], ident[:, :])
                last.then_inc(turned, 1)

            def gate(g):
                pe.wait_ge(xn_t_done, g.index + 1)
                for n in range(GROUP):
                    last = pe.matmul(logit_ps[:, g.index, n, :], xn_t[:, g.odd, n, :], gate_w[:, :], start=True, stop=True)
                last.then_inc(gated, 1)

            def step(g):
                two = g.back(2)
                if two.live:
                    gate(two)
                if g.live:
                    turn(g)

            over_tiles(pe, step, 2, GROUPS)
            pe.wait_ge(ready, 9)
            pe.wait_ge(taken_done, 1)
            picks = taken[:, :, :].rearrange("p t x -> p (t x)")
            pe.matmul(in_tile_ps[:, :], upto[:, :], picks, start=True, stop=True)
            pe.matmul(tile_ps[:, :], ones[:, :], picks, start=True, stop=True).then_inc(counted, 1)

        @block.scalar
        def _(act):
            def bring(g):
                act.wait_ge(turned, g.index + 1)
                wait(act, gated, g.index - 1)
                act.copy(xn_t[:, g.odd, :, :], turn_ps[g.odd][:, :, :]).then_inc(xn_t_done, 1)

            def keep_xn(g):
                act.wait_ge(xn_done, g.index + 1)
                act.copy(xn_groups[:, g.index, :, :], xn_now[:, g.odd, :, :]).then_inc(xn_kept, 1)

            xn_groups = xn[:, :, :].rearrange("p (g n) d -> p g n d", n=GROUP)

            def group_step(g):
                keep_xn(g)
                bring(g)

            over_tiles(act, group_step, 0, GROUPS)

            act.wait_ge(chosen, 13)
            act.activation(second[:, :], less[:, :], ACT.Exp).then_inc(second_done, 1)

            def fill(t):
                wait(act, scattered[t.odd], t.group * TOP * DMA)
                act.copy(rows_out[:, t.odd, :, 0:D], many(xn[:, t.index, :], TOP, 1)).then_inc(rows_filled, 1)

            over_tiles(act, fill, 0)

        @block.vector
        def _(dve):
            for t in range(TILES):
                last = dve.bn_aggr(mean_var[:, t, :], stats[:, t, :])
            last.then_inc(mean_done, 1)
            dve.wait_ge(mean_done, 1)
            dve.tensor_scalar(var_eps[:, :], mean_var[:, :, 1], EPS, None, ALU.add).then_inc(var_done, 1)
            groups = [slice(g * GROUP, (g + 1) * GROUP) for g in range(GROUPS)]
            for g, part in enumerate(groups):
                dve.tensor_tensor(xn[:, part, :], x[:, part, :], many(mean_var[:, part, 0], D), ALU.subtract).then_inc(centered, 1)
                dve.wait_ge(centered, g + 1)
                dve.wait_ge(rstd_done, sum(g >= first for first, _ in ROOT_PARTS))
                if g >= 2:
                    dve.wait_ge(turned, g - 1)
                    dve.wait_ge(xn_kept, g - 1)
                dve.tensor_tensor(xn_now[:, g % 2, :, :], xn[:, part, :], many(rstd[:, part], D), ALU.mult).then_inc(xn_done, 1)

            dve.wait_ge(ready, 9)
            dve.wait_ge(gated, GROUPS)
            dve.tensor_copy(logit[:, 0, :, :], logit_ps[:, :, :, :].rearrange("p g n x -> p (g n) x")).then_inc(chosen, 1)
            for k in range(TOP):
                dve.wait_ge(chosen, 6 * k + 1)
                dve.tensor_reduce(best[:, k, :], logit[:, k, :, :], AX.X, ALU.max).then_inc(chosen, 1)
                dve.wait_ge(chosen, 6 * k + 2)
                dve.tensor_tensor(even[:, :, :], logit[:, k, :, :], many(best[:, k, :], EXPERTS), ALU.is_equal).then_inc(chosen, 1)
                dve.wait_ge(chosen, 6 * k + 3)
                dve.scalar_tensor_tensor(even[:, :, :], even[:, :, :], -float(EXPERTS), many(number_up[:, :], TILES, 1),
                                         ALU.mult, ALU.add).then_inc(chosen, 1)
                dve.wait_ge(chosen, 6 * k + 4)
                dve.tensor_reduce(which[:, :], even[:, :, :], AX.X, ALU.min).then_inc(chosen, 1)
                dve.wait_ge(chosen, 6 * k + 5)
                dve.tensor_tensor(picked[:, k, :, :], many(number[:, :], TILES, 1), many(which[:, :], EXPERTS),
                                  ALU.is_equal).then_inc(chosen, 1)
                if k == 0:
                    dve.wait_ge(chosen, 6)
                    dve.scalar_tensor_tensor(logit[:, 1, :, :], picked[:, 0, :, :], LEAST, logit[:, 0, :, :], ALU.mult,
                                             ALU.add).then_inc(chosen, 1)
            dve.wait_ge(chosen, 12)
            dve.tensor_tensor(taken[:, :, :], picked[:, 0, :, :], picked[:, 1, :, :], ALU.add).then_inc(taken_done, 1)
            dve.tensor_tensor(less[:, :], best[:, 1, :], best[:, 0, :], ALU.subtract).then_inc(chosen, 1)
            dve.wait_ge(counted, 1)
            dve.tensor_copy(over[:, :, :], tile_ps[:, :].rearrange("p (t x) -> p x t", x=EXPERTS)).then_inc(placed, 1)
            dve.tensor_copy(in_tile[:, :, :], in_tile_ps[:, :].rearrange("p (t x) -> p t x", x=EXPERTS)).then_inc(placed, 1)
            dve.wait_ge(placed, 2)
            dve.tensor_tensor_scan(up_to_tile[:, :, :].rearrange("p x t -> p (x t)"), not_first[:, :, :].rearrange("p x t -> p (x t)"),
                                   over[:, :, :].rearrange("p x t -> p (x t)"), 0.0, ALU.mult, ALU.add).then_inc(placed, 1)
            dve.wait_ge(placed, 3)
            dve.tensor_tensor(before[:, :, :].rearrange("p t x -> p x t"), up_to_tile[:, :, :], over[:, :, :],
                              ALU.subtract).then_inc(placed, 1)
            dve.wait_ge(placed, 4)
            dve.scalar_tensor_tensor(order[:, :, :], before[:, :, :], -1.0, in_tile[:, :, :], ALU.add, ALU.add).then_inc(placed, 1)
            dve.wait_ge(placed, 5)
            dve.tensor_tensor(order[:, :, :], order[:, :, :], many(region[:, :], TILES, 1), ALU.add).then_inc(placed, 1)
            dve.wait_ge(placed, 6)
            for k in range(TOP):
                dve.tensor_tensor(spread[:, :, :], picked[:, k, :, :], order[:, :, :], ALU.mult).then_inc(placed, 1)
                dve.wait_ge(placed, 7 + 2 * k)
                dve.tensor_reduce(row[:, :, k], spread[:, :, :], AX.X, ALU.add).then_inc(placed, 1)
                dve.wait_ge(placed, 8 + 2 * k)

            def fill(t):
                wait(dve, scattered[t.odd], t.group * TOP * DMA)
                dve.tensor_copy(rows_out[:, t.odd, :, D:ROW].rearrange("p k o -> p (k o)").bitcast(I32), token[:, t.index, :])
                dve.tensor_copy(row_now[:, t.odd, :], row[:, t.index, :]).then_inc(targets_filled, 1)

            for t in range(2):
                fill(Tile(0, t))

            dve.wait_ge(second_done, 1)
            dve.tensor_scalar(both[:, :], second[:, :], 1.0, None, ALU.add).then_inc(shared, 1)
            dve.wait_ge(shared, 1)
            dve.reciprocal(share[:, :, 0], both[:, :]).then_inc(shared, 1)
            dve.wait_ge(shared, 2)
            dve.tensor_tensor(share[:, :, 1], share[:, :, 0], second[:, :], ALU.mult).then_inc(shared, 1)

            total = up_to_tile[:, :, TILES - 1]
            dve.tensor_tensor(pad[:, :], total, region[:, :], ALU.add).then_inc(plan, 1)
            dve.wait_ge(plan, 1)
            dve.tensor_copy(pad_i[:, :], pad[:, :]).then_inc(plan, 1)
            dve.tensor_tensor(over[:, :, :], many(total, TILES), many(steps[:, :], EXPERTS, 1), ALU.is_gt).then_inc(plan, 1)
            dve.wait_ge(plan, 3)
            dve.tensor_reduce(tiles[:, :], over[:, :, :], AX.X, ALU.add).then_inc(plan, 1)
            dve.wait_ge(plan, 4)
            dve.tensor_tensor_scan(end[:, :], unit[:, :], tiles[:, :], 0.0, ALU.mult, ALU.add).then_inc(plan, 1)
            dve.wait_ge(plan, 5)
            dve.tensor_tensor(start[:, :], end[:, :], tiles[:, :], ALU.subtract).then_inc(plan, 1)
            dve.tensor_tensor(past[:, :, :], many(index[:, :], EXPERTS), many(end[:, :], SORTED, 1), ALU.is_ge).then_inc(plan, 1)
            dve.wait_ge(plan, 7)
            dve.tensor_reduce(owner[:, :], past[:, :, :], AX.X, ALU.add).then_inc(plan, 1)
            dve.scalar_tensor_tensor(first_row[:, :], start[:, :], -float(P), region[:, :], ALU.mult, ALU.add).then_inc(plan, 1)
            dve.wait_ge(plan, 9)
            dve.tensor_tensor(own[:, :, :], many(owner[:, :], EXPERTS), many(number[:, :], SORTED, 1),
                              ALU.is_equal).then_inc(plan, 1)
            dve.wait_ge(plan, 10)
            dve.tensor_tensor(own[:, :, :], own[:, :, :], many(first_row[:, :], SORTED, 1), ALU.mult).then_inc(plan, 1)
            dve.wait_ge(plan, 11)
            dve.tensor_reduce(from_row[:, :], own[:, :, :], AX.X, ALU.add).then_inc(plan, 1)
            dve.tensor_scalar(spare[:, :], owner[:, :], float(EXPERTS), None, ALU.is_ge).then_inc(plan, 1)
            dve.tensor_scalar(table[:, 0, :], owner[:, :], float(EXPERTS - 1), None, ALU.min).then_inc(plan, 1)
            dve.tensor_scalar(blank_first[:, :], end[:, EXPERTS - 1:EXPERTS], -float(P), float(EXPERTS * REGION),
                              ALU.mult, ALU.add).then_inc(plan, 1)
            dve.wait_ge(plan, 15)
            dve.scalar_tensor_tensor(from_row[:, :], index[:, :], float(P), from_row[:, :], ALU.mult, ALU.add).then_inc(plan, 1)
            dve.wait_ge(plan, 16)
            dve.scalar_tensor_tensor(table[:, 1, :], spare[:, :], blank_first[:, 0:1], from_row[:, :], ALU.mult,
                                     ALU.add).then_inc(plan, 1)

            def later(t):
                if t.live and (not isinstance(t.group, int) or t.index >= 2):
                    fill(t)

            over_tiles(dve, later, 0)

        @block.gpsimd
        def _(pool):
            pool.memset(upto[:, :], 1.0).then_inc(filled, 1)
            pool.memset(not_first[:, :, :], 1.0).then_inc(filled, 1)
            pool.memset(blank[:, :, :], 0.0).then_inc(filled, 1)
            pool.memset(ones[:, :], 1.0).then_inc(ready, 1)
            pool.memset(unit[:, :], 1.0).then_inc(ready, 1)
            pool.iota(number[:, :], pattern=[[1, EXPERTS]], base=0, channel_multiplier=0,
                      allow_small_or_imprecise_dtypes=True).then_inc(ready, 1)
            pool.iota(number_up[:, :], pattern=[[1, EXPERTS]], base=EXPERTS, channel_multiplier=0,
                      allow_small_or_imprecise_dtypes=True).then_inc(ready, 1)
            pool.iota(region[:, :], pattern=[[REGION, EXPERTS]], base=0, channel_multiplier=0,
                      allow_small_or_imprecise_dtypes=True).then_inc(ready, 1)
            pool.iota(steps[:, :], pattern=[[P, TILES]], base=0, channel_multiplier=0,
                      allow_small_or_imprecise_dtypes=True).then_inc(ready, 1)
            pool.iota(index[:, :], pattern=[[1, SORTED]], base=0, channel_multiplier=0,
                      allow_small_or_imprecise_dtypes=True).then_inc(filled, 1)
            pool.iota(token[:, :, :], pattern=[[P * TOP, TILES], [1, TOP]], base=0, channel_multiplier=TOP).then_inc(filled, 1)
            pool.wait_ge(filled, 5)
            pool.affine_select(out=upto[:, :], in_=upto[:, :], compare_op=ALU.is_ge, fill=0.0, base=0,
                               pattern=[[1, P]], channel_multiplier=-1).then_inc(ready, 1)
            pool.affine_select(out=not_first[:, :, :], in_=not_first[:, :, :], compare_op=ALU.not_equal, fill=0.0, base=0,
                               pattern=[[0, EXPERTS], [1, TILES]], channel_multiplier=0).then_inc(ready, 1)
            pool.iota(blank[:, :, D:ROW].rearrange("p n o -> p (n o)").bitcast(I32), pattern=[[P, 2 * EXPERTS]],
                      base=TILES * P * TOP, channel_multiplier=1).then_inc(ready, 1)
            pool.wait_ge(ready, 9)
            pool.wait_ge(var_done, 1)
            for first, end in ROOT_PARTS:
                part = slice(first * GROUP, end * GROUP)
                pool.tensor_tensor(rstd[:, part], var_eps[:, part],
                                   eps_pow[:, 0:1].to_broadcast([P, (end - first) * GROUP]), ALU.pow).then_inc(rstd_done, 1)

            def scatter(t):
                pool.wait_ge(rows_filled, t.index + 1)
                pool.wait_ge(targets_filled, t.index + 1)
                apart(pool)
                for k in range(TOP):
                    pool.indirect_dma_start(keep["sorted"], bass.IndirectOffsetOnAxis(ap=row_now[:, t.odd, k:k + 1], axis=0),
                                            rows_out[:, t.odd, k, :], None).then_inc(scattered[t.odd], DMA)

            over_tiles(pool, scatter, 0)
            for o in range(2):
                pool.wait_ge(scattered[o], TILES // 2 * TOP * DMA)
            pool.wait_ge(plan, 17)


def run_experts(nc, dram, keep):
    ctx = ExitStack()
    with ctx:
        m = Memory(nc, ctx, "run")
        ident, w_in, w_out, b_in, b_out, table = (keep[n] for n in ("ident", "w_in", "w_out", "b_in", "b_out", "table"))
        BUFS, PICKS = 8, 4
        xs = m.sb("xs", [P, BUFS, ROW])
        xs_t = m.sb("xs_t", [P, 2, P])
        own_w_in = m.sb("own_w_in", [P, PICKS, MLP])
        own_w_out = m.sb("own_w_out", [P, PICKS, BLOCKS, D])
        own_b_out = m.sb("own_b_out", [P, PICKS, D])
        b_in_t = m.sb("b_in_t", [P, EXPERTS, BLOCKS])
        own_b_in = m.sb("own_b_in", [P, PICKS, BLOCKS])
        hid_t = m.sb("hid_t", [P, 2, BLOCKS, P])
        y = m.sb("y", [P, BUFS, D])
        turn_ps = m.ps("turn", [P, 512])
        hid_t_ps = [m.ps(f"hid_t{i}", [P, BLOCKS, P]) for i in range(2)]
        y_ps = [m.ps(f"y{i}", [P, 512]) for i in range(2)]

        xs_loaded = [m.sem(f"xs_loaded{i}") for i in range(BUFS)]
        stored = [m.sem(f"stored{i}") for i in range(BUFS)]
        turned, xs_t_done, hid_summed, hid_t_done = m.sem("turned"), m.sem("xs_t_done"), m.sem("hid_summed"), m.sem("hid_t_done")
        b_in_turned, b_in_ready = m.sem("b_in_turned"), m.sem("b_in_ready")
        picked_in, picked_out = m.sem("picked_in"), m.sem("picked_out")
        y_summed, y_done = m.sem("y_summed"), m.sem("y_done")

        sorted_rows = keep["sorted"]
        block = ctx.enter_context(nc.Block())

        @block.sync
        def _(sp):
            def load(t):
                wait(sp, stored[t.at], t.group * DMA)
                at = sp.value_load(table[0:1, 1, t.index:t.index + 1] if isinstance(t.index, int) else
                                   table[0:1, 1, bass.ds(t.index, 1)], min_val=0, max_val=EXPERTS * (REGION + P) - P)
                sp.dma_start(xs[:, t.at, :], sorted_rows[bass.ds(at, P), :]).then_inc(xs_loaded[t.at], DMA)

            over_tiles(sp, load, 0, SORTED, BUFS)

        @block.tensor
        def _(pe):
            pe.wait_ge(keep["w_loaded"], W_LOADS * DMA)
            pe.transpose(turn_ps[:, 0:EXPERTS * BLOCKS], b_in[:, :], ident[0:EXPERTS * BLOCKS, 0:EXPERTS * BLOCKS]).then_inc(b_in_turned, 1)
            pe.wait_ge(b_in_ready, 1)

            def turn(t):
                pe.wait_ge(xs_loaded[t.at], (t.group + 1) * DMA)
                wait(pe, xs_t_done, t.index)
                pe.transpose(turn_ps[:, 0:P], xs[:, t.at, 0:D], ident[:, :]).then_inc(turned, 1)

            def widen(t):
                pe.wait_ge(xs_t_done, t.index + 1)
                pe.wait_ge(picked_in, 2 * t.index + 2)
                wait(pe, hid_t_done, t.index - 1)
                for c in range(BLOCKS):
                    last = pe.matmul(hid_t_ps[t.odd][:, c, :], own_w_in[:, t.at % PICKS, c * P:(c + 1) * P], xs_t[:, t.odd, :],
                                     start=True, stop=True)
                last.then_inc(hid_summed, 1)

            def narrow(t):
                pe.wait_ge(hid_t_done, t.index + 1)
                pe.wait_ge(picked_out, 2 * t.index + 2)
                wait(pe, y_done, t.index - 1)
                for c in range(BLOCKS):
                    last = pe.matmul(y_ps[t.odd][:, 0:D], hid_t[:, t.odd, c, :], own_w_out[:, t.at % PICKS, c, :],
                                     start=(c == 0), stop=(c == BLOCKS - 1))
                last.then_inc(y_summed, 1)

            def step(t):
                one, three = t.back(1), t.back(3)
                if three.live:
                    narrow(three)
                if t.live:
                    turn(t)
                if one.live:
                    widen(one)

            over_tiles(pe, step, 3, SORTED, BUFS)

        @block.scalar
        def _(act):
            act.wait_ge(b_in_turned, 1)
            act.copy(b_in_t[:, :, :], turn_ps[:, 0:EXPERTS * BLOCKS].rearrange("p (x c) -> p x c", x=EXPERTS)).then_inc(b_in_ready, 1)

            def step(t):
                one = t.back(1)
                if t.live:
                    act.wait_ge(turned, t.index + 1)
                    wait(act, hid_summed, t.index - 1)
                    act.copy(xs_t[:, t.odd, :], turn_ps[:, 0:P]).then_inc(xs_t_done, 1)
                if one.live:
                    act.wait_ge(hid_summed, one.index + 1)
                    act.wait_ge(picked_in, 2 * one.index + 2)
                    wait(act, y_summed, one.index - 1)
                    for c in range(BLOCKS):
                        last = act.activation(hid_t[:, one.odd, c, :], hid_t_ps[one.odd][:, c, :], ACT.Gelu,
                                              bias=own_b_in[:, one.at % PICKS, c:c + 1])
                    last.then_inc(hid_t_done, 1)

            over_tiles(act, step, 1, SORTED, BUFS)

        @block.vector
        def _(dve):
            dve.wait_ge(keep["w_loaded"], W_LOADS * DMA)
            dve.wait_ge(b_in_ready, 1)

            def step(t):
                three = t.back(3)
                if t.live:
                    n = dve.value_load(table[0:1, 0, t.index:t.index + 1] if isinstance(t.index, int) else
                                       table[0:1, 0, bass.ds(t.index, 1)], min_val=0, max_val=EXPERTS - 1)
                    wait(dve, hid_summed, t.index - PICKS + 1)
                    dve.tensor_copy(own_w_in[:, t.at % PICKS, :], w_in[:, n, :]).then_inc(picked_in, 1)
                    wait(dve, hid_t_done, t.index - PICKS + 1)
                    dve.tensor_copy(own_b_in[:, t.at % PICKS, :], b_in_t[:, n, :]).then_inc(picked_in, 1)
                    wait(dve, y_summed, t.index - PICKS + 1)
                    dve.tensor_copy(own_w_out[:, t.at % PICKS, :, :], w_out[:, n, :, :]).then_inc(picked_out, 1)
                    wait(dve, y_done, t.index - PICKS + 1)
                    dve.tensor_copy(own_b_out[:, t.at % PICKS, :], b_out[:, n, :]).then_inc(picked_out, 1)
                if three.live:
                    dve.wait_ge(y_summed, three.index + 1)
                    dve.wait_ge(picked_out, 2 * three.index + 2)
                    wait(dve, stored[three.at], three.group * DMA)
                    dve.tensor_tensor(y[:, three.at, :], y_ps[three.odd][:, 0:D], own_b_out[:, three.at % PICKS, :],
                                      ALU.add).then_inc(y_done, 1)

            over_tiles(dve, step, 3, SORTED, BUFS)

        @block.gpsimd
        def _(pool):
            def store(t):
                pool.wait_ge(y_done, t.index + 1)
                pool.wait_ge(xs_loaded[t.at], (t.group + 1) * DMA)
                apart(pool)
                pool.indirect_dma_start(keep["result"], bass.IndirectOffsetOnAxis(ap=xs[:, t.at, D:ROW].bitcast(I32), axis=0),
                                        y[:, t.at, :], None).then_inc(stored[t.at], DMA)

            over_tiles(pool, store, 0, SORTED, BUFS)
            for i in range(BUFS):
                pool.wait_ge(stored[i], SORTED // BUFS * DMA)


def combine(nc, dram, keep, out):
    ctx = ExitStack()
    with ctx:
        m = Memory(nc, ctx, "comb")
        x, share = keep["x"], keep["share"]
        GROUP = 4
        GROUPS = TILES // GROUP
        POOL_GROUPS = (1, 3)
        DVE_GROUPS = [g for g in range(GROUPS) if g not in POOL_GROUPS]
        got = m.sb("got", [P, GROUPS, GROUP, TOP, D])
        gathered = [m.sem(f"gathered{g}") for g in range(GROUPS)]
        weighed, first_done, x_done, written = m.sem("weighed"), m.sem("first_done"), m.sem("x_done"), m.sem("written")
        pool_weighed, pool_first_done, pool_x_done = m.sem("pool_weighed"), m.sem("pool_first_done"), m.sem("pool_x_done")
        out_tiles = out.rearrange("b s d -> (b s) d").rearrange("(t p) d -> p t d", p=P)
        result = keep["result"][0:TILES * P * TOP, :].rearrange("(t p k) d -> p t k d", p=P, k=TOP)
        block = ctx.enter_context(nc.Block())

        @block.sync
        def _(sp):
            for g in range(GROUPS):
                sp.dma_start(got[:, g, :, :, :], result[:, g * GROUP:(g + 1) * GROUP, :, :]).then_inc(gathered[g], DMA)

        @block.vector
        def _(dve):
            for n, g in enumerate(DVE_GROUPS):
                part, now = slice(g * GROUP, (g + 1) * GROUP), got[:, g, :, :, :]
                dve.wait_ge(gathered[g], DMA)
                dve.tensor_tensor(now, now, many(share[:, part, :], D, 3), ALU.mult).then_inc(weighed, 1)
                dve.wait_ge(weighed, n + 1)
                dve.tensor_tensor(x[:, part, :], x[:, part, :], now[:, :, 0, :], ALU.add).then_inc(first_done, 1)
                dve.wait_ge(first_done, n + 1)
                dve.tensor_tensor(x[:, part, :], x[:, part, :], now[:, :, 1, :], ALU.add).then_inc(x_done, 1)

        @block.gpsimd
        def _(pool):
            for n, g in enumerate(POOL_GROUPS):
                part, now = slice(g * GROUP, (g + 1) * GROUP), got[:, g, :, :, :]
                pool.wait_ge(gathered[g], DMA)
                pool.tensor_tensor(now, now, many(share[:, part, :], D, 3), ALU.mult).then_inc(pool_weighed, 1)
                pool.wait_ge(pool_weighed, n + 1)
                pool.tensor_tensor(x[:, part, :], x[:, part, :], now[:, :, 0, :], ALU.add).then_inc(pool_first_done, 1)
                pool.wait_ge(pool_first_done, n + 1)
                pool.tensor_tensor(x[:, part, :], x[:, part, :], now[:, :, 1, :], ALU.add).then_inc(pool_x_done, 1)

        @block.scalar
        def _(act):
            def write(g):
                part = slice(g * GROUP, (g + 1) * GROUP)
                act.dma_start(out_tiles[:, part, :], x[:, part, :]).then_inc(written, DMA)

            for n, g in enumerate(DVE_GROUPS):
                act.wait_ge(x_done, n + 1)
                write(g)
            for n, g in enumerate(POOL_GROUPS):
                act.wait_ge(pool_x_done, n + 1)
                write(g)
            act.wait_ge(keep["mask_loaded"], 2 * DMA)
            act.wait_ge(written, GROUPS * DMA)




def setup(nc, dram, keep):
    x, ident, eps_pow = keep["x"], keep["ident"], keep["eps_pow"]
    x_tiles = dram["x"].rearrange("b s d -> (b s) d").rearrange("(t p) d -> p t d", p=P)
    with nc.Block() as block:

        @block.sync
        def _(sp):
            part = slice(0, TILES // X_PARTS)
            sp.dma_start(x[:, part, :], x_tiles[:, part, :]).then_inc(keep["x_loaded"], DMA)

        @block.gpsimd
        def _(pool):
            pool.memset(eps_pow[:, :], -0.5).then_inc(keep["ident_ready"], 1)
            pool.memset(ident[:, :], 0.0).then_inc(keep["ident_ready"], 1)
            pool.wait_ge(keep["ident_ready"], 2)
            pool.affine_select(out=ident[:, :], in_=ident[:, :], compare_op=ALU.not_equal, fill=1.0, base=0,
                               pattern=[[-1, P]], channel_multiplier=1).then_inc(keep["ident_ready"], 1)


def network(nc, dram, out):
    ctx = ExitStack()
    with ctx:
        m = Memory(nc, ctx, "net")
        keep = {
            "x": m.sb("x", [P, TILES, D]), "ident": m.sb("ident", [P, P]), "eps_pow": m.sb("eps_pow", [P, 1]),
            "mask": m.sb("mask", [P, TILES, PER_TILE * SEQ], I32), "x_loaded": m.sem("x_loaded"),
            "mask_loaded": m.sem("mask_loaded"), "ident_ready": m.sem("ident_ready"), "ident_count": 3,
            "ffn": {
                "w_in": m.sb("ffn_w", [P, 3 + EXPERTS, D]), "wsw_in": m.sb("ffn_wsw", [EXPERTS, D]),
                "bq": m.sb("ffn_bq", [P, 1]), "bk": m.sb("ffn_bk", [P, 1]), "bv": m.sb("ffn_bv", [P, D]),
                "gamma": m.sb("gamma", [P, D]), "beta": m.sb("beta", [P, D]), "bsw": m.sb("bsw", [P, EXPERTS]),
                "be": m.sb("be", [P, EXPERTS * D]),
            },
            "attn": {
                "w_in": m.sb("attn_w", [P, 4, D]), "bq": m.sb("attn_bq", [P, 1]), "bk": m.sb("attn_bk", [P, 1]),
                "bv": m.sb("attn_bv", [P, D]), "bo": m.sb("attn_bo", [P, D]),
            },
            "weights_loaded": m.sem("weights_loaded"),
            "w_in": m.sb("w_in", [P, EXPERTS, MLP]), "w_out": m.sb("w_out", [P, EXPERTS, BLOCKS, D]),
            "b_in": m.sb("b_in", [EXPERTS * BLOCKS, P]), "b_out": m.sb("b_out", [P, EXPERTS, D]), "w_loaded": m.sem("w_loaded"),
            "stats": m.sb("stats", [P, TILES, 6]), "share": m.sb("share", [P, TILES, TOP]), "table": m.sb("table", [P, 2, SORTED], I32),
            "sorted": nc.dram_tensor("sorted_rows", (EXPERTS * (REGION + P), ROW), F32, kind="Internal").ap(),
            "result": nc.dram_tensor("result_rows", ((TILES * TOP + 2 * EXPERTS) * P, D), F32, kind="Internal").ap(),
        }
        setup(nc, dram, keep)
        wide_attention(nc, dram, keep)
        routed_attention(nc, dram, keep)
        masked_attention(nc, dram, keep)
        select_experts(nc, dram, keep)
        run_experts(nc, dram, keep)
        combine(nc, dram, keep, out)


_INS = ["x", "ctx_1024", "mask_Bx1xSxS2_ik1"]
_INS += [f"L0_xattn_{n}" for n in ("Wq", "bq", "Wk", "bk", "Wv", "bv", "Wu", "bu")]
_INS += [f"L0_ffn_{n}" for n in ("Wq", "bq", "Wk", "bk", "Wv", "bv", "We", "be", "Wsw", "bsw", "gamma", "beta")]
_INS += [f"L1_xattn_{n}" for n in ("Wv", "bv", "Wk", "bk", "Wq", "bq", "Wo", "bo")]
_INS += [f"L1_ffn_{n}" for n in ("W_gate", "W_in", "b_in", "W_out", "b_out")]


def kernel(**inputs):
    import numpy as np
    from concourse import bacc
    from concourse.bass_utils import run_bass_kernel_spmd

    nc = bacc.Bacc("TRN2", target_bir_lowering=False, num_devices=1)
    arrays, dram = {}, {}
    for name in _INS:
        a = np.ascontiguousarray(inputs[name])
        arrays[f"in_{name}"] = a
        dram[name] = nc.dram_tensor(f"in_{name}", a.shape, mybir.dt.from_np(a.dtype), kind="ExternalInput").ap()
    out = nc.dram_tensor("out_x", inputs["x"].shape, F32, kind="ExternalOutput").ap()
    network(nc, dram, out)
    r = run_bass_kernel_spmd(nc, [arrays], core_ids=[0])
    return r.results[0]["out_x"]
```
